# Optimizing a Trainium2 kernel written in Bass

```python
import numpy as np
import jax
import jax.numpy as jnp

def _softmax(x, axis=-1):
    return jax.nn.softmax(x, axis=axis)

def _gelu(x):
    return jax.nn.gelu(x, approximate=True)

def _silu(x):
    return jax.nn.silu(x)

def _sigmoid(x):
    return jax.nn.sigmoid(x)

def _layernorm(x, axis=-1, eps=1e-05):
    m = jnp.mean(x, axis=axis, keepdims=True)
    v = jnp.var(x, axis=axis, keepdims=True)
    return (x - m) / jnp.sqrt(v + eps)

def _scatter_add(tgt, idx, src, axis=0):
    return tgt.at[idx].add(src)

def _segment_sum(src, seg, n):
    return jax.ops.segment_sum(src, seg, n)
kernel_name = 'mk_adaln_d1_jaxref_r4_e93ad5'

def setup_inputs(seed: int=0):
    np.random.seed(seed)
    _w = jnp.asarray

    def _L0_attn_setup():
        import jax, jax.numpy as jnp
        import numpy as np
        B, T, D = (4, 512, 256)
        N_HEADS = 16
        HEAD_DIM = D // N_HEADS

        def rope(x):
            t, dh = (x.shape[-2], x.shape[-1])
            half = dh // 2
            theta = 1.0 / 10000.0 ** (jnp.arange(half, dtype=jnp.float32) / half)
            ang = jnp.arange(t, dtype=jnp.float32)[:, None] * theta[None, :]
            sin, cos = (jnp.sin(ang), jnp.cos(ang))
            x1 = x[..., 0::2]
            x2 = x[..., 1::2]
            return jnp.concatenate([x1 * cos - x2 * sin, x1 * sin + x2 * cos], axis=-1)
        key = jax.random.key(seed)
        ks = jax.random.split(key, 9)
        s = 0.02
        return {'x': jax.random.normal(ks[0], (B, T, D), dtype=jnp.float32), 'W_q': jax.random.normal(ks[1], (D, D), dtype=jnp.float32) * s, 'b_q': jnp.zeros((D,), dtype=jnp.float32), 'W_k': jax.random.normal(ks[2], (D, D), dtype=jnp.float32) * s, 'b_k': jnp.zeros((D,), dtype=jnp.float32), 'W_v': jax.random.normal(ks[3], (D, D), dtype=jnp.float32) * s, 'b_v': jnp.zeros((D,), dtype=jnp.float32), 'W_o': jax.random.normal(ks[4], (D, D), dtype=jnp.float32) * s, 'b_o': jnp.zeros((D,), dtype=jnp.float32)}
    _L0_attn_in = _L0_attn_setup()

    def _L0_ffn_setup():
        import jax, jax.numpy as jnp
        import numpy as np
        D = 256
        H = 4
        HD = D // H
        E = 8
        FF = 1024
        CAP_FACTOR = 1.0

        def _ln(x, g, b, eps=1e-05):
            mu = jnp.mean(x, -1, keepdims=True)
            v = jnp.mean((x - mu) ** 2, -1, keepdims=True)
            return (x - mu) * jax.lax.rsqrt(v + eps) * g + b

        def _mha(x, w, b, ow, ob):
            L, N, _ = x.shape
            qkv = x @ w.T + b
            q, k, v = jnp.split(qkv, 3, axis=-1)
            rh = lambda t: t.reshape(L, N, H, HD).transpose(1, 2, 0, 3)
            q, k, v = (rh(q), rh(k), rh(v))
            scores = jnp.einsum('nhld,nhmd->nhlm', q, k) / np.float32(np.sqrt(HD))
            attn = jax.nn.softmax(scores, axis=-1)
            o = jnp.einsum('nhlm,nhmd->nhld', attn, v).transpose(2, 0, 1, 3).reshape(L, N, D)
            return o @ ow.T + ob

        def _moe(x, wg, w1, b1, w2, b2):
            L, N, _ = x.shape
            S = L * N
            cap = int(CAP_FACTOR * S) // E
            xf = x.reshape(S, D)
            gates = jax.nn.softmax(xf @ wg, axis=-1)
            idx = jnp.argmax(gates, axis=-1)
            mask1 = jax.nn.one_hot(idx, E, dtype=x.dtype)
            loc = jnp.sum((jnp.cumsum(mask1, 0) - 1.0) * mask1, -1).astype(jnp.int32)
            keep = loc < cap
            gate_val = jnp.take_along_axis(gates, idx[:, None], -1)[:, 0]
            slot = jnp.where(keep, idx.astype(jnp.int32) * cap + loc, E * cap)
            disp = jnp.zeros((E * cap, D), x.dtype).at[slot].set(xf, mode='drop')
            disp = disp.reshape(E, cap, D)
            h = jnp.einsum('ecd,edf->ecf', disp, w1) + b1[:, None, :]
            y = (jnp.einsum('ecf,efd->ecd', h, w2) + b2[:, None, :]).reshape(E * cap, D)
            out = jnp.where(keep[:, None], gate_val[:, None] * y[jnp.minimum(slot, E * cap - 1)], 0.0)
            return out.reshape(L, N, D)
        key = jax.random.key(seed)
        ks = jax.random.split(key, 8)
        L, N = (256, 16)
        s = 0.02
        return {'x': jax.random.normal(ks[0], (L, N, D), jnp.float32), 'in_proj_w': jax.random.normal(ks[1], (3 * D, D), jnp.float32) * s, 'in_proj_b': jnp.zeros((3 * D,), jnp.float32), 'out_proj_w': jax.random.normal(ks[2], (D, D), jnp.float32) * s, 'out_proj_b': jnp.zeros((D,), jnp.float32), 'ln1_g': jnp.ones((D,), jnp.float32), 'ln1_b': jnp.zeros((D,), jnp.float32), 'ln2_g': jnp.ones((D,), jnp.float32), 'ln2_b': jnp.zeros((D,), jnp.float32), 'wg': jax.random.normal(ks[3], (D, E), jnp.float32) * s, 'w1': jax.random.normal(ks[4], (E, D, FF), jnp.float32) * s, 'b1': jnp.zeros((E, FF), jnp.float32), 'w2': jax.random.normal(ks[5], (E, FF, D), jnp.float32) * s, 'b2': jnp.zeros((E, D), jnp.float32)}
    _L0_ffn_in = _L0_ffn_setup()
    _L0_c = _w((lambda *s: np.random.randn(*s).astype(np.float32) * 0.05)(4, 256))
    _L0_wmod = _w((lambda *s: np.random.randn(*s).astype(np.float32) * 0.05)(256, 6 * 256) * 256 ** (-0.5))
    _d = {'L0_attn_x': _L0_attn_in['x'], 'L0_attn_W_q': _L0_attn_in['W_q'], 'L0_attn_b_q': _L0_attn_in['b_q'], 'L0_attn_W_k': _L0_attn_in['W_k'], 'L0_attn_b_k': _L0_attn_in['b_k'], 'L0_attn_W_v': _L0_attn_in['W_v'], 'L0_attn_b_v': _L0_attn_in['b_v'], 'L0_attn_W_o': _L0_attn_in['W_o'], 'L0_attn_b_o': _L0_attn_in['b_o'], 'L0_ffn_in_proj_w': _L0_ffn_in['in_proj_w'], 'L0_ffn_in_proj_b': _L0_ffn_in['in_proj_b'], 'L0_ffn_out_proj_w': _L0_ffn_in['out_proj_w'], 'L0_ffn_out_proj_b': _L0_ffn_in['out_proj_b'], 'L0_ffn_ln1_g': _L0_ffn_in['ln1_g'], 'L0_ffn_ln1_b': _L0_ffn_in['ln1_b'], 'L0_ffn_ln2_g': _L0_ffn_in['ln2_g'], 'L0_ffn_ln2_b': _L0_ffn_in['ln2_b'], 'L0_ffn_wg': _L0_ffn_in['wg'], 'L0_ffn_w1': _L0_ffn_in['w1'], 'L0_ffn_b1': _L0_ffn_in['b1'], 'L0_ffn_w2': _L0_ffn_in['w2'], 'L0_ffn_b2': _L0_ffn_in['b2'], 'L0_c': _L0_c, 'L0_wmod': _L0_wmod}
    _x0 = _d['L0_attn_x']
    _d['L0_attn_x'] = jax.random.normal(jax.random.fold_in(jax.random.key(seed), 1), (4, 1024, 256), dtype=_x0.dtype)
    del _x0
    return _d

def reference(L0_attn_x, L0_attn_W_q, L0_attn_b_q, L0_attn_W_k, L0_attn_b_k, L0_attn_W_v, L0_attn_b_v, L0_attn_W_o, L0_attn_b_o, L0_ffn_in_proj_w, L0_ffn_in_proj_b, L0_ffn_out_proj_w, L0_ffn_out_proj_b, L0_ffn_ln1_g, L0_ffn_ln1_b, L0_ffn_ln2_g, L0_ffn_ln2_b, L0_ffn_wg, L0_ffn_w1, L0_ffn_b1, L0_ffn_w2, L0_ffn_b2, L0_c, L0_wmod):

    def _L0_attn_ref(x, W_q, b_q, W_k, b_k, W_v, b_v, W_o, b_o):
        import jax, jax.numpy as jnp
        import numpy as np
        B, T, D = (4, 512, 256)
        N_HEADS = 16
        HEAD_DIM = D // N_HEADS

        def rope(x):
            t, dh = (x.shape[-2], x.shape[-1])
            half = dh // 2
            theta = 1.0 / 10000.0 ** (jnp.arange(half, dtype=jnp.float32) / half)
            ang = jnp.arange(t, dtype=jnp.float32)[:, None] * theta[None, :]
            sin, cos = (jnp.sin(ang), jnp.cos(ang))
            x1 = x[..., 0::2]
            x2 = x[..., 1::2]
            return jnp.concatenate([x1 * cos - x2 * sin, x1 * sin + x2 * cos], axis=-1)
        b, t, d = x.shape
        h, dh = (N_HEADS, d // N_HEADS)

        def heads(y):
            return y.reshape(b, t, h, dh).transpose(0, 2, 1, 3)
        q = rope(heads(x @ W_q.T + b_q))
        k = rope(heads(x @ W_k.T + b_k))
        v = heads(x @ W_v.T + b_v)
        scores = jnp.einsum('bhtd,bhsd->bhts', q, k)
        causal = jnp.tril(jnp.ones((t, t), dtype=bool))
        mask = jnp.where(causal, 0.0, -jnp.inf)
        probs = jax.nn.softmax((scores + mask) / jnp.sqrt(jnp.float32(dh)), axis=-1)
        out = jnp.einsum('bhts,bhsd->bhtd', probs, v)
        out = out.transpose(0, 2, 1, 3).reshape(b, t, d)
        return out @ W_o.T + b_o

    def _L0_ffn_ref(x, in_proj_w, in_proj_b, out_proj_w, out_proj_b, ln1_g, ln1_b, ln2_g, ln2_b, wg, w1, b1, w2, b2):
        import jax, jax.numpy as jnp
        import numpy as np
        D = 256
        H = 4
        HD = D // H
        E = 8
        FF = 1024
        CAP_FACTOR = 1.0

        def _ln(x, g, b, eps=1e-05):
            mu = jnp.mean(x, -1, keepdims=True)
            v = jnp.mean((x - mu) ** 2, -1, keepdims=True)
            return (x - mu) * jax.lax.rsqrt(v + eps) * g + b

        def _mha(x, w, b, ow, ob):
            L, N, _ = x.shape
            qkv = x @ w.T + b
            q, k, v = jnp.split(qkv, 3, axis=-1)
            rh = lambda t: t.reshape(L, N, H, HD).transpose(1, 2, 0, 3)
            q, k, v = (rh(q), rh(k), rh(v))
            scores = jnp.einsum('nhld,nhmd->nhlm', q, k) / np.float32(np.sqrt(HD))
            attn = jax.nn.softmax(scores, axis=-1)
            o = jnp.einsum('nhlm,nhmd->nhld', attn, v).transpose(2, 0, 1, 3).reshape(L, N, D)
            return o @ ow.T + ob

        def _moe(x, wg, w1, b1, w2, b2):
            L, N, _ = x.shape
            S = L * N
            cap = int(CAP_FACTOR * S) // E
            xf = x.reshape(S, D)
            gates = jax.nn.softmax(xf @ wg, axis=-1)
            idx = jnp.argmax(gates, axis=-1)
            mask1 = jax.nn.one_hot(idx, E, dtype=x.dtype)
            loc = jnp.sum((jnp.cumsum(mask1, 0) - 1.0) * mask1, -1).astype(jnp.int32)
            keep = loc < cap
            gate_val = jnp.take_along_axis(gates, idx[:, None], -1)[:, 0]
            slot = jnp.where(keep, idx.astype(jnp.int32) * cap + loc, E * cap)
            disp = jnp.zeros((E * cap, D), x.dtype).at[slot].set(xf, mode='drop')
            disp = disp.reshape(E, cap, D)
            h = jnp.einsum('ecd,edf->ecf', disp, w1) + b1[:, None, :]
            y = (jnp.einsum('ecf,efd->ecd', h, w2) + b2[:, None, :]).reshape(E * cap, D)
            out = jnp.where(keep[:, None], gate_val[:, None] * y[jnp.minimum(slot, E * cap - 1)], 0.0)
            return out.reshape(L, N, D)
        y1 = _ln(x + _mha(x, in_proj_w, in_proj_b, out_proj_w, out_proj_b), ln1_g, ln1_b)
        y2 = _ln(y1 + _moe(y1, wg, w1, b1, w2, b2), ln2_g, ln2_b)
        return y2
    x = L0_attn_x
    mod = (_silu(L0_c) @ L0_wmod).reshape(L0_c.shape[0], 6, 1, -1)
    sa, ca, ga, sb, cb, gb = (mod[:, 0], mod[:, 1], mod[:, 2], mod[:, 3], mod[:, 4], mod[:, 5])
    ga = (2 * (ga >= 0) - 1) * jnp.maximum(jnp.abs(ga), 0.25)
    gb = (2 * (gb >= 0) - 1) * jnp.maximum(jnp.abs(gb), 0.25)
    h = _layernorm(x, axis=-1) * (1 + ca) + sa
    x = x + ga * _L0_attn_ref(h, L0_attn_W_q, L0_attn_b_q, L0_attn_W_k, L0_attn_b_k, L0_attn_W_v, L0_attn_b_v, L0_attn_W_o, L0_attn_b_o)
    h = _layernorm(x, axis=-1) * (1 + cb) + sb
    x = x + gb * _L0_ffn_ref(h, L0_ffn_in_proj_w, L0_ffn_in_proj_b, L0_ffn_out_proj_w, L0_ffn_out_proj_b, L0_ffn_ln1_g, L0_ffn_ln1_b, L0_ffn_ln2_g, L0_ffn_ln2_b, L0_ffn_wg, L0_ffn_w1, L0_ffn_b1, L0_ffn_w2, L0_ffn_b2)
    return x

_drawn_inputs = setup_inputs


def setup_inputs(seed=0):
    import zlib

    import numpy as np

    out = dict(_drawn_inputs(seed))
    spreads = {'L0_attn_b_q': (0.0, 0.8),
     'L0_attn_b_k': (0.0, 0.8),
     'L0_attn_b_v': (0.0, 0.8),
     'L0_attn_b_o': (0.0, 0.315),
     'L0_ffn_in_proj_b': (0.0, 0.8),
     'L0_ffn_out_proj_b': (0.0, 0.308),
     'L0_ffn_ln1_g': (1.0, 0.2),
     'L0_ffn_ln1_b': (0.0, 0.329),
     'L0_ffn_ln2_g': (1.0, 0.2),
     'L0_ffn_ln2_b': (0.0, 0.324),
     'L0_ffn_b1': (0.0, 0.8),
     'L0_ffn_b2': (0.0, 0.8)}
    factors = {'L0_attn_W_q': 8.0,
     'L0_attn_W_k': 8.0,
     'L0_attn_W_v': 8.0,
     'L0_attn_W_o': 6.22,
     'L0_ffn_in_proj_w': 4.328,
     'L0_ffn_out_proj_w': 3.622,
     'L0_ffn_wg': 5.548,
     'L0_ffn_w1': 6.032,
     'L0_ffn_w2': 5.757}
    for name, (base, spread) in spreads.items():
        noise = np.random.default_rng([zlib.crc32(name.encode()), seed]).standard_normal(out[name].shape)
        drawn = base * np.exp(spread * noise) if base else spread * noise
        out[name] = jnp.asarray(drawn.astype(out[name].dtype))
    for name, factor in factors.items():
        out[name] = (out[name] * factor).astype(out[name].dtype)
    return out
```

```python
from contextlib import ExitStack, contextmanager

import concourse.bass as bass
from concourse import mybir

F32 = mybir.dt.float32
BF16 = mybir.dt.bfloat16
I32 = mybir.dt.int32
U32 = mybir.dt.uint32
ALU = mybir.AluOpType
ACT = mybir.ActivationFunctionType
AX = mybir.AxisListType

P = 128
B = 4
T = 1024
D = 256
KC = D // P
NT = T // P
TILES = B * NT
H1 = 16
DH = D // H1
J = 4
G = H1 // J
HALF = 512
E = 8
FF = 1024
FC = FF // P
CAP = B * T // E
EPS = 1e-5
LOWEST = -3.0e38

Q_PART = (0, 0, 0, 1, 1, 2)
K_PART = (0, 1, 2, 0, 1, 0)
SROWS = len(Q_PART) * DH
MROWS = 3


class Counts:

    def __init__(self, eng):
        self.eng, self.seen = eng, {}

    def wait(self, sem, n=1):
        name = sem.name
        self.seen[name] = (sem, self.seen.get(name, (sem, 0))[1] + n)
        self.eng.wait_ge(sem, self.seen[name][1])

    @contextmanager
    def rounds(self, start, end):
        with self.eng.Fori(start, end) as i:
            before = dict(self.seen)
            yield i
            for name, (sem, n) in self.seen.items():
                more = n - before.get(name, (sem, 0))[1]
                if more:
                    self.eng.sem_inc(sem, -more)
            self.seen = {name: (sem, before.get(name, (sem, 0))[1]) for name, (sem, _) in self.seen.items()}


def fold_experts(nc, ins, hold):
    with ExitStack() as ctx:
        sb = lambda name, shape, dt=F32: ctx.enter_context(nc.sbuf_tensor(name, shape, dt))
        sem = lambda name: ctx.enter_context(nc.semaphore(name))
        w1 = [sb(f"f_w1_{n}", [P, FC, D]) for n in range(2)]
        w2 = [sb(f"f_w2_{n}", [P, FC, D]) for n in range(2)]
        b1 = [sb(f"f_b1_{n}", [P, FC]) for n in range(2)]
        b2 = [sb(f"f_b2_{n}", [1, D]) for n in range(2)]
        w12 = [sb(f"f_w12_{n}", [P, KC, D]) for n in range(2)]
        b12 = [sb(f"f_b12_{n}", [1, D]) for n in range(2)]
        zero = sb("f_zero", [P, 4 * D])
        w_ps = [ctx.enter_context(nc.psum_tensor(f"f_w_ps{n}", [P, KC, D], F32)) for n in range(2)]
        b_ps = [ctx.enter_context(nc.psum_tensor(f"f_b_ps{n}", [1, HALF], F32)) for n in range(2)]
        w_in = [sem("f_w_in0"), sem("f_w_in1")]
        w12_out = [sem("f_w12_out0"), sem("f_w12_out1")]
        w_free, ps_free, b2_ready, product = sem("f_w_free"), sem("f_ps_free"), sem("f_b2_ready"), sem("f_product")
        w12_ready, b12_ready, zero_ready, zero_out = sem("f_w12_ready"), sem("f_b12_ready"), sem("f_zero_ready"), sem("f_zero_out")
        block = ctx.enter_context(nc.Block())

        @block.sync
        def _(sp):
            c = Counts(sp)
            sp.sem_inc(w_free, 2)
            with c.rounds(0, E // 2) as i:
                for n in range(2):
                    c.wait(w_free)
                    for dst, src in ((w1[n], "w1_t"), (w2[n], "w2")):
                        src = ins[src].rearrange("(i n c p) d -> n p i c d", n=2, c=FC, p=P)[n]
                        sp.dma_start(dst[:], src[:, bass.ds(i, 1), :, :].rearrange("p o c d -> p (o c) d"))\
                          .then_inc(w_in[n], 16)
                    sp.dma_start(b1[n][:], ins["b1_t"].rearrange("(i n) p c -> n p i c", n=2)[n][:, bass.ds(i, 1), :]
                                 .rearrange("p o c -> p (o c)")).then_inc(w_in[n], 16)
                    sp.dma_start(b2[n][:], ins["b2"].rearrange("(i n) d -> n i d", n=2)[n][bass.ds(i, 1), :])\
                      .then_inc(w_in[n], 16)
            sp.wait_ge(zero_ready, 1)
            slots = hold["slots_in"].rearrange("(r p t) d -> r p (t d)", p=P, t=4)
            for r in range(E):
                sp.dma_start(slots[r], zero[:]).then_inc(zero_out, 16)
            sp.wait_ge(zero_out, 16 * E)

        @block.tensor
        def _(pe):
            c = Counts(pe)
            with c.rounds(0, E // 2):
                for n in range(2):
                    c.wait(w_in[n], 64)
                    c.wait(ps_free)
                    for m in range(KC):
                        for f in range(FC):
                            nc.tensor.matmul(w_ps[n][:, m, :], w1[n][:, f, m * P:(m + 1) * P], w2[n][:, f, :],
                                             start=(f == 0), stop=(f == FC - 1))
                    for f in range(FC):
                        last = nc.tensor.matmul(b_ps[n][0:1, 0:D], b1[n][:, f:f + 1], w2[n][:, f, :],
                                                start=(f == 0), stop=(f == FC - 1))
                    last.then_inc(product, 1)

        @block.vector
        def _(dve):
            c = Counts(dve)
            nc.vector.memset(zero[:], 0.0).then_inc(zero_ready, 1)
            for n in range(2):
                dve.sem_inc(w12_out[n], 32)
            with c.rounds(0, E // 2):
                for n in range(2):
                    c.wait(w12_out[n], 32)
                    c.wait(product)
                    nc.vector.tensor_tensor(b12[n][:], b2[n][:], b_ps[n][0:1, 0:D], ALU.add).then_inc(b12_ready, 1)
                    nc.vector.tensor_copy(w12[n][:], w_ps[n][:]).then_inc(w12_ready, 1)
            for n in range(2):
                c.wait(w12_out[n], 32)

        @block.scalar
        def _(act):
            c = Counts(act)
            act.sem_inc(ps_free, 2)
            w12_dram = hold["w12"].rearrange("(i n m p) d -> n p i m d", n=2, m=KC, p=P)
            b12_dram = hold["b12"].rearrange("(i n) d -> n i d", n=2)
            with c.rounds(0, E // 2) as i:
                for n in range(2):
                    c.wait(b12_ready)
                    c.wait(w12_ready)
                    act.sem_inc(ps_free, 1)
                    act.sem_inc(w_free, 1)
                    act.dma_start(b12_dram[n][bass.ds(i, 1), :], b12[n][:]).then_inc(w12_out[n], 16)
                    act.dma_start(w12_dram[n][:, bass.ds(i, 1), :, :].rearrange("p o m d -> p (o m) d"), w12[n][:])\
                       .then_inc(w12_out[n], 16)


def prepare(nc, ins, hold):
    x, c_t, wmod = ins["x"], ins["c_t"], ins["wmod"]
    with ExitStack() as ctx:
        sb = lambda name, shape, dt=F32: ctx.enter_context(nc.sbuf_tensor(name, shape, dt))
        sem = lambda name: ctx.enter_context(nc.semaphore(name))
        xs = sb("p_x", [P, TILES, D])
        wm = sb("p_wmod", [P, KC, 6 * D])
        cs = sb("p_c", [P, KC, B])
        sil = sb("p_silu", [P, KC, B])
        stats = sb("p_stats", [P, TILES, 6])
        rows = sb("p_rows", [B, 6, D])
        sign = sb("p_sign", [B, 2, D])
        mag = sb("p_mag", [B, 2, D])
        rows_ps = ctx.enter_context(nc.psum_tensor("p_rows_ps", [B, 3, HALF], F32))
        cols_ps = ctx.enter_context(nc.psum_tensor("p_cols_ps", [P, 2, KC, B], F32))
        x_in, w_in, c_in, out_done = sem("p_x_in"), sem("p_w_in"), sem("p_c_in"), sem("p_out")
        bn_done, var_ready, std_ready, stat_link = sem("p_bn"), sem("p_var"), sem("p_std"), sem("p_link")
        exp_ready, silu_ready, mod_ready, rows_ready = sem("p_exp"), sem("p_silu_r"), sem("p_mod"), sem("p_rows_r")
        mean_rstd, ca1_sa = hold["mean_rstd1"], hold["ca1_sa"]
        block = ctx.enter_context(nc.Block())

        @block.sync
        def _(sp):
            sp.dma_start(cs[:], c_t.rearrange("(c p) b -> p c b", p=P)).then_inc(c_in, 16)
            sp.dma_start(wm[:], wmod.rearrange("(c p) n -> p c n", p=P)).then_inc(w_in, 16)
            for b in range(B):
                if b:
                    sp.wait_ge(x_in, 16 * b)
                sp.dma_start(xs[:, NT * b:NT * (b + 1), :],
                             x[T * b:T * (b + 1), :].rearrange("(t p) d -> p t d", p=P)).then_inc(x_in, 16)
            sp.wait_ge(rows_ready, 2)
            for n, row in enumerate((2, 5, 4, 3)):
                sp.dma_start(hold["mod_rows"][n], rows[:, row, :]).then_inc(out_done, 16)
            sp.wait_ge(out_done, 64)

        @block.tensor
        def _(pe):
            pe.wait_ge(silu_ready, 1)
            pe.wait_ge(w_in, 16)
            for n in range(3):
                for c in range(KC):
                    last = nc.tensor.matmul(rows_ps[:, n, :], sil[:, c, :], wm[:, c, n * HALF:(n + 1) * HALF],
                                            start=(c == 0), stop=(c == KC - 1))
            for n in range(2):
                for m in range(KC):
                    for c in range(KC):
                        last = nc.tensor.matmul(cols_ps[:, n, m, :], wm[:, c, n * D + m * P:n * D + (m + 1) * P],
                                                sil[:, c, :], start=(c == 0), stop=(c == KC - 1))
            last.then_inc(mod_ready, 1)

        @block.scalar
        def _(act):
            act.wait_ge(c_in, 16)
            nc.scalar.activation(sil[:], cs[:], ACT.Exp, scale=-1.0).then_inc(exp_ready, 1)
            act.wait_ge(var_ready, 1)
            nc.scalar.activation(mean_rstd[:, :, 1], mean_rstd[:, :, 1], ACT.Sqrt).then_inc(std_ready, 1)

        @block.vector
        def _(dve):
            dve.wait_ge(exp_ready, 1)
            nc.vector.tensor_scalar(sil[:], sil[:], 1.0, None, ALU.add).then_inc(stat_link, 1)
            dve.wait_ge(stat_link, 1)
            nc.vector.reciprocal(sil[:], sil[:]).then_inc(stat_link, 1)
            dve.wait_ge(stat_link, 2)
            nc.vector.tensor_tensor(sil[:], sil[:], cs[:], ALU.mult).then_inc(silu_ready, 1)
            for t in range(TILES):
                if t % NT == 0:
                    dve.wait_ge(x_in, 16 * (t // NT + 1))
                nc.vector.bn_stats(stats[:, t, :], xs[:, t, :]).then_inc(bn_done, 1)
            for t in range(TILES):
                dve.wait_ge(bn_done, t + 1)
                last = nc.vector.bn_aggr(mean_rstd[:, t, :], stats[:, t, :]).then_inc(stat_link, 1)
            dve.wait_ge(stat_link, 2 + TILES)
            nc.vector.tensor_scalar(mean_rstd[:, :, 1], mean_rstd[:, :, 1], EPS, None, ALU.add).then_inc(var_ready, 1)
            dve.wait_ge(mod_ready, 1)
            flat = rows[:].rearrange("b s d -> b (s d)")
            nc.vector.tensor_copy(flat, rows_ps[:].rearrange("b n f -> b (n f)")).then_inc(rows_ready, 1)
            dve.wait_ge(rows_ready, 1)
            gates = rows[:].rearrange("b (n s) d -> b n s d", s=3)[:, :, 2, :]
            nc.vector.tensor_scalar(sign[:], gates, 0.0, 2.0, ALU.is_ge, ALU.mult).then_inc(stat_link, 1)
            nc.vector.scalar_tensor_tensor(mag[:], gates, -1.0, gates, ALU.mult, ALU.max).then_inc(stat_link, 1)
            dve.wait_ge(stat_link, 4 + TILES)
            nc.vector.tensor_scalar(sign[:], sign[:], 1.0, None, ALU.subtract).then_inc(stat_link, 1)
            nc.vector.tensor_scalar(mag[:], mag[:], 0.25, None, ALU.max).then_inc(stat_link, 1)
            nc.vector.tensor_scalar(rows[:, 4, :], rows[:, 4, :], 1.0, None, ALU.add).then_inc(stat_link, 1)
            dve.wait_ge(stat_link, 7 + TILES)
            nc.vector.tensor_tensor(gates, sign[:], mag[:], ALU.mult).then_inc(rows_ready, 1)
            nc.vector.tensor_scalar(ca1_sa[:, 0, :, :], cols_ps[:, 1, :, :], 1.0, None, ALU.add).then_inc(stat_link, 1)
            nc.vector.tensor_copy(ca1_sa[:, 1, :, :], cols_ps[:, 0, :, :]).then_inc(stat_link, 1)
            dve.wait_ge(std_ready, 1)
            nc.vector.reciprocal(mean_rstd[:, :, 1], mean_rstd[:, :, 1]).then_inc(stat_link, 1)


SLOTS = 4
STAGE1 = 2 * KC + 2 * SLOTS + NT // 2
CHUNKS = J * 12
BANK_USES = STAGE1 + G * CHUNKS
MISC_USES = 12 + 8
STEPS = 12
PT_BUFS = 3
UNIT_BUF = (0, 1, 2, 0)
BUF_USES = (2, 1, 1)
CHUNKS_PER_STEP = 5

CHUNK = []
for _qt in range(NT):
    if _qt < 4:
        CHUNK.append((_qt, 0, (_qt + 1) * P, True))
    else:
        CHUNK.append((_qt, 0, HALF, False))
        CHUNK.append((_qt, HALF, (_qt - 3) * P, True))

STEP = []
for _qh in range(2):
    for _kb in range(4 * _qh + 4):
        STEP.append((_qh, _kb, max(0, _kb - 4 * _qh) * P, _kb >= 4 * _qh))



def turn_of_misc(kind, g=0, qh=0):
    if kind == "maxima":
        return 0 if g == 0 else 3 * g - 1
    if kind == "output":
        return 1 + 3 * g + (2 if g < G - 1 else 1) * qh
    return 12 + g


def attention(nc, ins, hold):
    x, scratch, x2_dram = ins["x"], hold["qk_scratch"], hold["x2"]
    mean_rstd1, mean_var2, ca1_sa = hold["mean_rstd1"], hold["mean_rstd2"], hold["ca1_sa"]
    with ExitStack() as ctx:
        sb = lambda name, shape, dt=F32: ctx.enter_context(nc.sbuf_tensor(name, shape, dt))
        ps = lambda name, shape: ctx.enter_context(nc.psum_tensor(name, shape, F32))
        sem = lambda name: ctx.enter_context(nc.semaphore(name))
        wqk, wv, wo = sb("wqk", [P, KC, 2 * D]), sb("wv", [P, KC, D]), sb("wo", [P, KC, D])
        bqk, bv, bo = sb("bqk", [P, SLOTS]), sb("bv", [P, D]), sb("bo", [P, D])
        cos, sin = sb("cos", [P, T]), sb("sin", [P, T])
        ident, tri, after = sb("ident", [P, P]), sb("tri", [P, HALF]), sb("after", [P, P])
        ident16, after16 = sb("ident16", [P, P], BF16), sb("after16", [P, P], BF16)
        xb, xg, xn = sb("xb", [P, NT, D]), sb("xg", [P, NT, D]), sb("xn", [P, NT, D])
        ga, gabo = sb("ga", [P, D]), sb("gabo", [P, D])
        stat = sb("stat", [P, NT, 2])
        stat6, stat2 = sb("stat6", [P, NT, 6]), sb("stat2", [P, NT, 2])
        ht = sb("ht", [P, KC, T])
        qk = sb("qk", [P, SLOTS, T])
        sw = sb("sw", [P, SLOTS, T])
        part = sb("part", [P, SLOTS, 3, T], BF16)
        vp = sb("vp", [P, NT, H1, 32])
        qs = [sb(f"qs{n}", [P, J, T], BF16) for n in range(3)]
        ks = [sb(f"ks{n}", [P, J, T], BF16) for n in range(3)]
        pt = sb("pt", [P, PT_BUFS, J, HALF])
        mp = sb("mp", [P, J * NT, 2])
        negm = sb("negm", [P, J * NT])
        mres = sb("mres", [J * NT, P])
        mpart = sb("mpart", [J * NT, MROWS, P], BF16)
        junk = sb("junk", [P, 2, HALF], BF16)
        o_sb = sb("o_sb", [P, HALF])
        rec = sb("rec", [P, 4, J])
        y_sb = sw[:, 0, 0:2 * D].rearrange("p (t d) -> p t d", t=2)
        ot = xn
        bank_ps = ps("bank_ps", [P, 2, HALF])
        st_ps = ps("st_ps", [P, 2, 2, HALF])
        o_ps = ps("o_ps", [P, HALF])
        misc_ps = ps("misc_ps", [P, HALF])

        w_in, c_in, x_in, ga_in = sem("w_in"), sem("c_in"), sem("x_in"), sem("ga_in")
        xg_ready, ln_done = sem("xg_ready"), sem("ln_done")
        bank_for_act, bank_for_dve = sem("bank_for_act"), sem("bank_for_dve")
        bank_read = [sem("bank_read0"), sem("bank_read1")]
        swapped, t1_ready, t2_ready, roped = sem("swapped"), sem("t1_ready"), sem("t2_ready"), sem("roped")
        p1_ready, r1_ready, p2_ready, p3_ready = sem("p1_ready"), sem("r1_ready"), sem("p2_ready"), sem("p3_ready")
        parts_out = sem("parts_out")
        unit_in = [sem(f"unit_in{n}") for n in range(3)]
        m_ready, m_split, m_in = sem("m_ready"), sem("m_split"), sem("m_in")
        misc_full, misc_read = sem("misc_full"), sem("misc_read")
        st_full, exp_done, pv_done = sem("st_full"), sem("exp_done"), sem("pv_done")
        o_out, x2_ready, x2_out, link, init = sem("o_out"), sem("x2_ready"), sem("x2_out"), sem("link"), sem("init")
        block = ctx.enter_context(nc.Block())

        FREE = 1
        SENT = 16

        def bank_empty(eng, b, n):
            eng.wait_ge(bank_read[n % 2], BANK_USES // 2 * b + (n // 2 + FREE))

        def bank_moved(eng, b, n):
            eng.wait_ge(bank_read[n % 2], BANK_USES // 2 * b + (n // 2 + 1 + FREE))

        def buffer_use(b, g):
            n = UNIT_BUF[g]
            return BUF_USES[n] * b + ([h for h in range(G) if UNIT_BUF[h] == n].index(g) + 1)

        @block.sync
        def _(sp):
            for s in (*bank_read, misc_read, o_out, p3_ready, x2_ready, m_ready, ln_done, xg_ready):
                sp.sem_inc(s, FREE)
            sp.sem_inc(exp_done, 2 * FREE)
            sp.sem_inc(pv_done, PT_BUFS * FREE)
            for s in (*unit_in, parts_out, x2_out, m_in):
                sp.sem_inc(s, SENT)
            for dst, src in ((wqk, "wqk"), (wv, "wv"), (wo, "wo")):
                sp.dma_start(dst[:], ins[src].rearrange("(c p) n -> p c n", p=P)).then_inc(w_in, 16)
            sp.dma_start(bqk[:], ins["bqk"]).then_inc(w_in, 16)
            for dst, src in ((bv, "bv"), (bo, "bo")):
                sp.dma_start(dst[:], ins[src].partition_broadcast(P)).then_inc(w_in, 16)
            for dst, src in ((cos, "cos"), (sin, "sin"), (ident, "ident"), (tri, "tri"), (after, "after")):
                sp.dma_start(dst[:], ins[src]).then_inc(c_in, 16)
            xv = x.rearrange("(b t p) d -> p b t d", b=B, p=P)
            x2v = x2_dram.rearrange("(b t p) d -> p b t d", b=B, p=P)

            def minus_max_rows(b, g):
                sp.wait_ge(m_split, G * b + (g + 1))
                for r in range(MROWS):
                    row = qs[UNIT_BUF[g]][SROWS + r:SROWS + r + 1, :, :].rearrange("o j (q c) -> o (j q) c", c=P)
                    sp.dma_start(row, mpart[:, r, :]).then_inc(m_in, 16)

            with sp.Fori(0, B) as b:
                sp.wait_ge(ln_done, NT * b + FREE)
                sp.wait_ge(xg_ready, 2 * b + FREE)
                sp.dma_start(xb[:], xv[:, bass.ds(b, 1), :, :].rearrange("p o t d -> p (o t) d")).then_inc(x_in, 16)
                sp.wait_ge(x2_ready, NT // 2 * b + FREE)
                sp.dma_start(ga[:], hold["mod_rows"][0, bass.ds(b, 1), :].partition_broadcast(P)
                             .rearrange("p o d -> p (o d)")).then_inc(ga_in, 16)
                for s in range(SLOTS):
                    w, m = divmod(s, 2)
                    sp.wait_ge(p3_ready, SLOTS * b + (s + 1 + FREE))
                    sp.dma_start(scratch[w, :, m * P:(m + 1) * P, :].rearrange("s p t -> p s t"),
                                 part[:, s, :, :]).then_inc(parts_out, 16)
                sp.wait_ge(parts_out, 16 * SLOTS * b + (16 * SLOTS + SENT))
                for g in range(G):
                    n = UNIT_BUF[g]
                    sp.wait_ge(pv_done, STEPS * G * b + (STEPS * (g == G - 1) + PT_BUFS * FREE))
                    for r in range(len(Q_PART)):
                        for w, dst, p in ((0, qs[n], Q_PART[r]), (1, ks[n], K_PART[r])):
                            src = scratch[w, p, J * DH * g:J * DH * (g + 1), :].rearrange("(j d) t -> d j t", d=DH)
                            sp.dma_start(dst[DH * r:DH * (r + 1), :, :], src).then_inc(unit_in[n], 16)
                    if g:
                        minus_max_rows(b, g - 1)
                minus_max_rows(b, G - 1)
                sp.wait_ge(x2_ready, NT // 2 * b + (NT // 2 + FREE))
                sp.dma_start(x2v[:, bass.ds(b, 1), :, :].rearrange("p o t d -> p (o t) d"), xg[:]).then_inc(x2_out, 16)
            sp.wait_ge(x2_out, 16 * B + SENT)

        @block.gpsimd
        def _(pool):
            for n in range(3):
                nc.gpsimd.memset(ks[n][SROWS:SROWS + MROWS, :, :], 1.0).then_inc(init, 1)
                pool.wait_ge(init, n + 1)
            nc.gpsimd.memset(vp[:], 0.0).then_inc(init, 1)
            pool.wait_ge(init, 4)
            nc.gpsimd.memset(mp[:], LOWEST).then_inc(init, 1)
            pool.wait_ge(init, 5)
            nc.gpsimd.memset(vp[:, :, :, DH:DH + 1], 1.0).then_inc(init, 1)
            pool.wait_ge(init, 6)
            pool.wait_ge(w_in, 16 * 6)
            pool.wait_ge(c_in, 16 * 5)
            nc.gpsimd.tensor_copy(ident16[:], ident[:]).then_inc(init, 1)
            nc.gpsimd.tensor_copy(after16[:], after[:]).then_inc(init, 1)
            with pool.Fori(0, B) as b:
                pool.wait_ge(ga_in, 16 * b + 16)
                nc.gpsimd.tensor_tensor(gabo[:], ga[:], bo[:], ALU.mult).then_inc(xg_ready, 1)
                pool.wait_ge(xg_ready, 2 * b + (1 + FREE))
                pool.wait_ge(x_in, 16 * b + 16)
                pool.wait_ge(x2_out, 16 * b + SENT)
                pool.wait_ge(ln_done, NT * b + (1 + FREE))
                nc.gpsimd.tensor_tensor(xg[:], xb[:], gabo[:].unsqueeze(1).to_broadcast([P, NT, D]), ALU.add)\
                    .then_inc(xg_ready, 1)
                for s in range(SLOTS):
                    bank_moved(pool, b, 2 * KC + s)
                    bank_moved(pool, b, 2 * KC + SLOTS + s)
                    nc.gpsimd.tensor_tensor(sw[:, s, :], qk[:, s, :], sin[:], ALU.mult).then_inc(t2_ready, 1)
                for s in range(SLOTS):
                    pool.wait_ge(p2_ready, SLOTS * b + (s + 1))
                    nc.gpsimd.tensor_tensor(part[:, s, 2, :], qk[:, s, :], part[:, s, 1, :], ALU.subtract)\
                        .then_inc(p3_ready, 1)

        @block.tensor
        def _(pe):
            pe.wait_ge(c_in, 16 * 5)
            pe.wait_ge(w_in, 16 * 6)
            pe.wait_ge(init, 8)
            with pe.Fori(0, B) as b:
                def score_chunk(g, c):
                    n = STAGE1 + CHUNKS * g + c
                    qt, k0, keys, _ = CHUNK[c % len(CHUNK)]
                    buf, j = UNIT_BUF[g], c // len(CHUNK)
                    if c == 0:
                        pe.wait_ge(unit_in[buf], 32 * len(Q_PART) * buffer_use(b, g) + SENT)
                    bank_empty(pe, b, n)
                    nc.tensor.matmul(bank_ps[:, n % 2, 0:keys], qs[buf][0:SROWS, j, qt * P:(qt + 1) * P],
                                     ks[buf][0:SROWS, j, k0:k0 + keys], start=True, stop=True).then_inc(bank_for_dve, 1)

                def misc_empty(turn):
                    pe.wait_ge(misc_read, MISC_USES * b + (turn + FREE))

                def transpose_maxima(g):
                    misc_empty(turn_of_misc("maxima", g))
                    pe.wait_ge(m_ready, G * b + (g + 1 + FREE))
                    nc.tensor.transpose(misc_ps[0:J * NT, 0:P], negm[:], ident[:]).then_inc(misc_full, 1)

                def scores_for_exp(g, s):
                    qh, kb, off, _ = STEP[s]
                    buf = UNIT_BUF[g]
                    if s == 0:
                        pe.wait_ge(m_in, 16 * MROWS * G * b + (16 * MROWS * (g + 1) + SENT))
                    _, _, _, diagonal = STEP[s]
                    for h in range(2):
                        pe.wait_ge(exp_done, 2 * STEPS * G * b + (2 * STEPS * g + 2 * s + h - 1 + 2 * FREE))
                        for i in range(2):
                            j = 2 * h + i
                            if diagonal:
                                nc.tensor.matmul(st_ps[:, h, i, off:off + P], ident16[:], after16[:],
                                                 start=True, stop=False, skip_group_check=True)
                            last = nc.tensor.matmul(st_ps[:, h, i, off:HALF],
                                                    ks[buf][0:SROWS + MROWS, j, kb * P:(kb + 1) * P],
                                                    qs[buf][0:SROWS + MROWS, j, qh * HALF + off:(qh + 1) * HALF],
                                                    start=not diagonal, stop=True, skip_group_check=diagonal)
                        last.then_inc(st_full, 1)

                def weigh_values(g, s):
                    qh, kb, off, diagonal = STEP[s]
                    pe.wait_ge(exp_done, 2 * STEPS * G * b + (2 * STEPS * g + 2 * s + 2 + 2 * FREE))
                    if kb == 0:
                        pe.wait_ge(o_out, 2 * G * b + (2 * g + qh + FREE))
                    for j in range(J):
                        last = nc.tensor.matmul(o_ps[32 * j:32 * (j + 1), off:HALF], vp[:, kb, J * g + j, :],
                                                pt[:, s % PT_BUFS, j, off:HALF],
                                                start=(kb == 0), stop=(kb == 4 * qh + 3))
                    last.then_inc(pv_done, 1)

                def transpose_output(g, qh):
                    misc_empty(turn_of_misc("output", g, qh))
                    pe.wait_ge(o_out, 2 * G * b + (2 * g + qh + 1 + FREE))
                    for i in range(4):
                        last = nc.tensor.transpose(misc_ps[:, i * P:(i + 1) * P], o_sb[:, i * P:(i + 1) * P], ident[:])
                    last.then_inc(misc_full, 1)

                for n in range(2 * KC):
                    half, c = divmod(n, KC)
                    bank_empty(pe, b, n)
                    pe.wait_ge(ln_done, NT * b + (4 * (half + 1) + FREE))
                    for i in range(4):
                        last = nc.tensor.transpose(bank_ps[:, n % 2, i * P:(i + 1) * P],
                                                   xn[:, 4 * half + i, c * P:(c + 1) * P], ident[:])
                    last.then_inc(bank_for_act, 1)
                for half in range(2):
                    bank_moved(pe, b, 2 * half)
                    bank_moved(pe, b, 2 * half + 1)
                    for s in range(SLOTS):
                        n = 2 * KC + SLOTS * half + s
                        bank_empty(pe, b, n)
                        for c in range(KC):
                            last = nc.tensor.matmul(bank_ps[:, n % 2, :], wqk[:, c, s * P:(s + 1) * P],
                                                    ht[:, c, half * HALF:(half + 1) * HALF],
                                                    start=(c == 0), stop=(c == KC - 1))
                        last.then_inc(bank_for_act, 1)
                for i in range(NT // 2):
                    n = 2 * KC + 2 * SLOTS + i
                    bank_empty(pe, b, n)
                    for t in (2 * i, 2 * i + 1):
                        for c in range(KC):
                            last = nc.tensor.matmul(bank_ps[:, n % 2, (t % 2) * D:(t % 2 + 1) * D],
                                                    ht[:, c, t * P:(t + 1) * P], wv[:, c, :],
                                                    start=(c == 0), stop=(c == KC - 1))
                    last.then_inc(bank_for_dve, 1)

                for c in range(CHUNKS):
                    score_chunk(0, c)
                transpose_maxima(0)
                for g in range(G):
                    for s in range(STEPS):
                        if g + 1 < G:
                            for c in range(CHUNKS_PER_STEP * s, min(CHUNKS, CHUNKS_PER_STEP * (s + 1))):
                                score_chunk(g + 1, c)
                        scores_for_exp(g, s)
                        if s:
                            weigh_values(g, s - 1)
                        if s == 1 and g:
                            transpose_output(g - 1, 1)
                        if s == 6:
                            transpose_output(g, 0)
                    weigh_values(g, STEPS - 1)
                    if g + 1 < G:
                        transpose_maxima(g + 1)
                transpose_output(G - 1, 1)
                for n in range(2 * KC):
                    half, c = divmod(n, KC)
                    misc_empty(turn_of_misc("product", n))
                    for i in range(4):
                        last = nc.tensor.transpose(misc_ps[:, i * P:(i + 1) * P],
                                                   ot[:, 4 * half + i, c * P:(c + 1) * P], ident[:])
                    last.then_inc(misc_full, 1)
                for i in range(NT // 2):
                    misc_empty(turn_of_misc("product", 2 * KC + i))
                    for t in (2 * i, 2 * i + 1):
                        for c in range(KC):
                            last = nc.tensor.matmul(misc_ps[:, (t % 2) * D:(t % 2 + 1) * D],
                                                    ht[:, c, t * P:(t + 1) * P], wo[:, c, :],
                                                    start=(c == 0), stop=(c == KC - 1))
                    last.then_inc(misc_full, 1)

        @block.scalar
        def _(act):
            act.wait_ge(w_in, 16 * 6)
            act.wait_ge(c_in, 16 * 5)
            with act.Fori(0, B) as b:
                for n in range(2 * KC):
                    half, c = divmod(n, KC)
                    act.wait_ge(bank_for_act, n + 1)
                    nc.scalar.activation(ht[:, c, half * HALF:(half + 1) * HALF], bank_ps[:, n % 2, :], ACT.Identity,
                                         bias=ca1_sa[:, 1, c, bass.ds(b, 1)], scale=ca1_sa[:, 0, c, bass.ds(b, 1)])\
                        .then_inc(bank_read[n % 2], 1)
                act.wait_ge(p3_ready, SLOTS * b + FREE)
                act.wait_ge(parts_out, 16 * SLOTS * b + SENT)
                for half in range(2):
                    for s in range(SLOTS):
                        n = 2 * KC + SLOTS * half + s
                        act.wait_ge(bank_for_act, n + 1)
                        nc.scalar.activation(qk[:, s, half * HALF:(half + 1) * HALF], bank_ps[:, n % 2, :], ACT.Identity,
                                             bias=bqk[:, s:s + 1]).then_inc(bank_read[n % 2], 1)
                for s in range(SLOTS):
                    act.wait_ge(roped, SLOTS * b + (s + 1))
                    nc.scalar.activation(part[:, s, 0, :], qk[:, s, :], ACT.Copy).then_inc(p1_ready, 1)
                for s in range(SLOTS):
                    act.wait_ge(r1_ready, SLOTS * b + (s + 1))
                    nc.scalar.activation(part[:, s, 1, :], qk[:, s, :], ACT.Copy).then_inc(p2_ready, 1)

                def output_out(g, qh):
                    act.wait_ge(pv_done, STEPS * G * b + (STEPS * g + 4 + 8 * qh + PT_BUFS * FREE))
                    before = turn_of_misc("output", g, 0) if qh else (turn_of_misc("output", g - 1, 1) if g else 0)
                    act.wait_ge(misc_full, MISC_USES * b + (before + 1))
                    nc.scalar.activation(o_sb[:], o_ps[:], ACT.Copy).then_inc(o_out, 1)

                for g in range(G):
                    for s, (qh, kb, off, _) in enumerate(STEP):
                        act.wait_ge(pv_done, STEPS * G * b + (STEPS * g + s + FREE))
                        for h in range(2):
                            act.wait_ge(st_full, 2 * STEPS * G * b + (2 * STEPS * g + 2 * s + h + 1))
                            nc.scalar.activation(pt[:, s % PT_BUFS, 2 * h:2 * h + 2, off:HALF], st_ps[:, h, :, off:HALF],
                                                 ACT.Exp, scale=DH ** -0.5).then_inc(exp_done, 1)
                        if s == 4:
                            output_out(g, 0)
                    output_out(g, 1)
                for n in range(2 * KC):
                    half, c = divmod(n, KC)
                    act.wait_ge(misc_full, MISC_USES * b + (turn_of_misc("product", n) + 1))
                    nc.scalar.activation(ht[:, c, half * HALF:(half + 1) * HALF], misc_ps[:], ACT.Copy)\
                        .then_inc(misc_read, 1)
                act.sem_inc(bank_for_act, -(2 * KC + 2 * SLOTS))

        @block.vector
        def _(dve):
            dve.wait_ge(c_in, 16 * 5)
            dve.wait_ge(w_in, 16 * 6)
            dve.wait_ge(init, 6)
            swap = [DH * (i // DH) + (i + DH // 2) % DH for i in range(32)]
            with dve.Fori(0, B) as b:
                links = [0]

                def hand_over(ins):
                    links[0] += 1
                    ins.then_inc(link, 1)
                    dve.wait_ge(link, links[0])

                hand_over(nc.vector.tensor_copy(stat[:], mean_rstd1[:, bass.ds(NT * b, NT), :]))
                dve.wait_ge(x_in, 16 * b + 16)
                for t in range(NT):
                    nc.vector.tensor_scalar(xn[:, t, :], xb[:, t, :], stat[:, t, 0:1], stat[:, t, 1:2],
                                            ALU.subtract, ALU.mult).then_inc(ln_done, 1)
                for s in range(SLOTS):
                    dve.wait_ge(t2_ready, s + 1)
                    nc.vector.stream_shuffle(sw[:, s, :], sw[:, s, :], swap).then_inc(swapped, 1)
                    nc.vector.tensor_tensor(qk[:, s, :], qk[:, s, :], cos[:], ALU.mult).then_inc(t1_ready, 1)
                for i in range(NT // 2):
                    n = 2 * KC + 2 * SLOTS + i
                    dve.wait_ge(bank_for_dve, i + 1)
                    nc.vector.tensor_tensor(
                        vp[:, 2 * i:2 * i + 2, :, 0:DH],
                        bank_ps[:, n % 2, :].rearrange("p (t h d) -> p t h d", t=2, d=DH),
                        bv[:].rearrange("p (h d) -> p h d", d=DH).unsqueeze(1).to_broadcast([P, 2, H1, DH]),
                        ALU.add).then_inc(bank_read[n % 2], 1)
                for s in range(SLOTS):
                    dve.wait_ge(t1_ready, SLOTS * b + (s + 1))
                    dve.wait_ge(swapped, SLOTS * b + (s + 1))
                    nc.vector.tensor_tensor(qk[:, s, :], qk[:, s, :], sw[:, s, :], ALU.add).then_inc(roped, 1)
                for s in range(SLOTS):
                    dve.wait_ge(p1_ready, SLOTS * b + (s + 1))
                    nc.vector.tensor_tensor(qk[:, s, :], qk[:, s, :], part[:, s, 0, :], ALU.subtract).then_inc(r1_ready, 1)

                def chunk_maximum(g, c):
                    n = STAGE1 + CHUNKS * g + c
                    qt, _, keys, diagonal = CHUNK[c % len(CHUNK)]
                    row = c // len(CHUNK) * NT + qt
                    dve.wait_ge(bank_for_dve, NT // 2 + CHUNKS * g + c + 1)
                    if diagonal:
                        ins = nc.vector.tensor_tensor_reduce(
                            out=junk[:, n % 2, 0:keys], in0=bank_ps[:, n % 2, 0:keys], in1=tri[:, HALF - keys:HALF],
                            scale=1.0, scalar=LOWEST, op0=ALU.add, op1=ALU.max, accum_out=mp[:, row, 0:1])
                    else:
                        ins = nc.vector.tensor_reduce(mp[:, row, 1:2], bank_ps[:, n % 2, 0:keys], AX.X, ALU.max)
                    ins.then_inc(bank_read[n % 2], 1)

                def group_maxima(g):
                    bank_moved(dve, b, STAGE1 + CHUNKS * (g + 1) - 2)
                    bank_moved(dve, b, STAGE1 + CHUNKS * (g + 1) - 1)
                    nc.vector.tensor_reduce(negm[:], mp[:], AX.X, ALU.max, negate=True).then_inc(m_ready, 1)
                    turn = turn_of_misc("maxima", g)
                    dve.wait_ge(misc_full, MISC_USES * b + (turn + 1))
                    dve.wait_ge(m_in, 16 * MROWS * G * b + (16 * MROWS * g + SENT))
                    hand_over(nc.vector.tensor_copy(mpart[:, 0, :], misc_ps[0:J * NT, 0:P]))
                    nc.vector.tensor_tensor(mres[:], misc_ps[0:J * NT, 0:P], mpart[:, 0, :], ALU.subtract)\
                        .then_inc(misc_read, 1)
                    dve.wait_ge(misc_read, MISC_USES * b + (turn + 1 + FREE))
                    hand_over(nc.vector.tensor_copy(mpart[:, 1, :], mres[:]))
                    nc.vector.tensor_tensor(mpart[:, 2, :], mres[:], mpart[:, 1, :], ALU.subtract).then_inc(m_split, 1)

                def divide_output(g, qh):
                    dve.wait_ge(misc_full, MISC_USES * b + (turn_of_misc("output", g, qh) + 1))
                    o = misc_ps[:].rearrange("p (t j d) -> p t j d", t=4, j=J)
                    hand_over(nc.vector.reciprocal(rec[:], o[:, :, :, DH]))
                    nc.vector.tensor_tensor(
                        ot[:, 4 * qh:4 * qh + 4, J * DH * g:J * DH * (g + 1)].rearrange("p t (j d) -> p t j d", d=DH),
                        o[:, :, :, 0:DH], rec[:].unsqueeze(3).to_broadcast([P, 4, J, DH]), ALU.mult)\
                        .then_inc(misc_read, 1)

                for g in range(G + 1):
                    if g < G:
                        for c in range(CHUNKS):
                            chunk_maximum(g, c)
                            if c == 2 * CHUNKS_PER_STEP + 2 and g > 1:
                                divide_output(g - 2, 1)
                            if c == 7 * CHUNKS_PER_STEP + 1 and g:
                                divide_output(g - 1, 0)
                        group_maxima(g)
                    else:
                        divide_output(g - 2, 1)
                        divide_output(g - 1, 0)
                        divide_output(g - 1, 1)
                dve.wait_ge(xg_ready, 2 * b + (2 + FREE))
                for i in range(NT // 2):
                    turn = turn_of_misc("product", 2 * KC + i)
                    dve.wait_ge(misc_full, MISC_USES * b + (turn + 1))
                    if i:
                        dve.wait_ge(x2_ready, NT // 2 * b + (i + FREE))
                    nc.vector.tensor_tensor(y_sb, misc_ps[:].rearrange("p (t d) -> p t d", t=2),
                                            ga[:].unsqueeze(1).to_broadcast([P, 2, D]), ALU.mult).then_inc(misc_read, 1)
                    dve.wait_ge(misc_read, MISC_USES * b + (turn + 1 + FREE))
                    nc.vector.tensor_tensor(xg[:, 2 * i:2 * i + 2, :], xg[:, 2 * i:2 * i + 2, :], y_sb, ALU.add)\
                        .then_inc(x2_ready, 1)
                dve.wait_ge(x2_ready, NT // 2 * b + (NT // 2 + FREE))
                for t in range(NT):
                    hand_over(nc.vector.bn_stats(stat6[:, t, :], xg[:, t, :]))
                for t in range(NT):
                    hand_over(nc.vector.bn_aggr(stat2[:, t, :], stat6[:, t, :]))
                hand_over(nc.vector.tensor_copy(mean_var2[:, bass.ds(NT * b, NT), :], stat2[:]))
                dve.sem_inc(link, -links[0])
                dve.sem_inc(bank_for_dve, -(NT // 2 + G * CHUNKS))
                dve.sem_inc(t2_ready, -SLOTS)


PAIRS = NT // 2


def batch_attention(nc, ins, hold):
    with ExitStack() as ctx:
        sb = lambda name, shape, dt=F32: ctx.enter_context(nc.sbuf_tensor(name, shape, dt))
        sem = lambda name: ctx.enter_context(nc.semaphore(name))
        ps = lambda name, shape: ctx.enter_context(nc.psum_tensor(name, shape, F32))
        H2 = 4
        D2 = D // H2
        w_in, w_out, bias_in, bias_out = (sb("b_w_in", [P, KC, 3 * D]), sb("b_w_out", [P, KC, D]),
                                          sb("b_bias_in", [P, 3 * D]), sb("b_bias_out", [P, D]))
        cb1, sbb, ident = sb("b_cb1", [P, B, D]), sb("b_sb", [P, B, D]), sb("b_ident", [P, P])
        x2 = [sb(f"b_x2_{n}", [P, B, D]) for n in range(2)]
        h = [sb(f"b_h_{n}", [P, B, D]) for n in range(2)]
        hb = [sb(f"b_hb_{n}", [P, B, D]) for n in range(2)]
        h_t = sb("b_h_t", [P, KC, B * P])
        qkv = [sb(f"b_qkv_{n}", [P, B, 3 * D]) for n in range(2)]
        stat = [sb(f"b_stat_{n}", [P, B, 2]) for n in range(2)]
        prod = [sb(f"b_prod_{n}", [P, B, D]) for n in range(4)]
        score, top, pr, total = sb("b_score", [P, B, B, H2]), sb("b_top", [P, B, H2]), sb("b_pr", [P, B, B, H2]), sb("b_total", [P, B, H2])
        o, o_t = sb("b_o", [P, B, D]), sb("b_o_t", [P, KC, B * P])
        y = sb("b_y", [P, B, D])
        st6, st2 = sb("b_st6", [P, B, 6]), sb("b_st2", [P, B, 2])
        t_ps, qkv_ps, y_ps = ps("b_t_ps", [P, 2, HALF]), ps("b_qkv_ps", [P, 2, 2 * HALF]), ps("b_y_ps", [P, 2, HALF])
        mean_rstd2, mean_rstd3, y_all = hold["mean_rstd2"], hold["mean_rstd3"], hold["y_all"]

        c_in, y_done = sem("b_c_in"), sem("b_y_done")
        x2_in, x2_free = [sem("b_x2_in0"), sem("b_x2_in1")], sem("b_x2_free")
        var_ready, std_ready, h_for_pe, h_for_pool = sem("b_var"), sem("b_std"), sem("b_h_for_pe"), sem("b_h_for_pool")
        hb_ready, t_full, t_read = sem("b_hb_ready"), sem("b_t_full"), sem("b_t_read")
        qkv_full, qkv_out, qkv_read = sem("b_qkv_full"), sem("b_qkv_out"), sem("b_qkv_read")
        qkv_ready, qkv_for_pool = sem("b_qkv_ready"), sem("b_qkv_for_pool")
        qk_product, pr_for_pool, v_product = sem("b_qk_product"), sem("b_pr_for_pool"), sem("b_v_product")
        exp_in, exp_out, o_ready, o_full, o_read = sem("b_exp_in"), sem("b_exp_out"), sem("b_o_ready"), sem("b_o_full"), sem("b_o_read")
        y_full, y_read, y_ready, y_copied, link = sem("b_y_full"), sem("b_y_read"), sem("b_y_ready"), sem("b_y_copied"), sem("b_link")
        block = ctx.enter_context(nc.Block())
        x2v = hold["x2"].rearrange("(b i n p) d -> n p i b d", b=B, n=2, p=P)

        def schedule(c, front, back):
            front(0, 0)
            with c.rounds(0, PAIRS - 1) as i:
                for n in range(2):
                    front(2 * i + (n + 1), 1 - n)
                    back(2 * i + n, n)
            front(NT - 1, 1)
            back(NT - 2, 0)
            back(NT - 1, 1)

        @block.sync
        def _(sp):
            c = Counts(sp)
            sp.sem_inc(x2_free, 2)
            for dst, src in ((w_in, "w_in"), (w_out, "w_out")):
                sp.dma_start(dst[:], ins[src].rearrange("(c p) n -> p c n", p=P)).then_inc(c_in, 16)
            for dst, src in ((bias_in, "b_in"), (bias_out, "b_out")):
                sp.dma_start(dst[:], ins[src].partition_broadcast(P)).then_inc(c_in, 16)
            sp.dma_start(ident[:], ins["ident"]).then_inc(c_in, 16)
            for dst, n in ((cb1, 2), (sbb, 3)):
                sp.dma_start(dst[:], hold["mod_rows"][n].partition_broadcast(P)).then_inc(c_in, 16)
            with c.rounds(0, PAIRS) as i:
                for n in range(2):
                    c.wait(x2_free)
                    for b in range(B):
                        sp.dma_start(x2[n][:, b, :], x2v[n][:, bass.ds(i, 1), b, :].rearrange("p o d -> p (o d)"))                          .then_inc(x2_in[n], 16)

        @block.tensor
        def _(pe):
            c = Counts(pe)
            pe.wait_ge(c_in, 16 * 7)

            def front(tile, n):
                c.wait(h_for_pe)
                for k in range(KC):
                    for b in range(B):
                        last = nc.tensor.transpose(t_ps[:, k, b * P:(b + 1) * P], h[n][:, b, k * P:(k + 1) * P], ident[:])
                    last.then_inc(t_full, 1)
                c.wait(t_read, 2)
                for b in range(B):
                    c.wait(qkv_read)
                    for lo, hi in ((0, HALF), (HALF, 3 * D)):
                        for k in range(KC):
                            last = nc.tensor.matmul(qkv_ps[:, b % 2, lo:hi], h_t[:, k, b * P:(b + 1) * P],
                                                    w_in[:, k, lo:hi], start=(k == 0), stop=(k == KC - 1))
                    last.then_inc(qkv_full, 1)

            def back(tile, n):
                c.wait(y_read, 2)
                c.wait(o_ready)
                for k in range(KC):
                    for b in range(B):
                        last = nc.tensor.transpose(y_ps[:, k, b * P:(b + 1) * P], o[:, b, k * P:(k + 1) * P], ident[:])
                    last.then_inc(o_full, 1)
                c.wait(o_read, 2)
                for u in range(2):
                    for b in (2 * u, 2 * u + 1):
                        for k in range(KC):
                            last = nc.tensor.matmul(y_ps[:, u, (b % 2) * D:(b % 2 + 1) * D], o_t[:, k, b * P:(b + 1) * P],
                                                    w_out[:, k, :], start=(k == 0), stop=(k == KC - 1))
                    last.then_inc(y_full, 1)

            schedule(c, front, back)

        @block.scalar
        def _(act):
            c = Counts(act)
            c.wait(var_ready)
            nc.scalar.activation(mean_rstd2[:, :, 1], mean_rstd2[:, :, 1], ACT.Sqrt).then_inc(std_ready, 1)
            act.sem_inc(qkv_read, 2)

            def front(tile, n):
                for k in range(KC):
                    c.wait(t_full)
                    nc.scalar.activation(h_t[:, k, :], t_ps[:, k, :], ACT.Copy).then_inc(t_read, 1)
                for b in range(B):
                    c.wait(qkv_full)
                    nc.scalar.activation(qkv[n][:, b, :], qkv_ps[:, b % 2, 0:3 * D], ACT.Copy).then_inc(qkv_out, 1)

            def back(tile, n):
                c.wait(exp_in)
                nc.scalar.activation(pr[:], score[:], ACT.Exp, scale=D2 ** -0.5).then_inc(exp_out, 1)
                for k in range(KC):
                    c.wait(o_full)
                    nc.scalar.activation(o_t[:, k, :], y_ps[:, k, :], ACT.Copy).then_inc(o_read, 1)
                c.wait(y_ready)
                nc.scalar.activation(y_all[:].rearrange("p (b t) d -> p b t d", b=B)[:, :, bass.ds(tile, 1), :]
                                     .rearrange("p b o d -> p b (o d)"), y[:], ACT.Copy).then_inc(y_copied, 1)

            schedule(c, front, back)

        @block.gpsimd
        def _(pool):
            c = Counts(pool)
            pool.wait_ge(c_in, 16 * 7)

            def front(tile, n):
                c.wait(h_for_pool)
                nc.gpsimd.tensor_tensor(hb[n][:], h[n][:], bias_out[:].unsqueeze(1).to_broadcast([P, B, D]), ALU.add)                    .then_inc(hb_ready, 1)
                for b in range(B):
                    c.wait(qkv_out)
                    nc.gpsimd.tensor_tensor(qkv[n][:, b, :], qkv[n][:, b, :], bias_in[:], ALU.add).then_inc(qkv_ready, 1)
                    pool.sem_inc(qkv_read, 1)

            def back(tile, n):
                c.wait(qkv_for_pool)
                nc.gpsimd.tensor_tensor(prod[3][:], qkv[n][:, 3:4, 0:D].to_broadcast([P, B, D]), qkv[n][:, :, D:2 * D],
                                        ALU.mult).then_inc(qk_product, 1)
                c.wait(pr_for_pool)
                nc.gpsimd.tensor_tensor(prod[3][:].rearrange("p m (h d) -> p m h d", h=H2),
                                        qkv[n][:, :, 2 * D:3 * D].rearrange("p m (h d) -> p m h d", h=H2),
                                        pr[:, 3, :, :].unsqueeze(3).to_broadcast([P, B, H2, D2]), ALU.mult)                    .then_inc(v_product, 1)

            schedule(c, front, back)

        @block.vector
        def _(dve):
            c = Counts(dve)

            def hand_over(*instructions):
                for ins in instructions:
                    ins.then_inc(link, 1)
                c.wait(link, len(instructions))

            dve.sem_inc(y_copied, 1)
            hand_over(nc.vector.tensor_scalar(mean_rstd2[:, :, 1], mean_rstd2[:, :, 1], EPS, None, ALU.add))
            dve.sem_inc(var_ready, 1)
            c.wait(std_ready)
            hand_over(nc.vector.reciprocal(mean_rstd2[:, :, 1], mean_rstd2[:, :, 1]))
            dve.wait_ge(c_in, 16 * 7)
            dve.sem_inc(y_read, 2)

            def front(tile, n):
                hand_over(nc.vector.tensor_copy(stat[n][:], mean_rstd2[:].rearrange("p (b t) s -> p b t s", b=B)
                                                [:, :, bass.ds(tile, 1), :].rearrange("p b o s -> p b (o s)")))
                c.wait(x2_in[n], 64)
                hand_over(*[nc.vector.scalar_tensor_tensor(h[n][:, b, :], x2[n][:, b, :], stat[n][:, b, 0:1], cb1[:, b, :],
                                                           ALU.subtract, ALU.mult) for b in range(B)])
                dve.sem_inc(x2_free, 1)
                hand_over(*[nc.vector.scalar_tensor_tensor(h[n][:, b, :], h[n][:, b, :], stat[n][:, b, 1:2], sbb[:, b, :],
                                                           ALU.mult, ALU.add) for b in range(B)])
                dve.sem_inc(h_for_pe, 1)
                dve.sem_inc(h_for_pool, 1)

            def back(tile, n):
                c.wait(qkv_ready, B)
                dve.sem_inc(qkv_for_pool, 1)
                hand_over(*[nc.vector.tensor_tensor(prod[l][:], qkv[n][:, l:l + 1, 0:D].to_broadcast([P, B, D]),
                                                    qkv[n][:, :, D:2 * D], ALU.mult) for l in range(3)])
                sums = []
                for l in range(B):
                    if l == 3:
                        c.wait(qk_product)
                    sums.append(nc.vector.tensor_reduce(score[:, l, :, :].rearrange("p m h -> p (m h)"),
                                                        prod[l][:].rearrange("p m (h d) -> p (m h) d", h=H2),
                                                        AX.X, ALU.add))
                    sums[-1].then_inc(link, 1)
                c.wait(link, B)
                hand_over(nc.vector.tensor_reduce(top[:], score[:].rearrange("p l m h -> p l h m"), AX.X, ALU.max))
                hand_over(nc.vector.tensor_tensor(score[:], score[:], top[:].unsqueeze(2).to_broadcast([P, B, B, H2]),
                                                  ALU.subtract))
                dve.sem_inc(exp_in, 1)
                c.wait(exp_out)
                hand_over(nc.vector.tensor_reduce(total[:], pr[:].rearrange("p l m h -> p l h m"), AX.X, ALU.add))
                hand_over(nc.vector.reciprocal(total[:], total[:]))
                hand_over(nc.vector.tensor_tensor(pr[:], pr[:], total[:].unsqueeze(2).to_broadcast([P, B, B, H2]), ALU.mult))
                dve.sem_inc(pr_for_pool, 1)
                hand_over(*[nc.vector.tensor_tensor(prod[l][:].rearrange("p m (h d) -> p m h d", h=H2),
                                                    qkv[n][:, :, 2 * D:3 * D].rearrange("p m (h d) -> p m h d", h=H2),
                                                    pr[:, l, :, :].unsqueeze(3).to_broadcast([P, B, H2, D2]), ALU.mult)
                            for l in range(3)])
                c.wait(v_product)
                hand_over(*[nc.vector.tensor_tensor(prod[l][:, 0:2, :], prod[l][:, 0:2, :], prod[l][:, 2:4, :], ALU.add)
                            for l in range(B)])
                hand_over(*[nc.vector.tensor_tensor(o[:, l, :], prod[l][:, 0, :], prod[l][:, 1, :], ALU.add)
                            for l in range(B)])
                dve.sem_inc(o_ready, 1)
                c.wait(y_copied)
                c.wait(hb_ready)
                for u in range(2):
                    c.wait(y_full)
                    nc.vector.tensor_tensor(y[:, 2 * u:2 * u + 2, :], y_ps[:, u, :].rearrange("p (b d) -> p b d", b=2),
                                            hb[n][:, 2 * u:2 * u + 2, :], ALU.add).then_inc(y_done, 1)
                c.wait(y_done, 2)
                dve.sem_inc(y_read, 2)
                dve.sem_inc(y_ready, 1)
                hand_over(*[nc.vector.bn_stats(st6[:, b, :], y[:, b, :]) for b in range(B)])
                hand_over(*[nc.vector.bn_aggr(st2[:, b, :], st6[:, b, :]) for b in range(B)])
                hand_over(nc.vector.tensor_copy(mean_rstd3[:].rearrange("p (b t) s -> p b t s", b=B)
                                                [:, :, bass.ds(tile, 1), :].rearrange("p b o s -> p b (o s)"), st2[:]))

            schedule(c, front, back)


def experts(nc, ins, hold):
    with ExitStack() as ctx:
        sb = lambda name, shape, dt=F32: ctx.enter_context(nc.sbuf_tensor(name, shape, dt))
        sem = lambda name: ctx.enter_context(nc.semaphore(name))
        ps = lambda name, shape: ctx.enter_context(nc.psum_tensor(name, shape, F32))
        R = 4
        NR = TILES // R
        mean_rstd3, y_all = hold["mean_rstd3"], hold["y_all"]
        slots_in, slots_out = hold["slots_in"], hold["slots_out"]
        g1, b1, g2, b2 = (sb(f"e_{n}", [P, D]) for n in ("g1", "b1", "g2", "b2"))
        gb, gain, shift = sb("e_gb", [P, B, D]), sb("e_gain", [P, B, D]), sb("e_shift", [P, B, D])
        ident, wg = sb("e_ident", [P, P]), sb("e_wg", [P, KC, E])
        w12, b12 = sb("e_w12", [P, E, KC, D]), sb("e_b12", [P, E, D])
        order, upto, ones = sb("e_order", [P, E]), sb("e_upto", [P, P], BF16), sb("e_ones", [P, P], BF16)
        upto32 = sb("e_upto32", [P, P])
        stat = [sb(f"e_stat_{n}", [P, R, 2]) for n in range(2)]
        y1 = [sb(f"e_y1_{n}", [P, R, D]) for n in range(2)]
        y1_t = [sb(f"e_y1_t_{n}", [P, KC, R * P]) for n in range(2)]
        logits, expo = sb("e_logits", [P, TILES, E]), sb("e_expo", [P, TILES, E])
        top, gate, first, kept = sb("e_top", [P, TILES]), sb("e_gate", [P, TILES]), sb("e_first", [P, TILES]), sb("e_kept", [P, TILES])
        hot, hot16 = sb("e_hot", [P, TILES, E]), sb("e_hot16", [P, TILES, E], BF16)
        sums = [sb(f"e_sums_{n}", [P, TILES, E]) for n in range(2)]
        place, slot, to, frm = sb("e_place", [P, TILES]), sb("e_slot", [P, TILES]), sb("e_to", [P, TILES]), sb("e_from", [P, TILES])
        to_i, frm_i = sb("e_to_i", [P, TILES], I32), sb("e_from_i", [P, TILES], I32)
        rows = [sb(f"e_rows_{n}", [P, R, D]) for n in range(2)]
        rows_t = [sb(f"e_rows_t_{n}", [P, KC, R * P]) for n in range(2)]
        res = [sb(f"e_res_{n}", [P, R, D]) for n in range(2)]
        got = sb("e_got", [P, TILES, D])
        st6, mr4 = sb("e_st6", [P, R, 6]), sb("e_mr4", [P, TILES, 2])
        x2 = [sb(f"e_x2_{n}", [P, R, D]) for n in range(2)]
        fin = [sb(f"e_fin_{n}", [P, R, D]) for n in range(2)]
        t_ps = [ps(f"e_t_ps{n}", [P, KC, HALF]) for n in range(2)]
        p_ps = [ps(f"e_p_ps{n}", [P, HALF]) for n in range(2)]
        q_ps = [ps(f"e_q_ps{n}", [P, HALF]) for n in range(2)]

        names = ("c_in", "w_in", "link", "var_ready", "std_ready", "y1_for_pe", "y1_for_act", "y1_free", "t_full", "t_read",
                 "logit_full", "logit_read", "logits_ready", "exp_in", "exp_out", "hot_ready", "count_ready", "to_ready",
                 "from_ready", "scattered", "rows_free", "rows_t_ready", "res_full", "res_read", "res_ready",
                 "all_out", "gain_ready", "z_ready", "xb_ready", "x2_free", "fin_ready", "init", "y_kept", "all_y")
        S = {n: sem("e_" + n) for n in names}
        rows_in, res_out = [sem("e_rows_in0"), sem("e_rows_in1")], [sem("e_res_out0"), sem("e_res_out1")]
        x2_in, fin_out = [sem("e_x2_in0"), sem("e_x2_in1")], [sem("e_fin_out0"), sem("e_fin_out1")]
        gathered = sem("e_gathered")
        block = ctx.enter_context(nc.Block())
        CONSTS = 16 * 12
        slots_v = slots_in.rearrange("(i n t p) d -> n p i t d", n=2, t=R, p=P)
        res_v = slots_out.rearrange("(i n t p) d -> n p i t d", n=2, t=R, p=P)
        x2_v = hold["x2"].rearrange("(b n t p) d -> n p b t d", n=2, t=R, p=P)
        out_v = hold["out"].rearrange("(b n t p) d -> n p b t d", n=2, t=R, p=P)

        @block.sync
        def _(sp):
            c = Counts(sp)
            for dst, src in ((g1, "g1"), (b1, "ln1_b"), (g2, "g2"), (b2, "ln2_b"), (order, "order")):
                sp.dma_start(dst[:], ins[src].partition_broadcast(P)).then_inc(S["c_in"], 16)
            sp.dma_start(ident[:], ins["ident"]).then_inc(S["c_in"], 16)
            sp.dma_start(upto32[:], ins["upto"]).then_inc(S["c_in"], 16)
            sp.dma_start(wg[:], ins["wg"].rearrange("(c p) e -> p c e", p=P)).then_inc(S["c_in"], 16)
            sp.dma_start(gb[:], hold["mod_rows"][1].partition_broadcast(P)).then_inc(S["c_in"], 16)
            for h in range(2):
                e = E // 2
                sp.dma_start(w12[:, h * e:(h + 1) * e, :, :], hold["w12"].rearrange("(e c p) n -> p e c n", c=KC, p=P)
                             [:, h * e:(h + 1) * e, :, :]).then_inc(S["c_in"], 16)
            sp.dma_start(b12[:], hold["b12"].partition_broadcast(P)).then_inc(S["c_in"], 16)
            sp.sem_inc(S["rows_free"], 2)
            sp.sem_inc(S["x2_free"], 2)
            sp.wait_ge(S["scattered"], 16 * TILES)
            with c.rounds(0, E // 2) as i:
                for n in range(2):
                    c.wait(S["rows_free"])
                    sp.dma_start(rows[n][:], slots_v[n][:, bass.ds(i, 1), :, :].rearrange("p o t d -> p (o t) d"))\
                      .then_inc(rows_in[n], 16)
            with c.rounds(0, B) as b:
                for n in range(2):
                    c.wait(S["x2_free"])
                    sp.dma_start(x2[n][:], x2_v[n][:, bass.ds(b, 1), :, :].rearrange("p o t d -> p (o t) d"))\
                      .then_inc(x2_in[n], 16)

        @block.tensor
        def _(pe):
            c = Counts(pe)
            pe.wait_ge(S["c_in"], CONSTS)
            with c.rounds(0, NR // 2):
                for n in range(2):
                    c.wait(S["y1_for_pe"])
                    for k in range(KC):
                        for t in range(R):
                            last = nc.tensor.transpose(t_ps[n][:, k, t * P:(t + 1) * P], y1[n][:, t, k * P:(k + 1) * P], ident[:])
                        last.then_inc(S["t_full"], 1)
                    c.wait(S["t_read"], KC)
                    c.wait(S["logit_read"])
                    for t in range(R):
                        for k in range(KC):
                            last = nc.tensor.matmul(p_ps[n][:, t * E:(t + 1) * E], y1_t[n][:, k, t * P:(t + 1) * P], wg[:, k, :],
                                                    start=(k == 0), stop=(k == KC - 1))
                    last.then_inc(S["logit_full"], 1)
            pe.wait_ge(S["init"], 2)
            c.wait(S["hot_ready"])
            flat = hot16[:].rearrange("p t e -> p (t e)")
            nc.tensor.matmul(q_ps[0][:, 0:TILES * E], upto[:], flat, start=True, stop=True)
            nc.tensor.matmul(q_ps[1][:, 0:TILES * E], ones[:], flat, start=True, stop=True).then_inc(S["count_ready"], 1)
            with c.rounds(0, E // 2) as i:
                for n in range(2):
                    c.wait(rows_in[n], 16)
                    for k in range(KC):
                        for t in range(R):
                            last = nc.tensor.transpose(t_ps[n][:, k, t * P:(t + 1) * P], rows[n][:, t, k * P:(k + 1) * P], ident[:])
                        last.then_inc(S["t_full"], 1)
                    c.wait(S["t_read"], KC)
                    c.wait(S["res_read"], 2)
                    for u in range(2):
                        for t in (2 * u, 2 * u + 1):
                            for k in range(KC):
                                last = nc.tensor.matmul(p_ps[u][:, (t % 2) * D:(t % 2 + 1) * D], rows_t[n][:, k, t * P:(t + 1) * P],
                                                        w12[:, bass.ds(2 * i + n, 1), k, :].rearrange("p o n -> p (o n)"),
                                                        start=(k == 0), stop=(k == KC - 1))
                        last.then_inc(S["res_full"], 1)

        @block.scalar
        def _(act):
            c = Counts(act)
            c.wait(S["var_ready"])
            nc.scalar.activation(mean_rstd3[:, :, 1], mean_rstd3[:, :, 1], ACT.Sqrt).then_inc(S["std_ready"], 1)
            act.sem_inc(S["logit_read"], 2)
            with c.rounds(0, NR // 2) as i:
                for n in range(2):
                    tiles = bass.ds(2 * R * i + R * n, R)
                    for k in range(KC):
                        c.wait(S["t_full"])
                        nc.scalar.activation(y1_t[n][:, k, :], t_ps[n][:, k, :], ACT.Copy).then_inc(S["t_read"], 1)
                    c.wait(S["y1_for_act"])
                    nc.scalar.activation(y_all[:, tiles, :], y1[n][:], ACT.Copy).then_inc(S["y_kept"], 1)
                    c.wait(S["logit_full"])
                    nc.scalar.activation(logits[:, tiles, :].rearrange("p t e -> p (t e)"), p_ps[n][:, 0:R * E], ACT.Copy)\
                        .then_inc(S["logits_ready"], 1)
                    c.wait(S["logits_ready"])
                    act.sem_inc(S["logit_read"], 1)
            act.sem_inc(S["all_y"], 1)
            c.wait(S["exp_in"])
            nc.scalar.activation(expo[:], expo[:], ACT.Exp).then_inc(S["exp_out"], 1)
            with c.rounds(0, E // 2) as i:
                for n in range(2):
                    for k in range(KC):
                        c.wait(S["t_full"])
                        nc.scalar.activation(rows_t[n][:, k, :], t_ps[n][:, k, :], ACT.Copy).then_inc(S["t_read"], 1)
                    act.sem_inc(S["rows_free"], 1)
                    c.wait(S["res_ready"])
                    act.dma_start(res_v[n][:, bass.ds(i, 1), :, :].rearrange("p o t d -> p (o t) d"), res[n][:])\
                       .then_inc(res_out[n], 16)
            c.wait(S["var_ready"])
            nc.scalar.activation(mr4[:, :, 1], mr4[:, :, 1], ACT.Sqrt).then_inc(S["std_ready"], 1)
            with c.rounds(0, B) as b:
                for n in range(2):
                    c.wait(S["fin_ready"])
                    act.dma_start(out_v[n][:, bass.ds(b, 1), :, :].rearrange("p o t d -> p (o t) d"), fin[n][:])\
                       .then_inc(fin_out[n], 16)

        @block.gpsimd
        def _(pool):
            c = Counts(pool)
            nc.gpsimd.memset(ones[:], 1.0).then_inc(S["init"], 1)
            pool.wait_ge(S["c_in"], CONSTS)
            pool.wait_ge(S["init"], 1)
            nc.gpsimd.tensor_copy(upto[:], upto32[:]).then_inc(S["init"], 1)
            pool.wait_ge(S["init"], 2)
            nc.gpsimd.tensor_tensor(gain[:], gb[:], g2[:].unsqueeze(1).to_broadcast([P, B, D]), ALU.mult).then_inc(S["init"], 1)
            pool.wait_ge(S["init"], 3)
            nc.gpsimd.tensor_tensor(shift[:], gb[:], b2[:].unsqueeze(1).to_broadcast([P, B, D]), ALU.mult).then_inc(S["init"], 1)
            pool.wait_ge(S["init"], 4)
            c.wait(S["to_ready"])
            for t in range(TILES):
                nc.gpsimd.indirect_dma_start(
                    out=slots_in, out_offset=bass.IndirectOffsetOnAxis(ap=to_i[:, t:t + 1], axis=0),
                    in_=y_all[:, t, :], in_offset=None, bounds_check=E * CAP - 1, oob_is_err=False)\
                    .then_inc(S["scattered"], 16)
            c.wait(S["from_ready"])
            c.wait(S["all_out"])
            for t in range(TILES):
                nc.gpsimd.indirect_dma_start(
                    out=got[:, t, :], out_offset=None, in_=slots_out,
                    in_offset=bass.IndirectOffsetOnAxis(ap=frm_i[:, t:t + 1], axis=0)).then_inc(gathered, 16)
            with c.rounds(0, B) as b:
                for n in range(2):
                    c.wait(x2_in[n], 16)
                    nc.gpsimd.tensor_tensor(x2[n][:], x2[n][:], shift[:, bass.ds(b, 1), :].to_broadcast([P, R, D]), ALU.add)\
                        .then_inc(S["xb_ready"], 1)

        @block.vector
        def _(dve):
            c = Counts(dve)

            def hand_over(*instructions):
                for ins_ in instructions:
                    ins_.then_inc(S["link"], 1)
                c.wait(S["link"], len(instructions))

            hand_over(nc.vector.tensor_scalar(mean_rstd3[:, :, 1], mean_rstd3[:, :, 1], EPS, None, ALU.add))
            dve.sem_inc(S["var_ready"], 1)
            c.wait(S["std_ready"])
            hand_over(nc.vector.reciprocal(mean_rstd3[:, :, 1], mean_rstd3[:, :, 1]))
            dve.wait_ge(S["c_in"], CONSTS)
            dve.sem_inc(S["y_kept"], 2)
            with c.rounds(0, NR // 2) as i:
                for n in range(2):
                    tile = 2 * R * i + R * n
                    c.wait(S["y_kept"])
                    hand_over(nc.vector.tensor_copy(stat[n][:], mean_rstd3[:, bass.ds(tile, R), :]))
                    hand_over(*[nc.vector.scalar_tensor_tensor(
                        y1[n][:, t, :], y_all[:, bass.ds(tile + t, 1), :].rearrange("p o d -> p (o d)"), stat[n][:, t, 0:1], g1[:],
                        ALU.subtract, ALU.mult) for t in range(R)])
                    hand_over(*[nc.vector.scalar_tensor_tensor(y1[n][:, t, :], y1[n][:, t, :], stat[n][:, t, 1:2], b1[:],
                                                               ALU.mult, ALU.add) for t in range(R)])
                    dve.sem_inc(S["y1_for_pe"], 1)
                    dve.sem_inc(S["y1_for_act"], 1)
            c.wait(S["all_y"])
            wide = lambda a: a[:].unsqueeze(2).to_broadcast([P, TILES, E])
            hand_over(nc.vector.tensor_reduce(top[:], logits[:], AX.X, ALU.max))
            hand_over(nc.vector.tensor_tensor(expo[:], logits[:], wide(top), ALU.subtract),
                      nc.vector.tensor_tensor(hot[:], logits[:], wide(top), ALU.is_ge))
            dve.sem_inc(S["exp_in"], 1)
            hand_over(nc.vector.tensor_tensor(hot[:], hot[:], order[:].unsqueeze(1).to_broadcast([P, TILES, E]), ALU.mult))
            hand_over(nc.vector.tensor_reduce(first[:], hot[:], AX.X, ALU.max))
            hand_over(nc.vector.tensor_tensor(hot[:], hot[:], wide(first), ALU.is_equal))
            hand_over(nc.vector.tensor_copy(hot16[:], hot[:]))
            dve.sem_inc(S["hot_ready"], 1)
            c.wait(S["count_ready"])
            a, b = sums
            hand_over(nc.vector.memset(a[:, 0:1, :], 0.0),
                      nc.vector.tensor_copy(a[:, 1:TILES, :].rearrange("p t e -> p (t e)"), q_ps[1][:, 0:(TILES - 1) * E]))
            step = 1
            while step < TILES:
                hand_over(nc.vector.tensor_copy(b[:, 0:step, :], a[:, 0:step, :]),
                          nc.vector.tensor_tensor(b[:, step:, :], a[:, step:, :], a[:, 0:TILES - step, :], ALU.add))
                a, b = b, a
                step *= 2
            hand_over(nc.vector.tensor_tensor(a[:].rearrange("p t e -> p (t e)"), a[:].rearrange("p t e -> p (t e)"),
                                              q_ps[0][:, 0:TILES * E], ALU.add))
            hand_over(nc.vector.tensor_tensor(a[:], a[:], hot[:], ALU.mult))
            hand_over(nc.vector.tensor_reduce(place[:], a[:], AX.X, ALU.add))
            hand_over(nc.vector.tensor_scalar(slot[:], first[:], -float(CAP), float(E * CAP - 1), ALU.mult, ALU.add),
                      nc.vector.tensor_scalar(kept[:], place[:], float(CAP), None, ALU.is_le))
            hand_over(nc.vector.tensor_tensor(slot[:], slot[:], place[:], ALU.add),
                      nc.vector.tensor_scalar(to[:], kept[:], -float(2 * E * CAP), float(2 * E * CAP), ALU.mult, ALU.add))
            hand_over(nc.vector.tensor_tensor(to[:], to[:], slot[:], ALU.add),
                      nc.vector.tensor_scalar(frm[:], slot[:], float(E * CAP - 1), None, ALU.min))
            hand_over(nc.vector.tensor_copy(to_i[:], to[:]), nc.vector.tensor_copy(frm_i[:], frm[:]))
            dve.sem_inc(S["to_ready"], 1)
            dve.sem_inc(S["from_ready"], 1)
            c.wait(S["exp_out"])
            hand_over(nc.vector.tensor_reduce(gate[:], expo[:], AX.X, ALU.add))
            hand_over(nc.vector.reciprocal(gate[:], gate[:]))
            hand_over(nc.vector.tensor_tensor(gate[:], gate[:], kept[:], ALU.mult))
            dve.sem_inc(S["res_read"], 2)
            for n in range(2):
                dve.sem_inc(res_out[n], 16)
            with c.rounds(0, E // 2) as i:
                for n in range(2):
                    c.wait(res_out[n], 16)
                    for u in range(2):
                        c.wait(S["res_full"])
                        hand_over(nc.vector.tensor_tensor(
                            res[n][:, 2 * u:2 * u + 2, :], p_ps[u][:].rearrange("p (t d) -> p t d", t=2),
                            b12[:, bass.ds(2 * i + n, 1), :].to_broadcast([P, 2, D]), ALU.add))
                        dve.sem_inc(S["res_read"], 1)
                    dve.sem_inc(S["res_ready"], 1)
            for n in range(2):
                c.wait(res_out[n], 16)
            dve.sem_inc(S["all_out"], 1)
            dve.wait_ge(gathered, 16 * TILES)
            with c.rounds(0, NR) as r:
                tiles = bass.ds(R * r, R)
                hand_over(nc.vector.tensor_copy(stat[0][:, :, 0], gate[:, tiles]))
                hand_over(*[nc.vector.scalar_tensor_tensor(
                    y1[0][:, t, :], got[:, bass.ds(R * r + t, 1), :].rearrange("p o d -> p (o d)"), stat[0][:, t, 0:1],
                    y_all[:, bass.ds(R * r + t, 1), :].rearrange("p o d -> p (o d)"), ALU.mult, ALU.add) for t in range(R)])
                hand_over(nc.vector.tensor_copy(y_all[:, tiles, :], y1[0][:]),
                          *[nc.vector.bn_stats(st6[:, t, :], y1[0][:, t, :]) for t in range(R)])
                hand_over(*[nc.vector.bn_aggr(stat[1][:, t, :], st6[:, t, :]) for t in range(R)])
                hand_over(nc.vector.tensor_copy(mr4[:, tiles, :], stat[1][:]))
            hand_over(nc.vector.tensor_scalar(mr4[:, :, 1], mr4[:, :, 1], EPS, None, ALU.add))
            dve.sem_inc(S["var_ready"], 1)
            c.wait(S["std_ready"])
            hand_over(nc.vector.reciprocal(mr4[:, :, 1], mr4[:, :, 1]))
            for n in range(2):
                dve.sem_inc(fin_out[n], 16)
            dve.wait_ge(S["init"], 4)
            with c.rounds(0, B) as b:
                for n in range(2):
                    tile = NT * b + R * n
                    c.wait(fin_out[n], 16)
                    hand_over(nc.vector.tensor_copy(stat[n][:], mr4[:, bass.ds(tile, R), :]))
                    gain_b = gain[:, bass.ds(b, 1), :].rearrange("p o d -> p (o d)")
                    hand_over(*[nc.vector.scalar_tensor_tensor(
                        y1[n][:, t, :], y_all[:, bass.ds(tile + t, 1), :].rearrange("p o d -> p (o d)"), stat[n][:, t, 0:1], gain_b,
                        ALU.subtract, ALU.mult) for t in range(R)])
                    c.wait(S["xb_ready"])
                    hand_over(*[nc.vector.scalar_tensor_tensor(fin[n][:, t, :], y1[n][:, t, :], stat[n][:, t, 1:2], x2[n][:, t, :],
                                                               ALU.mult, ALU.add) for t in range(R)])
                    dve.sem_inc(S["x2_free"], 1)
                    dve.sem_inc(S["fin_ready"], 1)
            for n in range(2):
                c.wait(fin_out[n], 16)


def build(nc, ins, outs, stop=None):
    with ExitStack() as ctx:
        sb = lambda name, shape, dt=F32: ctx.enter_context(nc.sbuf_tensor(name, shape, dt))
        dram = lambda name, shape, dt=F32: nc.dram_tensor(name, shape, dt, kind="Internal").ap()
        hold = {
            "mean_rstd1": sb("mean_rstd1", [P, TILES, 2]),
            "mean_rstd2": sb("mean_rstd2", [P, TILES, 2]),
            "ca1_sa": sb("ca1_sa", [P, 2, KC, B]),
            "mod_rows": dram("mod_rows", (4, B, D)),
            "qk_scratch": dram("qk_scratch", (2, 3, D, T), BF16),
            "x2": outs["dbg_x2"] if stop else dram("x2", (B * T, D)),
            "w12": dram("w12", (E * D, D)),
            "b12": dram("b12", (E, D)),
            "slots_in": dram("slots_in", (E * CAP, D)),
            "slots_out": dram("slots_out", (E * CAP, D)),
            "out": outs["out"],
        }
        fold_experts(nc, ins, hold)
        prepare(nc, ins, hold)
        attention(nc, ins, hold)
        hold["mean_rstd3"] = sb("mean_rstd3", [P, TILES, 2])
        hold["y_all"] = sb("y_all", [P, TILES, D])
        batch_attention(nc, ins, hold)
        if not stop:
            experts(nc, ins, hold)
        if stop:
            with ExitStack() as c2:
                done = c2.enter_context(nc.semaphore("dbg_done"))
                block = c2.enter_context(nc.Block())

                @block.sync
                def _(sp):
                    sp.dma_start(outs["dbg_y"].rearrange("(t p) d -> p t d", p=P), hold["y_all"][:]).then_inc(done, 16)
                    sp.dma_start(outs["dbg_w12"], hold["w12"]).then_inc(done, 16)
                    sp.dma_start(outs["dbg_b12"], hold["b12"]).then_inc(done, 16)
                    sp.wait_ge(done, 48)


def layouts(i):
    import numpy as np
    order = np.arange(D).reshape(H1, DH // 2, 2).transpose(0, 2, 1).reshape(D)
    half = DH // 2
    theta = np.float32(1.0) / np.float32(10000.0) ** (np.arange(half, dtype=np.float32) / np.float32(half))
    angle = (np.arange(T, dtype=np.float32)[:, None] * theta[None, :]).astype(np.float32).T
    c, s = np.cos(angle), np.sin(angle)
    t = lambda a: np.ascontiguousarray(np.asarray(a).T)
    wq, wk = t(i["L0_attn_W_q"])[:, order], t(i["L0_attn_W_k"])[:, order]
    bq, bk = np.asarray(i["L0_attn_b_q"])[order], np.asarray(i["L0_attn_b_k"])[order]
    row, col = np.arange(P)[:, None], np.arange(HALF)[None, :]
    return {
        "x": np.asarray(i["L0_attn_x"]).reshape(B * T, D),
        "c_t": t(i["L0_c"]),
        "wmod": np.asarray(i["L0_wmod"]),
        "wqk": np.concatenate([wq, wk], 1),
        "bqk": np.ascontiguousarray(np.concatenate([bq, bk]).reshape(SLOTS, P).T),
        "wv": t(i["L0_attn_W_v"]), "bv": np.asarray(i["L0_attn_b_v"]),
        "wo": t(i["L0_attn_W_o"]), "bo": np.asarray(i["L0_attn_b_o"]),
        "w1_t": np.ascontiguousarray(np.asarray(i["L0_ffn_w1"]).transpose(0, 2, 1)).reshape(E * FF, D),
        "w2": np.asarray(i["L0_ffn_w2"]).reshape(E * FF, D),
        "b1_t": np.ascontiguousarray(np.asarray(i["L0_ffn_b1"]).reshape(E, FC, P).transpose(0, 2, 1)),
        "b2": np.asarray(i["L0_ffn_b2"]),
        "g1": np.asarray(i["L0_ffn_ln1_g"]), "ln1_b": np.asarray(i["L0_ffn_ln1_b"]),
        "g2": np.asarray(i["L0_ffn_ln2_g"]), "ln2_b": np.asarray(i["L0_ffn_ln2_b"]),
        "wg": np.asarray(i["L0_ffn_wg"]),
        "order": np.arange(E, 0, -1).astype(np.float32),
        "upto": np.triu(np.ones((P, P), np.float32)),
        "w_in": t(i["L0_ffn_in_proj_w"]), "b_in": np.asarray(i["L0_ffn_in_proj_b"]),
        "w_out": t(i["L0_ffn_out_proj_w"]), "b_out": np.asarray(i["L0_ffn_out_proj_b"]),
        "cos": np.tile(np.concatenate([c, c]), (P // DH, 1)).astype(np.float32),
        "sin": np.tile(np.concatenate([s, -s]), (P // DH, 1)).astype(np.float32),
        "ident": np.eye(P, dtype=np.float32),
        "tri": np.where(col - (HALF - P) > row, np.float32(-1e30), np.float32(0)).astype(np.float32),
        "after": np.where(row > col[:, :P], np.float32(-1e30), np.float32(0)).astype(np.float32),
    }


def kernel(**inputs):
    import numpy as np
    import concourse.bacc as bacc
    from concourse.bass_utils import run_bass_kernel_spmd as run

    nc = bacc.Bacc("TRN2", target_bir_lowering=False, num_devices=1)
    arrays = {f"in_{name}": np.ascontiguousarray(a) for name, a in layouts(inputs).items()}
    ins = {name[3:]: nc.dram_tensor(name, a.shape, mybir.dt.from_np(a.dtype), kind="ExternalInput").ap()
           for name, a in arrays.items()}
    out = nc.dram_tensor("out_dram", (B * T, D), F32, kind="ExternalOutput").ap()
    build(nc, ins, {"out": out})
    r = run(nc, [arrays], core_ids=[0])
    return r.results[0]["out_dram"].reshape(B, T, D)
```

```python
from contextlib import ExitStack, contextmanager

import concourse.bass as bass
from concourse import mybir

F32 = mybir.dt.float32
BF16 = mybir.dt.bfloat16
I32 = mybir.dt.int32
U32 = mybir.dt.uint32
ALU = mybir.AluOpType
ACT = mybir.ActivationFunctionType
AX = mybir.AxisListType

P = 128
B = 4
T = 1024
D = 256
KC = D // P
NT = T // P
TILES = B * NT
H1 = 16
DH = D // H1
J = 4
G = H1 // J
HALF = 512
E = 8
FF = 1024
FC = FF // P
CAP = B * T // E
EPS = 1e-5
LOWEST = -3.0e38

Q_PART = (0, 0, 0, 1, 1, 2)
K_PART = (0, 1, 2, 0, 1, 0)
SROWS = len(Q_PART) * DH
MROWS = 3


class Counts:

    def __init__(self, eng):
        self.eng, self.seen = eng, {}

    def wait(self, sem, n=1):
        name = sem.name
        self.seen[name] = (sem, self.seen.get(name, (sem, 0))[1] + n)
        self.eng.wait_ge(sem, self.seen[name][1])

    @contextmanager
    def rounds(self, start, end):
        with self.eng.Fori(start, end) as i:
            before = dict(self.seen)
            yield i
            for name, (sem, n) in self.seen.items():
                more = n - before.get(name, (sem, 0))[1]
                if more:
                    self.eng.sem_inc(sem, -more)
            self.seen = {name: (sem, before.get(name, (sem, 0))[1]) for name, (sem, _) in self.seen.items()}


def fold_experts(nc, ins, hold):
    with ExitStack() as ctx:
        sb = lambda name, shape, dt=F32: ctx.enter_context(nc.sbuf_tensor(name, shape, dt))
        sem = lambda name: ctx.enter_context(nc.semaphore(name))
        w1 = [sb(f"f_w1_{n}", [P, FC, D]) for n in range(2)]
        w2 = [sb(f"f_w2_{n}", [P, FC, D]) for n in range(2)]
        b1 = [sb(f"f_b1_{n}", [P, FC]) for n in range(2)]
        b2 = [sb(f"f_b2_{n}", [1, D]) for n in range(2)]
        w12 = [sb(f"f_w12_{n}", [P, KC, D]) for n in range(2)]
        b12 = [sb(f"f_b12_{n}", [1, D]) for n in range(2)]
        zero = sb("f_zero", [P, 4 * D])
        w_ps = [ctx.enter_context(nc.psum_tensor(f"f_w_ps{n}", [P, KC, D], F32)) for n in range(2)]
        b_ps = [ctx.enter_context(nc.psum_tensor(f"f_b_ps{n}", [1, HALF], F32)) for n in range(2)]
        w_in = [sem("f_w_in0"), sem("f_w_in1")]
        w12_out = [sem("f_w12_out0"), sem("f_w12_out1")]
        w_free, ps_free, b2_ready, product = sem("f_w_free"), sem("f_ps_free"), sem("f_b2_ready"), sem("f_product")
        w12_ready, b12_ready, zero_ready, zero_out = sem("f_w12_ready"), sem("f_b12_ready"), sem("f_zero_ready"), sem("f_zero_out")
        block = ctx.enter_context(nc.Block())

        @block.sync
        def _(sp):
            c = Counts(sp)
            sp.sem_inc(w_free, 2)
            with c.rounds(0, E // 2) as i:
                for n in range(2):
                    c.wait(w_free)
                    for dst, src in ((w1[n], "w1_t"), (w2[n], "w2")):
                        src = ins[src].rearrange("(i n c p) d -> n p i c d", n=2, c=FC, p=P)[n]
                        sp.dma_start(dst[:], src[:, bass.ds(i, 1), :, :].rearrange("p o c d -> p (o c) d"))\
                          .then_inc(w_in[n], 16)
                    sp.dma_start(b1[n][:], ins["b1_t"].rearrange("(i n) p c -> n p i c", n=2)[n][:, bass.ds(i, 1), :]
                                 .rearrange("p o c -> p (o c)")).then_inc(w_in[n], 16)
                    sp.dma_start(b2[n][:], ins["b2"].rearrange("(i n) d -> n i d", n=2)[n][bass.ds(i, 1), :])\
                      .then_inc(w_in[n], 16)
            sp.wait_ge(zero_ready, 1)
            slots = hold["slots_in"].rearrange("(r p t) d -> r p (t d)", p=P, t=4)
            for r in range(E):
                sp.dma_start(slots[r], zero[:]).then_inc(zero_out, 16)
            sp.wait_ge(zero_out, 16 * E)

        @block.tensor
        def _(pe):
            c = Counts(pe)
            with c.rounds(0, E // 2):
                for n in range(2):
                    c.wait(w_in[n], 64)
                    c.wait(ps_free)
                    for m in range(KC):
                        for f in range(FC):
                            nc.tensor.matmul(w_ps[n][:, m, :], w1[n][:, f, m * P:(m + 1) * P], w2[n][:, f, :],
                                             start=(f == 0), stop=(f == FC - 1))
                    for f in range(FC):
                        last = nc.tensor.matmul(b_ps[n][0:1, 0:D], b1[n][:, f:f + 1], w2[n][:, f, :],
                                                start=(f == 0), stop=(f == FC - 1))
                    last.then_inc(product, 1)

        @block.vector
        def _(dve):
            c = Counts(dve)
            nc.vector.memset(zero[:], 0.0).then_inc(zero_ready, 1)
            for n in range(2):
                dve.sem_inc(w12_out[n], 32)
            with c.rounds(0, E // 2):
                for n in range(2):
                    c.wait(w12_out[n], 32)
                    c.wait(product)
                    nc.vector.tensor_tensor(b12[n][:], b2[n][:], b_ps[n][0:1, 0:D], ALU.add).then_inc(b12_ready, 1)
                    nc.vector.tensor_copy(w12[n][:], w_ps[n][:]).then_inc(w12_ready, 1)
            for n in range(2):
                c.wait(w12_out[n], 32)

        @block.scalar
        def _(act):
            c = Counts(act)
            act.sem_inc(ps_free, 2)
            w12_dram = hold["w12"].rearrange("(i n m p) d -> n p i m d", n=2, m=KC, p=P)
            b12_dram = hold["b12"].rearrange("(i n) d -> n i d", n=2)
            with c.rounds(0, E // 2) as i:
                for n in range(2):
                    c.wait(b12_ready)
                    c.wait(w12_ready)
                    act.sem_inc(ps_free, 1)
                    act.sem_inc(w_free, 1)
                    act.dma_start(b12_dram[n][bass.ds(i, 1), :], b12[n][:]).then_inc(w12_out[n], 16)
                    act.dma_start(w12_dram[n][:, bass.ds(i, 1), :, :].rearrange("p o m d -> p (o m) d"), w12[n][:])\
                       .then_inc(w12_out[n], 16)


def prepare(nc, ins, hold):
    x, c_t, wmod = ins["x"], ins["c_t"], ins["wmod"]
    with ExitStack() as ctx:
        sb = lambda name, shape, dt=F32: ctx.enter_context(nc.sbuf_tensor(name, shape, dt))
        sem = lambda name: ctx.enter_context(nc.semaphore(name))
        xs = sb("p_x", [P, TILES, D])
        wm = sb("p_wmod", [P, KC, 6 * D])
        cs = sb("p_c", [P, KC, B])
        sil = sb("p_silu", [P, KC, B])
        stats = sb("p_stats", [P, TILES, 6])
        rows = sb("p_rows", [B, 6, D])
        sign = sb("p_sign", [B, 2, D])
        mag = sb("p_mag", [B, 2, D])
        rows_ps = ctx.enter_context(nc.psum_tensor("p_rows_ps", [B, 3, HALF], F32))
        cols_ps = ctx.enter_context(nc.psum_tensor("p_cols_ps", [P, 2, KC, B], F32))
        x_in, w_in, c_in, out_done = sem("p_x_in"), sem("p_w_in"), sem("p_c_in"), sem("p_out")
        bn_done, var_ready, std_ready, stat_link = sem("p_bn"), sem("p_var"), sem("p_std"), sem("p_link")
        exp_ready, silu_ready, mod_ready, rows_ready = sem("p_exp"), sem("p_silu_r"), sem("p_mod"), sem("p_rows_r")
        mean_rstd, ca1_sa = hold["mean_rstd1"], hold["ca1_sa"]
        block = ctx.enter_context(nc.Block())

        @block.sync
        def _(sp):
            sp.dma_start(cs[:], c_t.rearrange("(c p) b -> p c b", p=P)).then_inc(c_in, 16)
            sp.dma_start(wm[:], wmod.rearrange("(c p) n -> p c n", p=P)).then_inc(w_in, 16)
            for b in range(B):
                if b:
                    sp.wait_ge(x_in, 16 * b)
                sp.dma_start(xs[:, NT * b:NT * (b + 1), :],
                             x[T * b:T * (b + 1), :].rearrange("(t p) d -> p t d", p=P)).then_inc(x_in, 16)
            sp.wait_ge(rows_ready, 2)
            for n, row in enumerate((2, 5, 4, 3)):
                sp.dma_start(hold["mod_rows"][n], rows[:, row, :]).then_inc(out_done, 16)
            sp.wait_ge(out_done, 64)

        @block.tensor
        def _(pe):
            pe.wait_ge(silu_ready, 1)
            pe.wait_ge(w_in, 16)
            for n in range(3):
                for c in range(KC):
                    last = nc.tensor.matmul(rows_ps[:, n, :], sil[:, c, :], wm[:, c, n * HALF:(n + 1) * HALF],
                                            start=(c == 0), stop=(c == KC - 1))
            for n in range(2):
                for m in range(KC):
                    for c in range(KC):
                        last = nc.tensor.matmul(cols_ps[:, n, m, :], wm[:, c, n * D + m * P:n * D + (m + 1) * P],
                                                sil[:, c, :], start=(c == 0), stop=(c == KC - 1))
            last.then_inc(mod_ready, 1)

        @block.scalar
        def _(act):
            act.wait_ge(c_in, 16)
            nc.scalar.activation(sil[:], cs[:], ACT.Exp, scale=-1.0).then_inc(exp_ready, 1)
            act.wait_ge(var_ready, 1)
            nc.scalar.activation(mean_rstd[:, :, 1], mean_rstd[:, :, 1], ACT.Sqrt).then_inc(std_ready, 1)

        @block.vector
        def _(dve):
            dve.wait_ge(exp_ready, 1)
            nc.vector.tensor_scalar(sil[:], sil[:], 1.0, None, ALU.add).then_inc(stat_link, 1)
            dve.wait_ge(stat_link, 1)
            nc.vector.reciprocal(sil[:], sil[:]).then_inc(stat_link, 1)
            dve.wait_ge(stat_link, 2)
            nc.vector.tensor_tensor(sil[:], sil[:], cs[:], ALU.mult).then_inc(silu_ready, 1)
            for t in range(TILES):
                if t % NT == 0:
                    dve.wait_ge(x_in, 16 * (t // NT + 1))
                nc.vector.bn_stats(stats[:, t, :], xs[:, t, :]).then_inc(bn_done, 1)
            for t in range(TILES):
                dve.wait_ge(bn_done, t + 1)
                last = nc.vector.bn_aggr(mean_rstd[:, t, :], stats[:, t, :]).then_inc(stat_link, 1)
            dve.wait_ge(stat_link, 2 + TILES)
            nc.vector.tensor_scalar(mean_rstd[:, :, 1], mean_rstd[:, :, 1], EPS, None, ALU.add).then_inc(var_ready, 1)
            dve.wait_ge(mod_ready, 1)
            flat = rows[:].rearrange("b s d -> b (s d)")
            nc.vector.tensor_copy(flat, rows_ps[:].rearrange("b n f -> b (n f)")).then_inc(rows_ready, 1)
            dve.wait_ge(rows_ready, 1)
            gates = rows[:].rearrange("b (n s) d -> b n s d", s=3)[:, :, 2, :]
            nc.vector.tensor_scalar(sign[:], gates, 0.0, 2.0, ALU.is_ge, ALU.mult).then_inc(stat_link, 1)
            nc.vector.scalar_tensor_tensor(mag[:], gates, -1.0, gates, ALU.mult, ALU.max).then_inc(stat_link, 1)
            dve.wait_ge(stat_link, 4 + TILES)
            nc.vector.tensor_scalar(sign[:], sign[:], 1.0, None, ALU.subtract).then_inc(stat_link, 1)
            nc.vector.tensor_scalar(mag[:], mag[:], 0.25, None, ALU.max).then_inc(stat_link, 1)
            nc.vector.tensor_scalar(rows[:, 4, :], rows[:, 4, :], 1.0, None, ALU.add).then_inc(stat_link, 1)
            dve.wait_ge(stat_link, 7 + TILES)
            nc.vector.tensor_tensor(gates, sign[:], mag[:], ALU.mult).then_inc(rows_ready, 1)
            nc.vector.tensor_scalar(ca1_sa[:, 0, :, :], cols_ps[:, 1, :, :], 1.0, None, ALU.add).then_inc(stat_link, 1)
            nc.vector.tensor_copy(ca1_sa[:, 1, :, :], cols_ps[:, 0, :, :]).then_inc(stat_link, 1)
            dve.wait_ge(std_ready, 1)
            nc.vector.reciprocal(mean_rstd[:, :, 1], mean_rstd[:, :, 1]).then_inc(stat_link, 1)


SLOTS = 4
CHUNKS = J * 12
STEPS = 12
PT_BUFS = 3

CHUNK = []
for _qt in range(NT):
    if _qt < 4:
        CHUNK.append((_qt, 0, (_qt + 1) * P, True))
    else:
        CHUNK.append((_qt, 0, HALF, False))
        CHUNK.append((_qt, HALF, (_qt - 3) * P, True))

STEP = []
for _qh in range(2):
    for _kb in range(4 * _qh + 4):
        STEP.append((_qh, _kb, max(0, _kb - 4 * _qh) * P, _kb >= 4 * _qh))

PIECES = 9
PLACES = [(g, s) for g in range(G) for s in range(STEPS)] + [(G, i) for i in range(PIECES)]

TRANSPOSES, QK_USES, V_USES = 2 * KC, 2 * SLOTS, NT // 2
PROJECT = TRANSPOSES + QK_USES + V_USES
PROJECT_AT = {(0, 6): (0, 1), (0, 7): (2, 3)}
for _n in range(TRANSPOSES, PROJECT):
    PROJECT_AT[divmod(8 + _n - TRANSPOSES, STEPS)] = (_n,)


def at(place, first, every=2):
    s, rest = divmod(place[0] * STEPS + place[1] - first, every)
    return s if rest == 0 and 0 <= s < SLOTS and place[0] < G else None


EARLY = 2 * (PIECES - 1)
EARLY_STEP = STEPS - EARLY // 4


def chunks_at(place, last):
    g, s = place
    if g >= G - 1 and last:
        return []
    if g == G:
        return [(G + 1, ch) for ch in range(2 * s - 2, 2 * s)] if s else []
    if g == G - 1:
        return [(G, ch) for ch in range(4 * s, 4 * s + 4)]
    if g == 0 and s < EARLY_STEP:
        rest, steps = CHUNKS - EARLY, EARLY_STEP - 1
        return [(1, ch) for ch in range(EARLY + rest * max(s - 1, 0) // steps, EARLY + rest * s // steps)]
    if s < EARLY_STEP:
        return [(g + 1, ch) for ch in range(EARLY + 4 * s, EARLY + 4 * s + 4)]
    return [(g + 2, ch) for ch in range(4 * (s - EARLY_STEP), 4 * (s - EARLY_STEP) + 4)] if g + 2 < G else []


def bank_turns(last):
    turns = {}
    for place in PLACES:
        for n in () if last else PROJECT_AT.get(place, ()):
            turns["project", n] = len(turns)
        for chunk in chunks_at(place, last):
            turns[chunk] = len(turns)
    return turns


FIRST_TURNS = {("project", n): n for n in range(PROJECT)}
FIRST_TURNS.update({(G, ch): PROJECT + ch for ch in range(CHUNKS)})
FIRST_TURNS.update({(G + 1, ch): PROJECT + CHUNKS + ch for ch in range(EARLY)})
MISC_TURNS = 20


def misc_turn(kind, g=0, qh=0):
    if kind == "maxima":
        return 3 * g - 2 if g else 3 * G - 1
    if kind == "output":
        return 3 * g + 2 * qh if g < G - 1 or not qh else 3 * G - 2
    return 3 * G + g


def attention(nc, ins, hold):
    x, scratch, x2_dram = ins["x"], hold["qk_scratch"], hold["x2"]
    mean_rstd1, mean_var2, ca1_sa = hold["mean_rstd1"], hold["mean_rstd2"], hold["ca1_sa"]
    with ExitStack() as ctx:
        sb = lambda name, shape, dt=F32: ctx.enter_context(nc.sbuf_tensor(name, shape, dt))
        ps = lambda name, shape: ctx.enter_context(nc.psum_tensor(name, shape, F32))
        sem = lambda name: ctx.enter_context(nc.semaphore(name))
        wqk, wv, wo = sb("wqk", [P, KC, 2 * D]), sb("wv", [P, KC, D]), sb("wo", [P, KC, D])
        bqk, bv, bo = sb("bqk", [P, SLOTS]), sb("bv", [P, D]), sb("bo", [P, D])
        cos, sin = sb("cos", [P, T]), sb("sin", [P, T])
        ident, tri = sb("ident", [P, P]), sb("tri", [P, HALF])
        ident16, after16 = sb("ident16", [P, P], BF16), sb("after16", [P, P], BF16)
        xb, xn = sb("xb", [P, NT, D]), sb("xn", [P, NT, D])
        xg = xn
        ga, gabo = sb("ga", [P, D]), sb("gabo", [P, D])
        stat = sb("stat", [P, NT, 2])
        stat6, stat2 = sb("stat6", [P, NT, 6]), sb("stat2", [P, NT, 2])
        ht = sb("ht", [P, KC, T])
        qk = sb("qk", [P, SLOTS, T])
        sw = sb("sw", [P, 2, T])
        part = sb("part", [P, SLOTS, 3, T], BF16)
        v_next = xb
        vp = sb("vp", [P, NT, H1, DH + 1])
        qs = [sb(f"qs{n}", [P, J, T], BF16) for n in range(G)]
        ks = [sb(f"ks{n}", [P, J, T], BF16) for n in range(G)]
        pt = sb("pt", [P, PT_BUFS, J, HALF])
        mp = sb("mp", [P, J * NT, 2])
        negm = sb("negm", [P, J * NT])
        mres = sb("mres", [J * NT, P])
        mpart = sb("mpart", [J * NT, MROWS, P], BF16)
        junk = sb("junk", [P, 2, HALF], BF16)
        o_sb = sb("o_sb", [P, HALF])
        after = o_sb[:, 0:P]
        rec = sb("rec", [P, 4, J])
        ot = sb("ot", [P, NT, D])
        y_sb = [sw[:, n, 0:2 * D].rearrange("p (t d) -> p t d", t=2) for n in range(2)]
        bank_ps = ps("bank_ps", [P, 2, HALF])
        st_ps = ps("st_ps", [P, 2, 2, HALF])
        o_ps = ps("o_ps", [P, HALF])
        misc_ps = ps("misc_ps", [P, HALF])

        w_in, c_in, x_in, ga_in, xg_in = sem("w_in"), sem("c_in"), sem("x_in"), sem("ga_in"), sem("xg_in")
        xg_ready, ln_done = sem("xg_ready"), sem("ln_done")
        bank_for_act, bank_for_dve = sem("bank_for_act"), sem("bank_for_dve")
        bank_read = [sem("bank_read0"), sem("bank_read1")]
        swapped, t1_ready, t2_ready, roped = sem("swapped"), sem("t1_ready"), sem("t2_ready"), sem("roped")
        p1_ready, r1_ready, p2_ready, p3_ready = sem("p1_ready"), sem("r1_ready"), sem("p2_ready"), sem("p3_ready")
        parts_out, part_free, scratch_free, group_done = sem("parts_out"), sem("part_free"), sem("scratch_free"), sem("group_done")
        v_done, vp_free, v_moved, vp_ready, xb_free = sem("v_done"), sem("vp_free"), sem("v_moved"), sem("vp_ready"), sem("xb_free")
        x2_done = sem("x2_done")
        unit_in = [sem(f"unit_in{n}") for n in range(G)]
        m_ready, m_split, m_in = sem("m_ready"), sem("m_split"), sem("m_in")
        misc_full, misc_read = sem("misc_full"), sem("misc_read")
        st_full, exp_done, pv_done = sem("st_full"), sem("exp_done"), sem("pv_done")
        o_out, x2_ready, x2_out, link, init = sem("o_out"), sem("x2_ready"), sem("x2_out"), sem("link"), sem("init")
        y_ready, bn_done, stats_done, xn_free, o_zero = sem("y_ready"), sem("bn_done"), sem("stats_done"), sem("xn_free"), sem("o_zero")
        block = ctx.enter_context(nc.Block())

        FREE = 1
        SENT = 16
        UNIT = 16 * 2 * len(Q_PART)
        LOOP_TURNS, LAST_TURNS = bank_turns(False), bank_turns(True)

        class Round:

            def __init__(self, b, first=False, last=False):
                self.b, self.ahead, self.last, self.first = b, 0 if first else 1, last, first
                self.turns = FIRST_TURNS if first else LAST_TURNS if last else LOOP_TURNS

            def batch(self, per_batch, n):
                return per_batch * self.b + n

            def following(self, per_batch, n):
                return per_batch * self.b + (per_batch * self.ahead + n)

            def bank_count(self, turn):
                if self.first:
                    return turn // 2
                return len(LOOP_TURNS) // 2 * self.b + (len(FIRST_TURNS) // 2 + turn // 2)

            def product_turn(self, n):
                return misc_turn("product", n) - (1 if self.last else 0)

            def misc_count(self, turn):
                return 0 if self.first else MISC_TURNS * self.b + (1 + turn)

        def bank_empty(eng, r, use):
            turn = r.turns[use]
            eng.wait_ge(bank_read[turn % 2], r.bank_count(turn) + FREE)

        def bank_moved(eng, r, use):
            turn = r.turns[use]
            eng.wait_ge(bank_read[turn % 2], r.bank_count(turn) + (1 + FREE))

        @block.sync
        def _(sp):
            c = Counts(sp)
            for s in (*bank_read, misc_read, o_out, x2_ready, m_ready, ln_done, xg_ready, vp_ready, stats_done, part_free,
                      group_done, scratch_free):
                sp.sem_inc(s, FREE)
            for s in (exp_done, roped):
                sp.sem_inc(s, 2 * FREE)
            sp.sem_inc(pv_done, PT_BUFS * FREE)
            for s in (*unit_in, x2_out):
                sp.sem_inc(s, SENT)
            xv = x.rearrange("(b t p) d -> p b t d", b=B, p=P)
            x_next = x[T:, :].rearrange("(b t p) d -> p b t d", b=B - 1, p=P)
            x2v = x2_dram.rearrange("(b t p) d -> p b t d", b=B, p=P)
            sp.dma_start(xb[:], xv[:, 0, :, :]).then_inc(x_in, 16)
            for dst, src in ((wqk, "wqk"), (wv, "wv"), (wo, "wo")):
                sp.dma_start(dst[:], ins[src].rearrange("(c p) n -> p c n", p=P)).then_inc(w_in, 16)
            sp.dma_start(bqk[:], ins["bqk"]).then_inc(w_in, 16)
            for dst, src in ((bv, "bv"), (bo, "bo")):
                sp.dma_start(dst[:], ins[src].partition_broadcast(P)).then_inc(w_in, 16)
            for dst, src in ((cos[:], "cos"), (sin[:], "sin"), (ident[:], "ident"), (tri[:], "tri"), (after, "after")):
                sp.dma_start(dst, ins[src]).then_inc(c_in, 16)

            def parts_to_scratch(r):
                for s in range(SLOTS):
                    w, m = divmod(s, 2)
                    c.wait(p3_ready)
                    if s == 0:
                        c.wait(scratch_free)
                    sp.dma_start(scratch[w, :, m * P:(m + 1) * P, :].rearrange("s p t -> p s t"),
                                 part[:, s, :, :]).then_inc(parts_out, 16)
                c.wait(parts_out, 16 * SLOTS)
                sp.sem_inc(part_free, 1)

            def operands(g):
                for p in range(len(Q_PART)):
                    for w, dst, which in ((0, qs[g], Q_PART[p]), (1, ks[g], K_PART[p])):
                        src = scratch[w, which, J * DH * g:J * DH * (g + 1), :].rearrange("(j d) t -> d j t", d=DH)
                        sp.dma_start(dst[DH * p:DH * (p + 1), :, :], src).then_inc(unit_in[g], 16)

            def minus_max_rows(g):
                c.wait(m_split)
                for n in range(MROWS):
                    row = qs[g][SROWS + n:SROWS + n + 1, :, :].rearrange("o j (q c) -> o (j q) c", c=P)
                    sp.dma_start(row, mpart[:, n, :]).then_inc(m_in, 16)

            def one_round(r):
                b = r.b
                if not r.last:
                    c.wait(xb_free)
                    sp.dma_start(xb[:], x_next[:, bass.ds(b, 1), :, :].rearrange("p o t d -> p (o t) d")).then_inc(x_in, 16)
                c.wait(group_done)
                operands(G - 1)
                sp.dma_start(ga[:], hold["mod_rows"][0, bass.ds(b, 1), :].partition_broadcast(P)
                             .rearrange("p o d -> p (o d)")).then_inc(ga_in, 16)
                c.wait(stats_done)
                if r.last:
                    sp.wait_ge(x2_out, r.batch(16, SENT))
                else:
                    c.wait(xn_free)
                sp.dma_start(xg[:], xv[:, bass.ds(b, 1), :, :].rearrange("p o t d -> p (o t) d")).then_inc(xg_in, 16)
                minus_max_rows(1)
                minus_max_rows(2)
                if r.last:
                    minus_max_rows(3)
                else:
                    parts_to_scratch(r)
                    c.wait(group_done)
                    operands(0)
                    minus_max_rows(3)
                    for g in range(1, G - 1):
                        c.wait(group_done)
                        operands(g)
                    minus_max_rows(0)
                c.wait(x2_done)
                sp.dma_start(x2v[:, bass.ds(b, 1), :, :].rearrange("p o t d -> p (o t) d"), xg[:]).then_inc(x2_out, 16)

            parts_to_scratch(Round(0, first=True))
            for g in range(G - 1):
                operands(g)
            minus_max_rows(0)
            with c.rounds(0, B - 1) as b:
                one_round(Round(b))
            one_round(Round(B - 1, last=True))
            sp.wait_ge(x2_out, 16 * B + SENT)

        @block.gpsimd
        def _(pool):
            c = Counts(pool)
            for n in range(G):
                nc.gpsimd.memset(ks[n][SROWS:SROWS + MROWS, :, :], 1.0).then_inc(init, 1)
                pool.wait_ge(init, n + 1)
            nc.gpsimd.memset(vp[:, :, :, DH:DH + 1], 1.0).then_inc(init, 1)
            pool.wait_ge(init, G + 1)
            nc.gpsimd.memset(mp[:], LOWEST).then_inc(init, 1)
            pool.wait_ge(w_in, 16 * 6)
            pool.wait_ge(c_in, 16 * 5)
            nc.gpsimd.tensor_copy(ident16[:], ident[:]).then_inc(init, 1)
            nc.gpsimd.tensor_copy(after16[:], after).then_inc(init, 1)

            def times_sine(r, s):
                bank_moved(pool, r, ("project", TRANSPOSES + s))
                bank_moved(pool, r, ("project", TRANSPOSES + SLOTS + s))
                pool.wait_ge(roped, r.following(SLOTS, s + 1))
                nc.gpsimd.tensor_tensor(sw[:, s % 2, :], qk[:, s, :], sin[:], ALU.mult).then_inc(t2_ready, 1)

            def times_cosine(r, s):
                nc.gpsimd.tensor_tensor(qk[:, s, :], qk[:, s, :], cos[:], ALU.mult).then_inc(t1_ready, 1)

            def add_halves(r, s):
                pool.wait_ge(t1_ready, r.following(SLOTS, s + 1))
                pool.wait_ge(swapped, r.following(SLOTS, s + 1))
                nc.gpsimd.tensor_tensor(qk[:, s, :], qk[:, s, :], sw[:, s % 2, :], ALU.add).then_inc(roped, 1)

            def first_rest(r, s):
                pool.wait_ge(p1_ready, r.following(SLOTS, s + 1))
                nc.gpsimd.tensor_tensor(qk[:, s, :], qk[:, s, :], part[:, s, 0, :], ALU.subtract).then_inc(r1_ready, 1)

            def third_part(r, s):
                pool.wait_ge(p2_ready, r.following(SLOTS, s + 1))
                nc.gpsimd.tensor_tensor(part[:, s, 2, :], qk[:, s, :], part[:, s, 1, :], ALU.subtract)\
                    .then_inc(p3_ready, 1)

            def rotate_and_split(r):
                for s in range(SLOTS):
                    times_sine(r, s)
                    if s:
                        add_halves(r, s - 1)
                    if s == SLOTS - 1:
                        first_rest(r, 0)
                    times_cosine(r, s)
                add_halves(r, SLOTS - 1)
                for s in range(SLOTS):
                    if s:
                        first_rest(r, s)
                        third_part(r, s - 1)
                third_part(r, SLOTS - 1)

            def move_v(r):
                c.wait(v_done, V_USES)
                if not r.first:
                    c.wait(vp_free)
                nc.gpsimd.tensor_copy(vp[:, :, :, 0:DH], v_next[:].rearrange("p t (h d) -> p t h d", d=DH))\
                    .then_inc(v_moved, 1)
                c.wait(v_moved)
                pool.sem_inc(vp_ready, 1)
                pool.sem_inc(xb_free, 1)

            def residual(r):
                pool.wait_ge(xg_ready, r.batch(2, 2 + FREE))
                for i in range(NT // 2):
                    c.wait(y_ready)
                    nc.gpsimd.tensor_tensor(xg[:, 2 * i:2 * i + 2, :], xg[:, 2 * i:2 * i + 2, :], y_sb[i % 2], ALU.add)\
                        .then_inc(x2_ready, 1)

            def one_round(r):
                b = r.b
                pool.wait_ge(ga_in, 16 * b + 16)
                nc.gpsimd.tensor_tensor(gabo[:], ga[:], bo[:], ALU.mult).then_inc(xg_ready, 1)
                pool.wait_ge(xg_ready, 2 * b + (1 + FREE))
                pool.wait_ge(xg_in, 16 * b + 16)
                nc.gpsimd.tensor_tensor(xg[:], xg[:], gabo[:].unsqueeze(1).to_broadcast([P, NT, D]), ALU.add)\
                    .then_inc(xg_ready, 1)
                if not r.last:
                    rotate_and_split(r)
                    move_v(r)
                residual(r)

            r = Round(0, first=True)
            rotate_and_split(r)
            move_v(r)
            with c.rounds(0, B - 1) as b:
                one_round(Round(b))
            one_round(Round(B - 1, last=True))

        @block.tensor
        def _(pe):
            pe.wait_ge(c_in, 16 * 5)
            pe.wait_ge(w_in, 16 * 6)
            pe.wait_ge(init, G + 4)
            pe.wait_ge(o_zero, 1)

            def project(r, n):
                bank_empty(pe, r, ("project", n))
                bank = bank_ps[:, r.turns["project", n] % 2, :]
                if n < TRANSPOSES:
                    half, k = divmod(n, KC)
                    pe.wait_ge(ln_done, r.following(NT, 4 * (half + 1) + FREE))
                    for i in range(4):
                        last = nc.tensor.transpose(bank[:, i * P:(i + 1) * P],
                                                   xn[:, 4 * half + i, k * P:(k + 1) * P], ident[:])
                    last.then_inc(bank_for_act, 1)
                elif n < TRANSPOSES + QK_USES:
                    half, s = divmod(n - TRANSPOSES, SLOTS)
                    if s == 0:
                        bank_moved(pe, r, ("project", 2 * half))
                        bank_moved(pe, r, ("project", 2 * half + 1))
                    for k in range(KC):
                        last = nc.tensor.matmul(bank, wqk[:, k, s * P:(s + 1) * P], ht[:, k, half * HALF:(half + 1) * HALF],
                                                start=(k == 0), stop=(k == KC - 1))
                    last.then_inc(bank_for_act, 1)
                else:
                    i = n - TRANSPOSES - QK_USES
                    for t in (2 * i, 2 * i + 1):
                        for k in range(KC):
                            last = nc.tensor.matmul(bank[:, (t % 2) * D:(t % 2 + 1) * D],
                                                    ht[:, k, t * P:(t + 1) * P], wv[:, k, :],
                                                    start=(k == 0), stop=(k == KC - 1))
                    last.then_inc(bank_for_dve, 1)

            def score_chunk(r, chunk):
                g, ch = chunk[0] % G, chunk[1]
                qt, k0, keys, _ = CHUNK[ch % len(CHUNK)]
                j = ch // len(CHUNK)
                if ch == 0:
                    pe.wait_ge(unit_in[g], r.batch(UNIT, UNIT + SENT) if chunk[0] < G else r.following(UNIT, UNIT + SENT))
                    if g == G - 1:
                        pe.sem_inc(scratch_free, 1)
                bank_empty(pe, r, chunk)
                nc.tensor.matmul(bank_ps[:, r.turns[chunk] % 2, 0:keys], qs[g][0:SROWS, j, qt * P:(qt + 1) * P],
                                 ks[g][0:SROWS, j, k0:k0 + keys], start=True, stop=True).then_inc(bank_for_dve, 1)

            def misc_empty(r, turn):
                pe.wait_ge(misc_read, r.misc_count(turn) + FREE)

            def transpose_maxima(r, g):
                misc_empty(r, misc_turn("maxima", g))
                pe.wait_ge(m_ready, r.batch(G, g + 1 + FREE) if g else r.following(G, 1 + FREE))
                nc.tensor.transpose(misc_ps[0:J * NT, 0:P], negm[:], ident[:]).then_inc(misc_full, 1)

            def scores_for_exp(b, g, s, h):
                qh, kb, off, diagonal = STEP[s]
                if s == 0 and h == 0:
                    pe.wait_ge(m_in, 16 * MROWS * G * b + 16 * MROWS * (g + 1))
                pe.wait_ge(exp_done, 2 * STEPS * G * b + (2 * STEPS * g + 2 * s + h - 1 + 2 * FREE))
                for i in range(2):
                    j = 2 * h + i
                    if diagonal:
                        nc.tensor.matmul(st_ps[:, h, i, off:off + P], ident16[:], after16[:],
                                         start=True, stop=False, skip_group_check=True)
                    last = nc.tensor.matmul(st_ps[:, h, i, off:HALF],
                                            ks[g][0:SROWS + MROWS, j, kb * P:(kb + 1) * P],
                                            qs[g][0:SROWS + MROWS, j, qh * HALF + off:(qh + 1) * HALF],
                                            start=not diagonal, stop=True, skip_group_check=diagonal)
                last.then_inc(st_full, 1)

            def weigh_values(b, g, s, h):
                qh, kb, off, _ = STEP[s]
                pe.wait_ge(exp_done, 2 * STEPS * G * b + (2 * STEPS * g + 2 * s + h + 1 + 2 * FREE))
                if kb == 0 and h == 0:
                    pe.wait_ge(o_out, 2 * G * b + (2 * g + qh + FREE))
                if g == 0 and s == 0 and h == 0:
                    pe.wait_ge(vp_ready, b + (1 + FREE))
                for j in (2 * h, 2 * h + 1):
                    last = nc.tensor.matmul(o_ps[32 * j:32 * j + DH + 1, off:HALF], vp[:, kb, J * g + j, :],
                                            pt[:, s % PT_BUFS, j, off:HALF],
                                            start=(kb == 0), stop=(kb == 4 * qh + 3))
                if h:
                    last.then_inc(pv_done, 1)

            def transpose_output(r, g, qh):
                misc_empty(r, misc_turn("output", g, qh))
                pe.wait_ge(o_out, r.batch(2 * G, 2 * g + qh + 1 + FREE))
                for i in range(4):
                    last = nc.tensor.transpose(misc_ps[:, i * P:(i + 1) * P], o_sb[:, i * P:(i + 1) * P], ident[:])
                last.then_inc(misc_full, 1)

            def output_product(r, n):
                misc_empty(r, r.product_turn(n))
                if n < TRANSPOSES:
                    half, k = divmod(n, KC)
                    for i in range(4):
                        last = nc.tensor.transpose(misc_ps[:, i * P:(i + 1) * P],
                                                   ot[:, 4 * half + i, k * P:(k + 1) * P], ident[:])
                else:
                    i = n - TRANSPOSES
                    for t in (2 * i, 2 * i + 1):
                        for k in range(KC):
                            last = nc.tensor.matmul(misc_ps[:, (t % 2) * D:(t % 2 + 1) * D],
                                                    ht[:, k, t * P:(t + 1) * P], wo[:, k, :],
                                                    start=(k == 0), stop=(k == KC - 1))
                last.then_inc(misc_full, 1)

            def one_round(r):
                b = r.b
                for place in PLACES:
                    g, s = place
                    if not r.last:
                        for n in PROJECT_AT.get(place, ()):
                            project(r, n)
                    chunks = iter(chunks_at(place, r.last))

                    def next_chunk():
                        for chunk in chunks:
                            score_chunk(r, chunk)
                            break

                    next_chunk()
                    if g < G:
                        for h in range(2):
                            scores_for_exp(b, g, s, h)
                            next_chunk()
                        for h in range(2):
                            if s:
                                weigh_values(b, g, s - 1, h)
                            next_chunk()
                        if s == 1 and g:
                            transpose_output(r, g - 1, 1)
                        if s == 6:
                            transpose_output(r, g, 0)
                        if s == EARLY_STEP and g < G - 1:
                            transpose_maxima(r, g + 1)
                        if s == STEPS - 1:
                            for h in range(2):
                                weigh_values(b, g, s, h)
                    elif s == 0:
                        transpose_output(r, G - 1, 1)
                        if not r.last:
                            transpose_maxima(r, 0)
                    else:
                        output_product(r, s - 1)
                    next_chunk()

            r = Round(0, first=True)
            for n in range(PROJECT):
                project(r, n)
            for ch in range(CHUNKS):
                score_chunk(r, (G, ch))
            transpose_maxima(r, 0)
            for ch in range(EARLY):
                score_chunk(r, (G + 1, ch))
            with pe.Fori(0, B - 1) as b:
                one_round(Round(b))
            one_round(Round(B - 1, last=True))

        @block.scalar
        def _(act):
            c = Counts(act)
            act.wait_ge(w_in, 16 * 6)
            act.wait_ge(c_in, 16 * 5)

            def projected(r, n):
                turn = r.turns["project", n]
                bank, read = bank_ps[:, turn % 2, :], bank_read[turn % 2]
                if n < TRANSPOSES:
                    half, k = divmod(n, KC)
                    c.wait(bank_for_act)
                    nc.scalar.activation(ht[:, k, half * HALF:(half + 1) * HALF], bank, ACT.Identity,
                                         bias=ca1_sa[:, 1, k, bass.ds(r.b + r.ahead, 1)],
                                         scale=ca1_sa[:, 0, k, bass.ds(r.b + r.ahead, 1)]).then_inc(read, 1)
                else:
                    half, s = divmod(n - TRANSPOSES, SLOTS)
                    if n == TRANSPOSES:
                        c.wait(part_free)
                    c.wait(bank_for_act)
                    nc.scalar.activation(qk[:, s, half * HALF:(half + 1) * HALF], bank, ACT.Identity,
                                         bias=bqk[:, s:s + 1]).then_inc(read, 1)

            def first_part(r, s):
                act.wait_ge(roped, r.following(SLOTS, s + 1 + 2 * FREE))
                nc.scalar.activation(part[:, s, 0, :], qk[:, s, :], ACT.Copy).then_inc(p1_ready, 1)

            def second_part(r, s):
                act.wait_ge(r1_ready, r.following(SLOTS, s + 1))
                nc.scalar.activation(part[:, s, 1, :], qk[:, s, :], ACT.Copy).then_inc(p2_ready, 1)

            def output_out(r, g, qh):
                act.wait_ge(pv_done, r.batch(STEPS * G, STEPS * g + 4 + 8 * qh + PT_BUFS * FREE))
                if qh:
                    act.wait_ge(misc_full, r.misc_count(misc_turn("output", g, 0) + 1))
                elif g:
                    act.wait_ge(misc_full, r.misc_count(misc_turn("output", g - 1, 1) + 1))
                else:
                    act.wait_ge(misc_full, r.misc_count(0))
                nc.scalar.activation(o_sb[:], o_ps[:], ACT.Copy).then_inc(o_out, 1)
                if qh:
                    act.sem_inc(group_done, 1)

            def one_round(r):
                b = r.b
                for place in PLACES:
                    g, s = place
                    if not r.last:
                        for n in PROJECT_AT.get(place, ()):
                            if n < TRANSPOSES + QK_USES:
                                projected(r, n)
                            if n == TRANSPOSES - 1:
                                act.sem_inc(xn_free, 1)
                        if at(place, 17) is not None:
                            first_part(r, at(place, 17))
                        if at(place, 20) is not None:
                            second_part(r, at(place, 20))
                    if g < G:
                        off = STEP[s][2]
                        act.wait_ge(pv_done, STEPS * G * b + (STEPS * g + s + FREE))
                        for h in range(2):
                            act.wait_ge(st_full, 2 * STEPS * G * b + (2 * STEPS * g + 2 * s + h + 1))
                            nc.scalar.activation(pt[:, s % PT_BUFS, 2 * h:2 * h + 2, off:HALF], st_ps[:, h, :, off:HALF],
                                                 ACT.Exp, scale=DH ** -0.5).then_inc(exp_done, 1)
                        if s == 0 and g:
                            output_out(r, g - 1, 1)
                        if s == 4:
                            output_out(r, g, 0)
                    elif s == 0:
                        output_out(r, G - 1, 1)
                        act.sem_inc(vp_free, 1)
                    elif s <= TRANSPOSES:
                        half, k = divmod(s - 1, KC)
                        act.wait_ge(misc_full, r.misc_count(r.product_turn(s - 1) + 1))
                        nc.scalar.activation(ht[:, k, half * HALF:(half + 1) * HALF], misc_ps[:], ACT.Copy)\
                            .then_inc(misc_read, 1)

            r = Round(0, first=True)
            for n in range(TRANSPOSES + QK_USES):
                projected(r, n)
            for s in range(SLOTS):
                first_part(r, s)
            for s in range(SLOTS):
                second_part(r, s)
            with c.rounds(0, B - 1) as b:
                one_round(Round(b))
            one_round(Round(B - 1, last=True))

        @block.vector
        def _(dve):
            c = Counts(dve)
            nc.vector.memset(o_ps[:], 0.0).then_inc(o_zero, 1)
            dve.wait_ge(c_in, 16 * 5)
            dve.wait_ge(w_in, 16 * 6)
            dve.wait_ge(init, G + 4)
            swap = [DH * (i // DH) + (i + DH // 2) % DH for i in range(32)]

            def hand_over(*instructions):
                for ins in instructions:
                    ins.then_inc(link, 1)
                c.wait(link, len(instructions))

            def norm(r, half):
                if half == 0:
                    hand_over(nc.vector.tensor_copy(stat[:], mean_rstd1[:, bass.ds(NT * r.b + NT * r.ahead, NT), :]))
                    dve.wait_ge(x_in, r.following(16, 16))
                    dve.wait_ge(x2_out, r.batch(16, SENT))
                for t in range(4 * half, 4 * half + 4):
                    nc.vector.tensor_scalar(xn[:, t, :], xb[:, t, :], stat[:, t, 0:1], stat[:, t, 1:2],
                                            ALU.subtract, ALU.mult).then_inc(ln_done, 1)

            def swap_halves(s):
                c.wait(t2_ready)
                nc.vector.stream_shuffle(sw[:, s % 2, :], sw[:, s % 2, :], swap).then_inc(swapped, 1)

            def v_out(r, i):
                turn = r.turns["project", TRANSPOSES + QK_USES + i]
                if i == 0:
                    dve.wait_ge(vp_ready, r.following(1, FREE))
                c.wait(bank_for_dve)
                hand_over(nc.vector.tensor_tensor(
                    v_next[:, 2 * i:2 * i + 2, :], bank_ps[:, turn % 2, :].rearrange("p (t d) -> p t d", t=2),
                    bv[:].unsqueeze(1).to_broadcast([P, 2, D]), ALU.add))
                dve.sem_inc(v_done, 1)
                dve.sem_inc(bank_read[turn % 2], 1)

            def chunk_maximum(r, chunk):
                turn, ch = r.turns[chunk], chunk[1]
                qt, _, keys, diagonal = CHUNK[ch % len(CHUNK)]
                row = ch // len(CHUNK) * NT + qt
                c.wait(bank_for_dve)
                if diagonal:
                    ins = nc.vector.tensor_tensor_reduce(
                        out=junk[:, turn % 2, 0:keys], in0=bank_ps[:, turn % 2, 0:keys], in1=tri[:, HALF - keys:HALF],
                        scale=1.0, scalar=LOWEST, op0=ALU.add, op1=ALU.max, accum_out=mp[:, row, 0:1])
                else:
                    ins = nc.vector.tensor_reduce(mp[:, row, 1:2], bank_ps[:, turn % 2, 0:keys], AX.X, ALU.max)
                ins.then_inc(bank_read[turn % 2], 1)

            def group_maxima(r, g):
                bank_moved(dve, r, (g, CHUNKS - 2))
                bank_moved(dve, r, (g, CHUNKS - 1))
                hand_over(nc.vector.tensor_reduce(negm[:], mp[:], AX.X, ALU.max, negate=True))
                dve.sem_inc(m_ready, 1)

            def split_maxima(r, g):
                turn = misc_turn("maxima", g)
                dve.wait_ge(misc_full, r.misc_count(turn) + 1)
                if not r.first:
                    dve.wait_ge(m_in, r.batch(16 * MROWS * G, 16 * MROWS * (g if g else G)))
                hand_over(nc.vector.tensor_copy(mpart[:, 0, :], misc_ps[0:J * NT, 0:P]))
                nc.vector.tensor_tensor(mres[:], misc_ps[0:J * NT, 0:P], mpart[:, 0, :], ALU.subtract)\
                    .then_inc(misc_read, 1)
                dve.wait_ge(misc_read, r.misc_count(turn) + (1 + FREE))
                hand_over(nc.vector.tensor_copy(mpart[:, 1, :], mres[:]))
                nc.vector.tensor_tensor(mpart[:, 2, :], mres[:], mpart[:, 1, :], ALU.subtract).then_inc(m_split, 1)

            def divide_output(r, g, qh):
                dve.wait_ge(misc_full, r.misc_count(misc_turn("output", g, qh) + 1))
                o = misc_ps[:].rearrange("p (t j d) -> p t j d", t=4, j=J)
                hand_over(nc.vector.reciprocal(rec[:], o[:, :, :, DH]))
                nc.vector.tensor_tensor(
                    ot[:, 4 * qh:4 * qh + 4, J * DH * g:J * DH * (g + 1)].rearrange("p t (j d) -> p t j d", d=DH),
                    o[:, :, :, 0:DH], rec[:].unsqueeze(3).to_broadcast([P, 4, J, DH]), ALU.mult)\
                    .then_inc(misc_read, 1)

            def statistics(r, i):
                dve.wait_ge(x2_ready, r.batch(NT // 2, i + 1 + FREE))
                for t in (2 * i, 2 * i + 1):
                    nc.vector.bn_stats(stat6[:, t, :], xg[:, t, :]).then_inc(bn_done, 1)

            def gated(r, i):
                turn = r.product_turn(TRANSPOSES + i)
                dve.wait_ge(misc_full, r.misc_count(turn + 1))
                hand_over(nc.vector.tensor_tensor(y_sb[i % 2], misc_ps[:].rearrange("p (t d) -> p t d", t=2),
                                                  ga[:].unsqueeze(1).to_broadcast([P, 2, D]), ALU.mult))
                dve.sem_inc(misc_read, 1)
                dve.sem_inc(y_ready, 1)
                if i:
                    statistics(r, i - 1)

            def one_round(r):
                b = r.b
                for place in PLACES:
                    g, s = place
                    if not r.last:
                        for n in PROJECT_AT.get(place, ()):
                            if n >= TRANSPOSES + QK_USES:
                                v_out(r, n - TRANSPOSES - QK_USES)
                    for chunk in chunks_at(place, r.last):
                        chunk_maximum(r, chunk)
                    if g < G:
                        if s == 2 and g:
                            divide_output(r, g - 1, 1)
                        if s == 7:
                            divide_output(r, g, 0)
                        if g < G - 1:
                            if s == EARLY_STEP - 1:
                                group_maxima(r, g + 1)
                            if s == EARLY_STEP + 1:
                                split_maxima(r, g + 1)
                        elif s == STEPS - 1 and not r.last:
                            group_maxima(r, G)
                    elif s == 0:
                        divide_output(r, G - 1, 1)
                        if not r.last:
                            split_maxima(r, 0)
                    elif s > TRANSPOSES:
                        gated(r, s - 1 - TRANSPOSES)
                    if not r.last:
                        if place in ((0, 4), (0, 5)):
                            norm(r, s - 4)
                        if at(place, 13) is not None:
                            swap_halves(at(place, 13))
                statistics(r, NT // 2 - 1)
                dve.sem_inc(x2_done, 1)
                c.wait(bn_done, NT)
                dve.sem_inc(stats_done, 1)
                hand_over(*[nc.vector.bn_aggr(stat2[:, t, :], stat6[:, t, :]) for t in range(NT)])
                hand_over(nc.vector.tensor_copy(mean_var2[:, bass.ds(NT * b, NT), :], stat2[:]))

            r = Round(0, first=True)
            norm(r, 0)
            norm(r, 1)
            for s in range(2):
                swap_halves(s)
            for i in range(V_USES):
                v_out(r, i)
            for s in range(2, SLOTS):
                swap_halves(s)
            for ch in range(CHUNKS):
                chunk_maximum(r, (G, ch))
            group_maxima(r, G)
            split_maxima(r, 0)
            for ch in range(EARLY):
                chunk_maximum(r, (G + 1, ch))
            with c.rounds(0, B - 1) as b:
                one_round(Round(b))
            one_round(Round(B - 1, last=True))


PAIRS = NT // 2


def batch_attention(nc, ins, hold):
    with ExitStack() as ctx:
        sb = lambda name, shape, dt=F32: ctx.enter_context(nc.sbuf_tensor(name, shape, dt))
        sem = lambda name: ctx.enter_context(nc.semaphore(name))
        ps = lambda name, shape: ctx.enter_context(nc.psum_tensor(name, shape, F32))
        H2 = 4
        D2 = D // H2
        w_in, w_out, bias_in, bias_out = (sb("b_w_in", [P, KC, 3 * D]), sb("b_w_out", [P, KC, D]),
                                          sb("b_bias_in", [P, 3 * D]), sb("b_bias_out", [P, D]))
        cb1, sbb, ident = sb("b_cb1", [P, B, D]), sb("b_sb", [P, B, D]), sb("b_ident", [P, P])
        x2 = [sb(f"b_x2_{n}", [P, B, D]) for n in range(2)]
        h = [sb(f"b_h_{n}", [P, B, D]) for n in range(2)]
        hb = [sb(f"b_hb_{n}", [P, B, D]) for n in range(2)]
        h_t = sb("b_h_t", [P, KC, B * P])
        qkv = [sb(f"b_qkv_{n}", [P, B, 3 * D]) for n in range(2)]
        stat = [sb(f"b_stat_{n}", [P, B, 2]) for n in range(2)]
        prod = [sb(f"b_prod_{n}", [P, B, D]) for n in range(4)]
        score, top, pr, total = sb("b_score", [P, B, B, H2]), sb("b_top", [P, B, H2]), sb("b_pr", [P, B, B, H2]), sb("b_total", [P, B, H2])
        o, o_t = sb("b_o", [P, B, D]), sb("b_o_t", [P, KC, B * P])
        y = sb("b_y", [P, B, D])
        st6, st2 = sb("b_st6", [P, B, 6]), sb("b_st2", [P, B, 2])
        t_ps, qkv_ps, y_ps = ps("b_t_ps", [P, 2, HALF]), ps("b_qkv_ps", [P, 2, 2 * HALF]), ps("b_y_ps", [P, 2, HALF])
        mean_rstd2, mean_rstd3, y_all = hold["mean_rstd2"], hold["mean_rstd3"], hold["y_all"]

        c_in, y_done = sem("b_c_in"), sem("b_y_done")
        x2_in, x2_free = [sem("b_x2_in0"), sem("b_x2_in1")], sem("b_x2_free")
        var_ready, std_ready, h_for_pe, h_for_pool = sem("b_var"), sem("b_std"), sem("b_h_for_pe"), sem("b_h_for_pool")
        h_free, hb_free, hb_made = sem("b_h_free"), sem("b_hb_free"), sem("b_hb_made")
        hb_ready, t_full, t_read = sem("b_hb_ready"), sem("b_t_full"), sem("b_t_read")
        qkv_full, qkv_out, qkv_read = sem("b_qkv_full"), sem("b_qkv_out"), sem("b_qkv_read")
        qkv_for_pool = sem("b_qkv_for_pool")
        qkv_ready, bias_added, prod_free = sem("b_qkv_ready"), sem("b_bias_added"), sem("b_prod_free")
        qk_product, pr_for_pool, v_product = sem("b_qk_product"), sem("b_pr_for_pool"), sem("b_v_product")
        exp_in, exp_out, o_ready, o_full, o_read = sem("b_exp_in"), sem("b_exp_out"), sem("b_o_ready"), sem("b_o_full"), sem("b_o_read")
        y_full, y_read, y_ready, y_copied, link = sem("b_y_full"), sem("b_y_read"), sem("b_y_ready"), sem("b_y_copied"), sem("b_link")
        block = ctx.enter_context(nc.Block())
        x2v = hold["x2"].rearrange("(b i n p) d -> n p i b d", b=B, n=2, p=P)

        def schedule(c, one_round):
            one_round(0, None, None, 1)
            one_round(1, 0, None, 0)
            with c.rounds(0, PAIRS - 1) as i:
                for this in (1, 2):
                    one_round(2 * i + (this + 1), 2 * i + this, 2 * i + (this - 1), this % 2)
            one_round(None, NT - 1, NT - 2, 1)
            one_round(None, None, NT - 1, 0)

        @block.sync
        def _(sp):
            c = Counts(sp)
            sp.sem_inc(x2_free, 2)
            for dst, src in ((w_in, "w_in"), (w_out, "w_out")):
                sp.dma_start(dst[:], ins[src].rearrange("(c p) n -> p c n", p=P)).then_inc(c_in, 16)
            for dst, src in ((bias_in, "b_in"), (bias_out, "b_out")):
                sp.dma_start(dst[:], ins[src].partition_broadcast(P)).then_inc(c_in, 16)
            sp.dma_start(ident[:], ins["ident"]).then_inc(c_in, 16)
            for dst, n in ((cb1, 2), (sbb, 3)):
                sp.dma_start(dst[:], hold["mod_rows"][n].partition_broadcast(P)).then_inc(c_in, 16)
            with c.rounds(0, PAIRS) as i:
                for n in range(2):
                    c.wait(x2_free)
                    for b in range(B):
                        sp.dma_start(x2[n][:, b, :], x2v[n][:, bass.ds(i, 1), b, :].rearrange("p o d -> p (o d)"))                          .then_inc(x2_in[n], 16)

        @block.tensor
        def _(pe):
            c = Counts(pe)
            pe.wait_ge(c_in, 16 * 7)

            def project(n):
                c.wait(h_for_pe)
                for k in range(KC):
                    for b in range(B):
                        last = nc.tensor.transpose(t_ps[:, k, b * P:(b + 1) * P], h[n][:, b, k * P:(k + 1) * P], ident[:])
                    last.then_inc(t_full, 1)
                c.wait(t_read, 2)
                for b in range(B):
                    c.wait(qkv_read)
                    for lo, hi in ((0, HALF), (HALF, 3 * D)):
                        for k in range(KC):
                            last = nc.tensor.matmul(qkv_ps[:, b % 2, lo:hi], h_t[:, k, b * P:(b + 1) * P],
                                                    w_in[:, k, lo:hi], start=(k == 0), stop=(k == KC - 1))
                    last.then_inc(qkv_full, 1)

            def output():
                c.wait(y_read, 2)
                c.wait(o_ready)
                for k in range(KC):
                    for b in range(B):
                        last = nc.tensor.transpose(y_ps[:, k, b * P:(b + 1) * P], o[:, b, k * P:(k + 1) * P], ident[:])
                    last.then_inc(o_full, 1)
                c.wait(o_read, 2)
                for u in range(2):
                    for b in (2 * u, 2 * u + 1):
                        for k in range(KC):
                            last = nc.tensor.matmul(y_ps[:, u, (b % 2) * D:(b % 2 + 1) * D], o_t[:, k, b * P:(b + 1) * P],
                                                    w_out[:, k, :], start=(k == 0), stop=(k == KC - 1))
                    last.then_inc(y_full, 1)

            def one_round(after, this, before, n):
                if after is not None:
                    project(1 - n)
                if this is not None:
                    output()

            schedule(c, one_round)

        @block.scalar
        def _(act):
            c = Counts(act)
            c.wait(var_ready)
            nc.scalar.activation(mean_rstd2[:, :, 1], mean_rstd2[:, :, 1], ACT.Sqrt).then_inc(std_ready, 1)
            act.sem_inc(qkv_read, 2)

            def one_round(after, this, before, n):
                if after is not None:
                    for k in range(KC):
                        c.wait(t_full)
                        nc.scalar.activation(h_t[:, k, :], t_ps[:, k, :], ACT.Copy).then_inc(t_read, 1)
                if this is not None:
                    c.wait(exp_in)
                    nc.scalar.activation(pr[:], score[:], ACT.Exp, scale=D2 ** -0.5).then_inc(exp_out, 1)
                if before is not None:
                    c.wait(y_ready)
                    nc.scalar.activation(y_all[:].rearrange("p (b t) d -> p b t d", b=B)[:, :, bass.ds(before, 1), :]
                                         .rearrange("p b o d -> p b (o d)"), y[:], ACT.Copy).then_inc(y_copied, 1)
                if after is not None:
                    for b in range(B):
                        c.wait(qkv_full)
                        nc.scalar.activation(qkv[1 - n][:, b, :], qkv_ps[:, b % 2, 0:3 * D], ACT.Copy).then_inc(qkv_out, 1)
                        c.wait(qkv_out)
                        act.sem_inc(qkv_read, 1)
                        act.sem_inc(qkv_for_pool, 1)
                if this is not None:
                    for k in range(KC):
                        c.wait(o_full)
                        nc.scalar.activation(o_t[:, k, :], y_ps[:, k, :], ACT.Copy).then_inc(o_read, 1)

            schedule(c, one_round)

        @block.gpsimd
        def _(pool):
            c = Counts(pool)
            pool.wait_ge(c_in, 16 * 7)

            def one_round(after, this, before, n):
                if this is not None:
                    c.wait(prod_free, 2)
                    for l in (2, 3):
                        nc.gpsimd.tensor_tensor(prod[l][:], qkv[n][:, l:l + 1, 0:D].to_broadcast([P, B, D]),
                                                qkv[n][:, :, D:2 * D], ALU.mult).then_inc(qk_product, 1)
                if after is not None:
                    c.wait(h_for_pool)
                    c.wait(hb_free)
                    nc.gpsimd.tensor_tensor(hb[1 - n][:], h[1 - n][:], bias_out[:].unsqueeze(1).to_broadcast([P, B, D]), ALU.add)\
                        .then_inc(hb_made, 1)
                    c.wait(hb_made)
                    pool.sem_inc(h_free, 1)
                    pool.sem_inc(hb_ready, 1)
                if this is not None:
                    c.wait(pr_for_pool)
                    for l in (2, 3):
                        nc.gpsimd.tensor_tensor(prod[l][:].rearrange("p m (h d) -> p m h d", h=H2),
                                                qkv[n][:, :, 2 * D:3 * D].rearrange("p m (h d) -> p m h d", h=H2),
                                                pr[:, l, :, :].unsqueeze(3).to_broadcast([P, B, H2, D2]), ALU.mult)\
                            .then_inc(v_product, 1)
                if after is not None:
                    for b in range(B):
                        c.wait(qkv_for_pool)
                        nc.gpsimd.tensor_tensor(qkv[1 - n][:, b, :], qkv[1 - n][:, b, :], bias_in[:], ALU.add)\
                            .then_inc(bias_added, 1)
                    c.wait(bias_added, B)
                    pool.sem_inc(qkv_ready, 1)

            schedule(c, one_round)

        @block.vector
        def _(dve):
            c = Counts(dve)

            def hand_over(*instructions):
                for ins in instructions:
                    ins.then_inc(link, 1)
                c.wait(link, len(instructions))

            dve.sem_inc(y_copied, 1)
            hand_over(nc.vector.tensor_scalar(mean_rstd2[:, :, 1], mean_rstd2[:, :, 1], EPS, None, ALU.add))
            dve.sem_inc(var_ready, 1)
            c.wait(std_ready)
            hand_over(nc.vector.reciprocal(mean_rstd2[:, :, 1], mean_rstd2[:, :, 1]))
            dve.wait_ge(c_in, 16 * 7)
            dve.sem_inc(y_read, 2)
            dve.sem_inc(h_free, 2)
            dve.sem_inc(hb_free, 2)
            dve.sem_inc(prod_free, 2)

            def norm(tile, n):
                c.wait(h_free)
                hand_over(nc.vector.tensor_copy(stat[n][:], mean_rstd2[:].rearrange("p (b t) s -> p b t s", b=B)
                                                [:, :, bass.ds(tile, 1), :].rearrange("p b o s -> p b (o s)")))
                c.wait(x2_in[n], 64)
                hand_over(*[nc.vector.scalar_tensor_tensor(h[n][:, b, :], x2[n][:, b, :], stat[n][:, b, 0:1], cb1[:, b, :],
                                                           ALU.subtract, ALU.mult) for b in range(B)])
                dve.sem_inc(x2_free, 1)
                hand_over(*[nc.vector.scalar_tensor_tensor(h[n][:, b, :], h[n][:, b, :], stat[n][:, b, 1:2], sbb[:, b, :],
                                                           ALU.mult, ALU.add) for b in range(B)])
                dve.sem_inc(h_for_pe, 1)
                dve.sem_inc(h_for_pool, 1)

            def attend(n):
                c.wait(qkv_ready)
                hand_over(*[nc.vector.tensor_tensor(prod[l][:], qkv[n][:, l:l + 1, 0:D].to_broadcast([P, B, D]),
                                                    qkv[n][:, :, D:2 * D], ALU.mult) for l in range(2)])
                sums = []
                for l in range(B):
                    if l >= 2:
                        c.wait(qk_product)
                    sums.append(nc.vector.tensor_reduce(score[:, l, :, :].rearrange("p m h -> p (m h)"),
                                                        prod[l][:].rearrange("p m (h d) -> p (m h) d", h=H2),
                                                        AX.X, ALU.add))
                    sums[-1].then_inc(link, 1)
                c.wait(link, B)
                hand_over(nc.vector.tensor_reduce(top[:], score[:].rearrange("p l m h -> p l h m"), AX.X, ALU.max))
                hand_over(nc.vector.tensor_tensor(score[:], score[:], top[:].unsqueeze(2).to_broadcast([P, B, B, H2]),
                                                  ALU.subtract))
                dve.sem_inc(exp_in, 1)

            def weigh(n):
                c.wait(exp_out)
                hand_over(nc.vector.tensor_reduce(total[:], pr[:].rearrange("p l m h -> p l h m"), AX.X, ALU.add))
                hand_over(nc.vector.reciprocal(total[:], total[:]))
                hand_over(nc.vector.tensor_tensor(pr[:], pr[:], total[:].unsqueeze(2).to_broadcast([P, B, B, H2]), ALU.mult))
                dve.sem_inc(pr_for_pool, 1)
                hand_over(*[nc.vector.tensor_tensor(prod[l][:].rearrange("p m (h d) -> p m h d", h=H2),
                                                    qkv[n][:, :, 2 * D:3 * D].rearrange("p m (h d) -> p m h d", h=H2),
                                                    pr[:, l, :, :].unsqueeze(3).to_broadcast([P, B, H2, D2]), ALU.mult)
                            for l in range(2)])
                pairs = lambda l: nc.vector.tensor_tensor(prod[l][:, 0:2, :], prod[l][:, 0:2, :], prod[l][:, 2:4, :], ALU.add)
                hand_over(pairs(0), pairs(1))
                c.wait(v_product, 2)
                hand_over(pairs(2), pairs(3))
                hand_over(*[nc.vector.tensor_tensor(o[:, l, :], prod[l][:, 0, :], prod[l][:, 1, :], ALU.add)
                            for l in range(B)])
                dve.sem_inc(o_ready, 1)
                dve.sem_inc(prod_free, 2)

            def output(tile, n):
                c.wait(y_copied)
                c.wait(hb_ready)
                for u in range(2):
                    c.wait(y_full)
                    nc.vector.tensor_tensor(y[:, 2 * u:2 * u + 2, :], y_ps[:, u, :].rearrange("p (b d) -> p b d", b=2),
                                            hb[n][:, 2 * u:2 * u + 2, :], ALU.add).then_inc(y_done, 1)
                c.wait(y_done, 2)
                dve.sem_inc(hb_free, 1)
                dve.sem_inc(y_read, 2)
                dve.sem_inc(y_ready, 1)
                hand_over(*[nc.vector.bn_stats(st6[:, b, :], y[:, b, :]) for b in range(B)])
                hand_over(*[nc.vector.bn_aggr(st2[:, b, :], st6[:, b, :]) for b in range(B)])
                hand_over(nc.vector.tensor_copy(mean_rstd3[:].rearrange("p (b t) s -> p b t s", b=B)
                                                [:, :, bass.ds(tile, 1), :].rearrange("p b o s -> p b (o s)"), st2[:]))

            def one_round(after, this, before, n):
                if after is not None:
                    norm(after, 1 - n)
                if this is not None:
                    attend(n)
                if before is not None:
                    output(before, 1 - n)
                if this is not None:
                    weigh(n)

            schedule(c, one_round)


def experts(nc, ins, hold):
    with ExitStack() as ctx:
        sb = lambda name, shape, dt=F32: ctx.enter_context(nc.sbuf_tensor(name, shape, dt))
        sem = lambda name: ctx.enter_context(nc.semaphore(name))
        ps = lambda name, shape: ctx.enter_context(nc.psum_tensor(name, shape, F32))
        R = 4
        NR = TILES // R
        mean_rstd3, y_all = hold["mean_rstd3"], hold["y_all"]
        slots_in, slots_out = hold["slots_in"], hold["slots_out"]
        g1, b1, g2, b2 = (sb(f"e_{n}", [P, D]) for n in ("g1", "b1", "g2", "b2"))
        gb, gain, shift = sb("e_gb", [P, B, D]), sb("e_gain", [P, B, D]), sb("e_shift", [P, B, D])
        ident, wg = sb("e_ident", [P, P]), sb("e_wg", [P, KC, E])
        w12, b12 = sb("e_w12", [P, E, KC, D]), sb("e_b12", [P, E, D])
        order, upto, ones = sb("e_order", [P, E]), sb("e_upto", [P, P], BF16), sb("e_ones", [P, P], BF16)
        upto32 = sb("e_upto32", [P, P])
        stat = [sb(f"e_stat_{n}", [P, R, 2]) for n in range(2)]
        y1 = [sb(f"e_y1_{n}", [P, R, D]) for n in range(2)]
        y1_t = [sb(f"e_y1_t_{n}", [P, KC, R * P]) for n in range(2)]
        logits, expo = sb("e_logits", [P, TILES, E]), sb("e_expo", [P, TILES, E])
        top, gate, first, kept = sb("e_top", [P, TILES]), sb("e_gate", [P, TILES]), sb("e_first", [P, TILES]), sb("e_kept", [P, TILES])
        hot, hot16 = sb("e_hot", [P, TILES, E]), sb("e_hot16", [P, TILES, E], BF16)
        sums = [sb(f"e_sums_{n}", [P, TILES, E]) for n in range(2)]
        place, slot, to, frm = sb("e_place", [P, TILES]), sb("e_slot", [P, TILES]), sb("e_to", [P, TILES]), sb("e_from", [P, TILES])
        to_i, frm_i = sb("e_to_i", [P, TILES], I32), sb("e_from_i", [P, TILES], I32)
        rows = [sb(f"e_rows_{n}", [P, R, D]) for n in range(2)]
        rows_t = [sb(f"e_rows_t_{n}", [P, KC, R * P]) for n in range(2)]
        res = [sb(f"e_res_{n}", [P, R, D]) for n in range(2)]
        got = sb("e_got", [P, TILES, D])
        st6, mr4 = sb("e_st6", [P, R, 6]), [sb(f"e_mr4_{n}", [P, R, 2]) for n in range(2)]
        minus = [sb(f"e_minus_{n}", [P, R]) for n in range(2)]
        x2 = sb("e_x2", [P, TILES, D])
        z, zn = [sb(f"e_z_{n}", [P, R, D]) for n in range(2)], [sb(f"e_zn_{n}", [P, R, D]) for n in range(2)]
        t_ps = [ps(f"e_t_ps{n}", [P, KC, HALF]) for n in range(2)]
        p_ps = [ps(f"e_p_ps{n}", [P, HALF]) for n in range(2)]
        q_ps = [ps(f"e_q_ps{n}", [P, HALF]) for n in range(2)]

        names = ("c_in", "link", "var_ready", "std_ready", "y1_for_pe", "y1_for_act", "y1_free", "t_full", "t_read",
                 "logit_full", "logit_read", "logits_ready", "exp_in", "exp_out", "hot_ready", "count_ready", "to_ready",
                 "from_ready", "scattered", "rows_free", "rows_t_ready", "res_full", "res_read", "res_ready",
                 "all_out", "x2_in", "xb_ready", "z_ready", "z_normal", "zn_free", "scaled", "fin_ready", "fin_for_sp", "got_used",
                 "init", "y_kept", "all_y", "w_in", "rstd_ready")
        S = {n: sem("e_" + n) for n in names}
        rows_in, res_out = [sem("e_rows_in0"), sem("e_rows_in1")], [sem("e_res_out0"), sem("e_res_out1")]
        fin_out = sem("e_fin_out")
        gathered = [sem("e_gathered0"), sem("e_gathered1")]
        block = ctx.enter_context(nc.Block())
        CONSTS, WEIGHTS = 16 * 9, 16 * 3
        slots_v = slots_in.rearrange("(i n t p) d -> n p i t d", n=2, t=R, p=P)
        res_v = slots_out.rearrange("(i n t p) d -> n p i t d", n=2, t=R, p=P)
        out_v = hold["out"].rearrange("(t p) d -> p t d", p=P)

        @block.sync
        def _(sp):
            c = Counts(sp)
            for dst, src in ((g1, "g1"), (b1, "ln1_b"), (g2, "g2"), (b2, "ln2_b"), (order, "order")):
                sp.dma_start(dst[:], ins[src].partition_broadcast(P)).then_inc(S["c_in"], 16)
            sp.dma_start(ident[:], ins["ident"]).then_inc(S["c_in"], 16)
            sp.dma_start(upto32[:], ins["upto"]).then_inc(S["c_in"], 16)
            sp.dma_start(wg[:], ins["wg"].rearrange("(c p) e -> p c e", p=P)).then_inc(S["c_in"], 16)
            sp.dma_start(gb[:], hold["mod_rows"][1].partition_broadcast(P)).then_inc(S["c_in"], 16)
            for h in range(2):
                e = E // 2
                sp.dma_start(w12[:, h * e:(h + 1) * e, :, :], hold["w12"].rearrange("(e c p) n -> p e c n", c=KC, p=P)
                             [:, h * e:(h + 1) * e, :, :]).then_inc(S["w_in"], 16)
            sp.dma_start(b12[:], hold["b12"].partition_broadcast(P)).then_inc(S["w_in"], 16)
            sp.dma_start(x2[:], hold["x2"].rearrange("(t p) d -> p t d", p=P)).then_inc(S["x2_in"], 16)
            sp.sem_inc(S["rows_free"], 2)
            sp.wait_ge(S["scattered"], 16 * TILES)
            with c.rounds(0, E // 2) as i:
                for n in range(2):
                    c.wait(S["rows_free"])
                    sp.dma_start(rows[n][:], slots_v[n][:, bass.ds(i, 1), :, :].rearrange("p o t d -> p (o t) d"))\
                      .then_inc(rows_in[n], 16)
            for r in range(NR):
                c.wait(S["fin_for_sp"])
                sp.dma_start(out_v[:, R * r:R * (r + 1), :], x2[:, R * r:R * (r + 1), :]).then_inc(fin_out, 16)
            sp.wait_ge(fin_out, 16 * NR)

        @block.tensor
        def _(pe):
            c = Counts(pe)
            pe.wait_ge(S["c_in"], CONSTS)
            with c.rounds(0, NR // 2):
                for n in range(2):
                    c.wait(S["y1_for_pe"])
                    for k in range(KC):
                        for t in range(R):
                            last = nc.tensor.transpose(t_ps[n][:, k, t * P:(t + 1) * P], y1[n][:, t, k * P:(k + 1) * P], ident[:])
                        last.then_inc(S["t_full"], 1)
                    c.wait(S["t_read"], KC)
                    c.wait(S["logit_read"])
                    for t in range(R):
                        for k in range(KC):
                            last = nc.tensor.matmul(p_ps[n][:, t * E:(t + 1) * E], y1_t[n][:, k, t * P:(t + 1) * P], wg[:, k, :],
                                                    start=(k == 0), stop=(k == KC - 1))
                    last.then_inc(S["logit_full"], 1)
            pe.wait_ge(S["init"], 2)
            c.wait(S["hot_ready"])
            flat = hot16[:].rearrange("p t e -> p (t e)")
            nc.tensor.matmul(q_ps[0][:, 0:TILES * E], upto[:], flat, start=True, stop=True)
            nc.tensor.matmul(q_ps[1][:, 0:TILES * E], ones[:], flat, start=True, stop=True).then_inc(S["count_ready"], 1)

            def transpose_rows(n):
                c.wait(rows_in[n], 16)
                for k in range(KC):
                    for t in range(R):
                        last = nc.tensor.transpose(t_ps[n][:, k, t * P:(t + 1) * P], rows[n][:, t, k * P:(k + 1) * P], ident[:])
                    last.then_inc(S["t_full"], 1)

            def multiply(expert, n):
                c.wait(S["t_read"], KC)
                for u in range(2):
                    c.wait(S["res_read"])
                    for t in (2 * u, 2 * u + 1):
                        for k in range(KC):
                            last = nc.tensor.matmul(p_ps[u][:, (t % 2) * D:(t % 2 + 1) * D], rows_t[n][:, k, t * P:(t + 1) * P],
                                                    w12[:, bass.ds(expert, 1), k, :].rearrange("p o n -> p (o n)"),
                                                    start=(k == 0), stop=(k == KC - 1))
                    last.then_inc(S["res_full"], 1)

            pe.wait_ge(S["w_in"], WEIGHTS)
            transpose_rows(0)
            with c.rounds(0, E // 2 - 1) as i:
                for n in range(2):
                    transpose_rows(1 - n)
                    multiply(2 * i + n, n)
            transpose_rows(1)
            multiply(E - 2, 0)
            multiply(E - 1, 1)

        @block.scalar
        def _(act):
            c = Counts(act)
            c.wait(S["var_ready"])
            nc.scalar.activation(mean_rstd3[:, :, 1], mean_rstd3[:, :, 1], ACT.Sqrt).then_inc(S["std_ready"], 1)
            act.sem_inc(S["logit_read"], 2)
            with c.rounds(0, NR // 2) as i:
                for n in range(2):
                    tiles = bass.ds(2 * R * i + R * n, R)
                    for k in range(KC):
                        c.wait(S["t_full"])
                        nc.scalar.activation(y1_t[n][:, k, :], t_ps[n][:, k, :], ACT.Copy).then_inc(S["t_read"], 1)
                    c.wait(S["y1_for_act"])
                    nc.scalar.activation(y_all[:, tiles, :], y1[n][:], ACT.Copy).then_inc(S["y_kept"], 1)
                    c.wait(S["logit_full"])
                    nc.scalar.activation(logits[:, tiles, :].rearrange("p t e -> p (t e)"), p_ps[n][:, 0:R * E], ACT.Copy)\
                        .then_inc(S["logits_ready"], 1)
                    c.wait(S["logits_ready"])
                    act.sem_inc(S["logit_read"], 1)
            act.sem_inc(S["all_y"], 1)
            c.wait(S["exp_in"])
            nc.scalar.activation(expo[:], expo[:], ACT.Exp).then_inc(S["exp_out"], 1)

            def rows_from_ps(n):
                for k in range(KC):
                    c.wait(S["t_full"])
                    nc.scalar.activation(rows_t[n][:, k, :], t_ps[n][:, k, :], ACT.Copy).then_inc(S["t_read"], 1)
                act.sem_inc(S["rows_free"], 1)

            def store(pair, n):
                c.wait(S["res_ready"])
                act.dma_start(res_v[n][:, bass.ds(pair, 1), :, :].rearrange("p o t d -> p (o t) d"), res[n][:])\
                   .then_inc(res_out[n], 16)

            rows_from_ps(0)
            with c.rounds(0, E // 2 - 1) as i:
                for n in range(2):
                    rows_from_ps(1 - n)
                    store(i, n)
            rows_from_ps(1)
            store(E // 2 - 1, 0)
            store(E // 2 - 1, 1)

            def deviation(n):
                c.wait(S["var_ready"])
                nc.scalar.activation(mr4[n][:, :, 1], mr4[n][:, :, 1], ACT.Sqrt).then_inc(S["std_ready"], 1)

            def normalise(n):
                c.wait(S["rstd_ready"])
                c.wait(S["zn_free"])
                for t in range(R):
                    last = nc.scalar.activation(zn[n][:, t, :], z[n][:, t, :], ACT.Identity,
                                                bias=minus[n][:, t:t + 1], scale=mr4[n][:, t, 1:2]).then_inc(S["z_normal"], 1)

            with c.rounds(0, NR // 2):
                for n in range(2):
                    deviation(n)
                    normalise(n)

        @block.gpsimd
        def _(pool):
            c = Counts(pool)
            nc.gpsimd.memset(ones[:], 1.0).then_inc(S["init"], 1)
            pool.wait_ge(S["c_in"], CONSTS)
            pool.wait_ge(S["init"], 1)
            nc.gpsimd.tensor_copy(upto[:], upto32[:]).then_inc(S["init"], 1)
            pool.wait_ge(S["init"], 2)
            nc.gpsimd.tensor_tensor(gain[:], gb[:], g2[:].unsqueeze(1).to_broadcast([P, B, D]), ALU.mult).then_inc(S["init"], 1)
            pool.wait_ge(S["init"], 3)
            nc.gpsimd.tensor_tensor(shift[:], gb[:], b2[:].unsqueeze(1).to_broadcast([P, B, D]), ALU.mult).then_inc(S["init"], 1)
            pool.wait_ge(S["init"], 4)
            pool.wait_ge(S["x2_in"], 16)
            for b in range(B):
                nc.gpsimd.tensor_tensor(x2[:, NT * b:NT * (b + 1), :], x2[:, NT * b:NT * (b + 1), :],
                                        shift[:, b:b + 1, :].to_broadcast([P, NT, D]), ALU.add).then_inc(S["xb_ready"], 1)
            c.wait(S["xb_ready"], B)
            c.wait(S["to_ready"])
            for t in range(TILES):
                nc.gpsimd.indirect_dma_start(
                    out=slots_in, out_offset=bass.IndirectOffsetOnAxis(ap=to_i[:, t:t + 1], axis=0),
                    in_=y_all[:, t, :], in_offset=None, bounds_check=E * CAP - 1, oob_is_err=False)\
                    .then_inc(S["scattered"], 16)
            c.wait(S["from_ready"])
            c.wait(S["all_out"])

            def gather(r):
                for t in range(R * r, R * (r + 1)):
                    nc.gpsimd.indirect_dma_start(
                        out=got[:, t, :], out_offset=None, in_=slots_out,
                        in_offset=bass.IndirectOffsetOnAxis(ap=frm_i[:, t:t + 1], axis=0)).then_inc(gathered[r % 2], 16)

            gather(0)
            gather(1)
            for r in range(NR + 1):
                if r + 2 < NR:
                    c.wait(S["got_used"])
                    gather(r + 2)
                if r:
                    c.wait(S["scaled"])
                    rows = x2[:, R * (r - 1):R * r, :]
                    nc.gpsimd.tensor_tensor(rows, rows, zn[(r - 1) % 2][:], ALU.add)\
                        .then_inc(S["fin_ready"], 1)
                    c.wait(S["fin_ready"])
                    pool.sem_inc(S["zn_free"], 1)
                    pool.sem_inc(S["fin_for_sp"], 1)

        @block.vector
        def _(dve):
            c = Counts(dve)

            def hand_over(*instructions):
                for ins_ in instructions:
                    ins_.then_inc(S["link"], 1)
                c.wait(S["link"], len(instructions))

            hand_over(nc.vector.tensor_scalar(mean_rstd3[:, :, 1], mean_rstd3[:, :, 1], EPS, None, ALU.add))
            dve.sem_inc(S["var_ready"], 1)
            c.wait(S["std_ready"])
            hand_over(nc.vector.reciprocal(mean_rstd3[:, :, 1], mean_rstd3[:, :, 1]))
            dve.wait_ge(S["c_in"], CONSTS)
            dve.sem_inc(S["y_kept"], 2)
            with c.rounds(0, NR // 2) as i:
                for n in range(2):
                    tile = 2 * R * i + R * n
                    c.wait(S["y_kept"])
                    hand_over(nc.vector.tensor_copy(stat[n][:], mean_rstd3[:, bass.ds(tile, R), :]))
                    hand_over(*[nc.vector.scalar_tensor_tensor(
                        y1[n][:, t, :], y_all[:, bass.ds(tile + t, 1), :].rearrange("p o d -> p (o d)"), stat[n][:, t, 0:1], g1[:],
                        ALU.subtract, ALU.mult) for t in range(R)])
                    hand_over(*[nc.vector.scalar_tensor_tensor(y1[n][:, t, :], y1[n][:, t, :], stat[n][:, t, 1:2], b1[:],
                                                               ALU.mult, ALU.add) for t in range(R)])
                    dve.sem_inc(S["y1_for_pe"], 1)
                    dve.sem_inc(S["y1_for_act"], 1)
            c.wait(S["all_y"])
            wide = lambda a: a[:].unsqueeze(2).to_broadcast([P, TILES, E])
            hand_over(nc.vector.tensor_reduce(top[:], logits[:], AX.X, ALU.max))
            hand_over(nc.vector.tensor_tensor(expo[:], logits[:], wide(top), ALU.subtract),
                      nc.vector.tensor_tensor(hot[:], logits[:], wide(top), ALU.is_ge))
            dve.sem_inc(S["exp_in"], 1)
            hand_over(nc.vector.tensor_tensor(hot[:], hot[:], order[:].unsqueeze(1).to_broadcast([P, TILES, E]), ALU.mult))
            hand_over(nc.vector.tensor_reduce(first[:], hot[:], AX.X, ALU.max))
            hand_over(nc.vector.tensor_tensor(hot[:], hot[:], wide(first), ALU.is_equal))
            hand_over(nc.vector.tensor_copy(hot16[:], hot[:]))
            dve.sem_inc(S["hot_ready"], 1)
            c.wait(S["count_ready"])
            a, b = sums
            hand_over(nc.vector.memset(a[:, 0:1, :], 0.0),
                      nc.vector.tensor_copy(a[:, 1:TILES, :].rearrange("p t e -> p (t e)"), q_ps[1][:, 0:(TILES - 1) * E]))
            step = 1
            while step < TILES:
                hand_over(nc.vector.tensor_copy(b[:, 0:step, :], a[:, 0:step, :]),
                          nc.vector.tensor_tensor(b[:, step:, :], a[:, step:, :], a[:, 0:TILES - step, :], ALU.add))
                a, b = b, a
                step *= 2
            hand_over(nc.vector.tensor_tensor(a[:].rearrange("p t e -> p (t e)"), a[:].rearrange("p t e -> p (t e)"),
                                              q_ps[0][:, 0:TILES * E], ALU.add))
            hand_over(nc.vector.tensor_tensor(a[:], a[:], hot[:], ALU.mult))
            hand_over(nc.vector.tensor_reduce(place[:], a[:], AX.X, ALU.add))
            hand_over(nc.vector.tensor_scalar(slot[:], first[:], -float(CAP), float(E * CAP - 1), ALU.mult, ALU.add),
                      nc.vector.tensor_scalar(kept[:], place[:], float(CAP), None, ALU.is_le))
            hand_over(nc.vector.tensor_tensor(slot[:], slot[:], place[:], ALU.add),
                      nc.vector.tensor_scalar(to[:], kept[:], -float(2 * E * CAP), float(2 * E * CAP), ALU.mult, ALU.add))
            hand_over(nc.vector.tensor_tensor(to[:], to[:], slot[:], ALU.add),
                      nc.vector.tensor_scalar(frm[:], slot[:], float(E * CAP - 1), None, ALU.min))
            hand_over(nc.vector.tensor_copy(to_i[:], to[:]), nc.vector.tensor_copy(frm_i[:], frm[:]))
            dve.sem_inc(S["to_ready"], 1)
            dve.sem_inc(S["from_ready"], 1)
            c.wait(S["exp_out"])
            hand_over(nc.vector.tensor_reduce(gate[:], expo[:], AX.X, ALU.add))
            hand_over(nc.vector.reciprocal(gate[:], gate[:]))
            hand_over(nc.vector.tensor_tensor(gate[:], gate[:], kept[:], ALU.mult))
            dve.sem_inc(S["res_read"], 2)
            dve.wait_ge(S["w_in"], WEIGHTS)
            for n in range(2):
                dve.sem_inc(res_out[n], 16)
            with c.rounds(0, E // 2) as i:
                for n in range(2):
                    c.wait(res_out[n], 16)
                    for u in range(2):
                        c.wait(S["res_full"])
                        hand_over(nc.vector.tensor_tensor(
                            res[n][:, 2 * u:2 * u + 2, :], p_ps[u][:].rearrange("p (t d) -> p t d", t=2),
                            b12[:, bass.ds(2 * i + n, 1), :].to_broadcast([P, 2, D]), ALU.add))
                        dve.sem_inc(S["res_read"], 1)
                    dve.sem_inc(S["res_ready"], 1)
            for n in range(2):
                c.wait(res_out[n], 16)
            dve.sem_inc(S["all_out"], 1)
            dve.wait_ge(S["init"], 4)
            dve.sem_inc(S["zn_free"], 2)

            def total(pair, n):
                r = 2 * pair + n
                hand_over(nc.vector.tensor_copy(stat[n][:, :, 0], gate[:, bass.ds(R * r, R)]))
                dve.wait_ge(gathered[n], 16 * R * pair + 16 * R)
                hand_over(*[nc.vector.scalar_tensor_tensor(
                    z[n][:, t, :], got[:, bass.ds(R * r + t, 1), :].rearrange("p o d -> p (o d)"), stat[n][:, t, 0:1],
                    y_all[:, bass.ds(R * r + t, 1), :].rearrange("p o d -> p (o d)"), ALU.mult, ALU.add) for t in range(R)])
                dve.sem_inc(S["got_used"], 1)
                hand_over(*[nc.vector.bn_stats(st6[:, t, :], z[n][:, t, :]) for t in range(R)])
                hand_over(*[nc.vector.bn_aggr(mr4[n][:, t, :], st6[:, t, :]) for t in range(R)])
                hand_over(nc.vector.tensor_scalar(mr4[n][:, :, 1], mr4[n][:, :, 1], EPS, None, ALU.add))
                dve.sem_inc(S["var_ready"], 1)

            def invert(n):
                c.wait(S["std_ready"])
                hand_over(nc.vector.reciprocal(mr4[n][:, :, 1], mr4[n][:, :, 1]))
                hand_over(nc.vector.scalar_tensor_tensor(minus[n][:], mr4[n][:, :, 0], -1.0, mr4[n][:, :, 1], ALU.mult, ALU.mult))
                dve.sem_inc(S["rstd_ready"], 1)

            def scale(b, n):
                c.wait(S["z_normal"], R)
                hand_over(nc.vector.tensor_tensor(zn[n][:], zn[n][:], gain[:, bass.ds(b, 1), :].to_broadcast([P, R, D]), ALU.mult))
                dve.sem_inc(S["scaled"], 1)

            total(0, 0)
            invert(0)
            with c.rounds(0, NR // 2 - 1) as i:
                for n in range(2):
                    total(i + n, 1 - n)
                    scale(i, n)
                    invert(1 - n)
            total(NR // 2 - 1, 1)
            scale(B - 1, 0)
            invert(1)
            scale(B - 1, 1)


def build(nc, ins, outs, stop=None):
    with ExitStack() as ctx:
        sb = lambda name, shape, dt=F32: ctx.enter_context(nc.sbuf_tensor(name, shape, dt))
        dram = lambda name, shape, dt=F32: nc.dram_tensor(name, shape, dt, kind="Internal").ap()
        hold = {
            "mean_rstd1": sb("mean_rstd1", [P, TILES, 2]),
            "mean_rstd2": sb("mean_rstd2", [P, TILES, 2]),
            "ca1_sa": sb("ca1_sa", [P, 2, KC, B]),
            "mod_rows": dram("mod_rows", (4, B, D)),
            "qk_scratch": dram("qk_scratch", (2, 3, D, T), BF16),
            "x2": outs["dbg_x2"] if stop else dram("x2", (B * T, D)),
            "w12": dram("w12", (E * D, D)),
            "b12": dram("b12", (E, D)),
            "slots_in": dram("slots_in", (E * CAP, D)),
            "slots_out": dram("slots_out", (E * CAP, D)),
            "out": outs["out"],
        }
        fold_experts(nc, ins, hold)
        prepare(nc, ins, hold)
        attention(nc, ins, hold)
        hold["mean_rstd3"] = sb("mean_rstd3", [P, TILES, 2])
        hold["y_all"] = sb("y_all", [P, TILES, D])
        batch_attention(nc, ins, hold)
        if not stop:
            experts(nc, ins, hold)
        if stop:
            with ExitStack() as c2:
                done = c2.enter_context(nc.semaphore("dbg_done"))
                block = c2.enter_context(nc.Block())

                @block.sync
                def _(sp):
                    sp.dma_start(outs["dbg_y"].rearrange("(t p) d -> p t d", p=P), hold["y_all"][:]).then_inc(done, 16)
                    sp.dma_start(outs["dbg_w12"], hold["w12"]).then_inc(done, 16)
                    sp.dma_start(outs["dbg_b12"], hold["b12"]).then_inc(done, 16)
                    sp.wait_ge(done, 48)


def layouts(i):
    import numpy as np
    order = np.arange(D).reshape(H1, DH // 2, 2).transpose(0, 2, 1).reshape(D)
    half = DH // 2
    theta = np.float32(1.0) / np.float32(10000.0) ** (np.arange(half, dtype=np.float32) / np.float32(half))
    angle = (np.arange(T, dtype=np.float32)[:, None] * theta[None, :]).astype(np.float32).T
    c, s = np.cos(angle), np.sin(angle)
    t = lambda a: np.ascontiguousarray(np.asarray(a).T)
    wq, wk = t(i["L0_attn_W_q"])[:, order], t(i["L0_attn_W_k"])[:, order]
    bq, bk = np.asarray(i["L0_attn_b_q"])[order], np.asarray(i["L0_attn_b_k"])[order]
    row, col = np.arange(P)[:, None], np.arange(HALF)[None, :]
    return {
        "x": np.asarray(i["L0_attn_x"]).reshape(B * T, D),
        "c_t": t(i["L0_c"]),
        "wmod": np.asarray(i["L0_wmod"]),
        "wqk": np.concatenate([wq, wk], 1),
        "bqk": np.ascontiguousarray(np.concatenate([bq, bk]).reshape(SLOTS, P).T),
        "wv": t(i["L0_attn_W_v"]), "bv": np.asarray(i["L0_attn_b_v"]),
        "wo": t(i["L0_attn_W_o"]), "bo": np.asarray(i["L0_attn_b_o"]),
        "w1_t": np.ascontiguousarray(np.asarray(i["L0_ffn_w1"]).transpose(0, 2, 1)).reshape(E * FF, D),
        "w2": np.asarray(i["L0_ffn_w2"]).reshape(E * FF, D),
        "b1_t": np.ascontiguousarray(np.asarray(i["L0_ffn_b1"]).reshape(E, FC, P).transpose(0, 2, 1)),
        "b2": np.asarray(i["L0_ffn_b2"]),
        "g1": np.asarray(i["L0_ffn_ln1_g"]), "ln1_b": np.asarray(i["L0_ffn_ln1_b"]),
        "g2": np.asarray(i["L0_ffn_ln2_g"]), "ln2_b": np.asarray(i["L0_ffn_ln2_b"]),
        "wg": np.asarray(i["L0_ffn_wg"]),
        "order": np.arange(E, 0, -1).astype(np.float32),
        "upto": np.triu(np.ones((P, P), np.float32)),
        "w_in": t(i["L0_ffn_in_proj_w"]), "b_in": np.asarray(i["L0_ffn_in_proj_b"]),
        "w_out": t(i["L0_ffn_out_proj_w"]), "b_out": np.asarray(i["L0_ffn_out_proj_b"]),
        "cos": np.tile(np.concatenate([c, c]), (P // DH, 1)).astype(np.float32),
        "sin": np.tile(np.concatenate([s, -s]), (P // DH, 1)).astype(np.float32),
        "ident": np.eye(P, dtype=np.float32),
        "tri": np.where(col - (HALF - P) > row, np.float32(-1e30), np.float32(0)).astype(np.float32),
        "after": np.where(row > col[:, :P], np.float32(-1e30), np.float32(0)).astype(np.float32),
    }


def kernel(**inputs):
    import numpy as np
    import concourse.bacc as bacc
    from concourse.bass_utils import run_bass_kernel_spmd as run

    nc = bacc.Bacc("TRN2", target_bir_lowering=False, num_devices=1)
    arrays = {f"in_{name}": np.ascontiguousarray(a) for name, a in layouts(inputs).items()}
    ins = {name[3:]: nc.dram_tensor(name, a.shape, mybir.dt.from_np(a.dtype), kind="ExternalInput").ap()
           for name, a in arrays.items()}
    out = nc.dram_tensor("out_dram", (B * T, D), F32, kind="ExternalOutput").ap()
    build(nc, ins, {"out": out})
    r = run(nc, [arrays], core_ids=[0])
    return r.results[0]["out_dram"].reshape(B, T, D)
```

```python
from contextlib import ExitStack, contextmanager

import concourse.bass as bass
from concourse import mybir

F32 = mybir.dt.float32
BF16 = mybir.dt.bfloat16
I32 = mybir.dt.int32
ALU = mybir.AluOpType
ACT = mybir.ActivationFunctionType
AX = mybir.AxisListType

P = 128
B = 4
T = 1024
D = 256
KC = D // P
NT = T // P
TILES = B * NT
H1 = 16
DH = D // H1
J = 4
G = H1 // J
HALF = 512
E = 8
FF = 1024
FC = FF // P
CAP = B * T // E
EPS = 1e-5
LOWEST = -3.0e38

Q_PART = (0, 0, 0, 1, 1, 2)
K_PART = (0, 1, 2, 0, 1, 0)
SROWS = len(Q_PART) * DH
MROWS = 3


class Counts:

    def __init__(self, eng):
        self.eng, self.seen = eng, {}

    def wait(self, sem, n=1):
        name = sem.name
        self.seen[name] = (sem, self.seen.get(name, (sem, 0))[1] + n)
        self.eng.wait_ge(sem, self.seen[name][1])

    @contextmanager
    def rounds(self, start, end):
        with self.eng.Fori(start, end) as i:
            before = dict(self.seen)
            yield i
            for name, (sem, n) in self.seen.items():
                more = n - before.get(name, (sem, 0))[1]
                if more:
                    self.eng.sem_inc(sem, -more)
            self.seen = {name: (sem, before.get(name, (sem, 0))[1]) for name, (sem, _) in self.seen.items()}


def prepare(nc, ins, hold):
    x, c_t, wmod = ins["x"], ins["c_t"], ins["wmod"]
    with ExitStack() as ctx:
        sb = lambda name, shape, dt=F32: ctx.enter_context(nc.sbuf_tensor(name, shape, dt))
        sem = lambda name: ctx.enter_context(nc.semaphore(name))
        xs = sb("p_x", [P, NT, D])
        wm = sb("p_wmod", [P, KC, 6 * D])
        cs = sb("p_c", [P, KC, B])
        sil = sb("p_silu", [P, KC, B])
        stats = sb("p_stats", [P, NT, 6])
        rows = sb("p_rows", [B, 6, D])
        sign = sb("p_sign", [B, 2, D])
        mag = sb("p_mag", [B, 2, D])
        rows_ps = ctx.enter_context(nc.psum_tensor("p_rows_ps", [B, 3, HALF], F32))
        cols_ps = ctx.enter_context(nc.psum_tensor("p_cols_ps", [P, 2, KC, B], F32))
        x_in = sem("p_x_in")
        VAR, STD = 1, 2
        mod_link = sem("p_mod_link")
        w_in, c_in, out_done = sem("p_w_in"), sem("p_c_in"), sem("p_out")
        bn_done, std_step, stat_link = sem("p_bn"), sem("p_std"), sem("p_link")
        exp_ready, silu_ready, mod_ready, rows_ready = sem("p_exp"), sem("p_silu_r"), sem("p_mod"), sem("p_rows_r")
        mean_rstd, ca1_sa = hold["mean_rstd1"], hold["ca1_sa"]
        block = ctx.enter_context(nc.Block())

        @block.sync
        def _(sp):
            sp.dma_start(cs[:], c_t.rearrange("(c p) b -> p c b", p=P)).then_inc(c_in, 16)
            sp.dma_start(wm[:], wmod.rearrange("(c p) n -> p c n", p=P)).then_inc(w_in, 16)
            sp.dma_start(xs[:], x[0:T, :].rearrange("(t p) d -> p t d", p=P)).then_inc(x_in, 16)
            sp.wait_ge(rows_ready, 2)
            for n, row in enumerate((2, 5, 4, 3)):
                sp.dma_start(hold["mod_rows"][n], rows[:, row, :]).then_inc(out_done, 16)
            sp.wait_ge(out_done, 64)

        @block.tensor
        def _(pe):
            pe.wait_ge(silu_ready, 1)
            pe.wait_ge(w_in, 16)
            for n in range(3):
                for c in range(KC):
                    last = nc.tensor.matmul(rows_ps[:, n, :], sil[:, c, :], wm[:, c, n * HALF:(n + 1) * HALF],
                                            start=(c == 0), stop=(c == KC - 1))
            for n in range(2):
                for m in range(KC):
                    for c in range(KC):
                        last = nc.tensor.matmul(cols_ps[:, n, m, :], wm[:, c, n * D + m * P:n * D + (m + 1) * P],
                                                sil[:, c, :], start=(c == 0), stop=(c == KC - 1))
            last.then_inc(mod_ready, 1)

        @block.scalar
        def _(act):
            act.wait_ge(c_in, 16)
            nc.scalar.activation(sil[:], cs[:], ACT.Exp, scale=-1.0).then_inc(exp_ready, 1)
            act.wait_ge(std_step, VAR)
            nc.scalar.activation(mean_rstd[:, 0:NT, 1], mean_rstd[:, 0:NT, 1], ACT.Sqrt).then_inc(std_step, 1)

        @block.vector
        def _(dve):
            dve.wait_ge(exp_ready, 1)
            nc.vector.tensor_scalar(sil[:], sil[:], 1.0, None, ALU.add).then_inc(mod_link, 1)
            dve.wait_ge(mod_link, 1)
            nc.vector.reciprocal(sil[:], sil[:]).then_inc(mod_link, 1)
            dve.wait_ge(mod_link, 2)
            nc.vector.tensor_tensor(sil[:], sil[:], cs[:], ALU.mult).then_inc(silu_ready, 1)
            dve.wait_ge(x_in, 16)
            for t in range(NT):
                nc.vector.bn_stats(stats[:, t, :], xs[:, t, :]).then_inc(bn_done, 1)
            dve.wait_ge(bn_done, NT)
            for t in range(NT):
                nc.vector.bn_aggr(mean_rstd[:, t, :], stats[:, t, :]).then_inc(stat_link, 1)
            dve.wait_ge(stat_link, NT)
            nc.vector.tensor_scalar(mean_rstd[:, 0:NT, 1], mean_rstd[:, 0:NT, 1], EPS, None, ALU.add).then_inc(std_step, 1)
            dve.wait_ge(mod_ready, 1)
            flat = rows[:].rearrange("b s d -> b (s d)")
            nc.vector.tensor_copy(flat, rows_ps[:].rearrange("b n f -> b (n f)")).then_inc(rows_ready, 1)
            dve.wait_ge(rows_ready, 1)
            gates = rows[:].rearrange("b (n s) d -> b n s d", s=3)[:, :, 2, :]
            nc.vector.tensor_scalar(sign[:], gates, 0.0, 2.0, ALU.is_ge, ALU.mult).then_inc(mod_link, 1)
            nc.vector.scalar_tensor_tensor(mag[:], gates, -1.0, gates, ALU.mult, ALU.max).then_inc(mod_link, 1)
            dve.wait_ge(mod_link, 4)
            nc.vector.tensor_scalar(sign[:], sign[:], 1.0, None, ALU.subtract).then_inc(mod_link, 1)
            nc.vector.tensor_scalar(mag[:], mag[:], 0.25, None, ALU.max).then_inc(mod_link, 1)
            nc.vector.tensor_scalar(rows[:, 4, :], rows[:, 4, :], 1.0, None, ALU.add).then_inc(mod_link, 1)
            dve.wait_ge(mod_link, 7)
            nc.vector.tensor_tensor(gates, sign[:], mag[:], ALU.mult).then_inc(rows_ready, 1)
            nc.vector.tensor_scalar(ca1_sa[:, 0, :, :], cols_ps[:, 1, :, :], 1.0, None, ALU.add).then_inc(mod_link, 1)
            nc.vector.tensor_copy(ca1_sa[:, 1, :, :], cols_ps[:, 0, :, :]).then_inc(mod_link, 1)
            dve.wait_ge(std_step, STD)
            nc.vector.reciprocal(mean_rstd[:, 0:NT, 1], mean_rstd[:, 0:NT, 1]).then_inc(stat_link, 1)


SLOTS = 4
CHUNKS = J * 12
STEPS = 12
PT_BUFS = 3

CHUNK = []
for _qt in range(NT):
    if _qt < 4:
        CHUNK.append((_qt, 0, (_qt + 1) * P, True))
    else:
        CHUNK.append((_qt, 0, HALF, False))
        CHUNK.append((_qt, HALF, (_qt - 3) * P, True))

STEP = []
for _qh in range(2):
    for _kb in range(4 * _qh + 4):
        STEP.append((_qh, _kb, max(0, _kb - 4 * _qh) * P, _kb >= 4 * _qh))

PIECES = 9
PLACES = [(g, s) for g in range(G) for s in range(STEPS)] + [(G, i) for i in range(PIECES)]

TRANSPOSES, QK_USES, V_USES = 2 * KC, 2 * SLOTS, NT // 2
PROJECT = TRANSPOSES + QK_USES + V_USES
PROJECT_AT = {(0, 6): (0, 1), (0, 7): (2, 3)}
for _n in range(TRANSPOSES, PROJECT):
    PROJECT_AT[divmod(8 + _n - TRANSPOSES, STEPS)] = (_n,)


def at(place, first, every=2):
    s, rest = divmod(place[0] * STEPS + place[1] - first, every)
    return s if rest == 0 and 0 <= s < SLOTS and place[0] < G else None


EARLY = 2 * (PIECES - 1)
EARLY_STEP = STEPS - EARLY // 4


def chunks_at(place, last):
    g, s = place
    if g >= G - 1 and last:
        return []
    if g == G:
        return [(G + 1, ch) for ch in range(2 * s - 2, 2 * s)] if s else []
    if g == G - 1:
        return [(G, ch) for ch in range(4 * s, 4 * s + 4)]
    if g == 0 and s < EARLY_STEP:
        rest, steps = CHUNKS - EARLY, EARLY_STEP - 1
        return [(1, ch) for ch in range(EARLY + rest * max(s - 1, 0) // steps, EARLY + rest * s // steps)]
    if s < EARLY_STEP:
        return [(g + 1, ch) for ch in range(EARLY + 4 * s, EARLY + 4 * s + 4)]
    return [(g + 2, ch) for ch in range(4 * (s - EARLY_STEP), 4 * (s - EARLY_STEP) + 4)] if g + 2 < G else []


def bank_turns(last):
    turns = {}
    for place in PLACES:
        for n in () if last else PROJECT_AT.get(place, ()):
            turns["project", n] = len(turns)
        for chunk in chunks_at(place, last):
            turns[chunk] = len(turns)
    return turns


FIRST_TURNS = {("project", n): n for n in range(PROJECT)}
FIRST_TURNS.update({(G, ch): PROJECT + ch for ch in range(CHUNKS)})
FIRST_TURNS.update({(G + 1, ch): PROJECT + CHUNKS + ch for ch in range(EARLY)})
MISC_TURNS = 20


def misc_turn(kind, g=0, qh=0):
    if kind == "maxima":
        return 3 * g - 2 if g else 3 * G - 1
    if kind == "output":
        return 3 * g + 2 * qh if g < G - 1 or not qh else 3 * G - 2
    return 3 * G + g


def attention(nc, ins, hold):
    x, scratch, x2_dram = ins["x"], hold["qk_scratch"], hold["x2"]
    mean_rstd1, mean_var2, ca1_sa = hold["mean_rstd1"], hold["mean_rstd2"], hold["ca1_sa"]
    with ExitStack() as ctx:
        sb = lambda name, shape, dt=F32: ctx.enter_context(nc.sbuf_tensor(name, shape, dt))
        ps = lambda name, shape: ctx.enter_context(nc.psum_tensor(name, shape, F32))
        sem = lambda name: ctx.enter_context(nc.semaphore(name))
        wqk, wv, wo = sb("wqk", [P, KC, 2 * D]), sb("wv", [P, KC, D]), sb("wo", [P, KC, D])
        bqk, bv, bo = sb("bqk", [P, SLOTS]), sb("bv", [P, D]), sb("bo", [P, D])
        cos, sin = sb("cos", [P, T]), sb("sin", [P, T])
        ident, tri = sb("ident", [P, P]), sb("tri", [P, HALF])
        ident16, after16 = sb("ident16", [P, P], BF16), sb("after16", [P, P], BF16)
        xb, xn = sb("xb", [P, NT, D]), sb("xn", [P, NT, D])
        xg = xn
        ga, gabo = sb("ga", [P, D]), sb("gabo", [P, D])
        stat = sb("stat", [P, NT, 2])
        stat6, stat2 = sb("stat6", [P, NT, 6]), sb("stat2", [P, NT, 2])
        ht = sb("ht", [P, KC, T])
        qk = sb("qk", [P, SLOTS, T])
        sw = sb("sw", [P, 2, T])
        part = sb("part", [P, SLOTS, 3, T], BF16)
        x_more = [xn[:], sw[:].rearrange("p n t -> p (n t)").rearrange("p (t d) -> p t d", d=D)]
        v_next = xb
        vp = sb("vp", [P, NT, H1, DH + 1])
        qs = [sb(f"qs{n}", [P, J, T], BF16) for n in range(G)]
        ks = [sb(f"ks{n}", [P, J, T], BF16) for n in range(G)]
        pt = sb("pt", [P, PT_BUFS, J, HALF])
        mp = sb("mp", [P, J * NT, 2])
        negm = sb("negm", [P, J * NT])
        mres = sb("mres", [J * NT, P])
        mpart = sb("mpart", [J * NT, MROWS, P], BF16)
        junk = sb("junk", [P, 2, HALF], BF16)
        o_sb = sb("o_sb", [P, HALF])
        after = o_sb[:, 0:P]
        rec = sb("rec", [P, 4, J])
        b1, b12c, b12 = sb("b1", [P, E * FC]), sb("b12c", [P, E * KC]), sb("b12_sb", [E * KC, P])
        ot = sb("ot", [P, NT, D])
        wide = lambda a: a.rearrange("p j t -> p (j t)").rearrange("p (c d) -> p c d", c=FC)
        w1 = [wide(pt[:, 0, :, :]), wide(pt[:, 2, :, :]), wide(qs[2][:].bitcast(F32)), wide(qs[1][:].bitcast(F32))]
        w2 = [wide(pt[:, 1, :, :]), ot[:], wide(qs[3][:].bitcast(F32)), wide(ks[3][:].bitcast(F32))]
        EXPERT_BUF = (0, 1, 2, 3, 0, 1, 2, 0)
        y_sb = [sw[:, n, 0:2 * D].rearrange("p (t d) -> p t d", t=2) for n in range(2)]
        bank_ps = ps("bank_ps", [P, 2, HALF])
        st_ps = ps("st_ps", [P, 2, 2, HALF])
        o_ps = ps("o_ps", [P, HALF])
        misc_ps = ps("misc_ps", [P, HALF])
        w12_ps = [st_ps[:, n, 0, :].rearrange("p (m d) -> p m d", m=KC) for n in range(2)]

        fold_in, fold_free = [sem(f"fold_in{n}") for n in range(4)], sem("fold_free")
        w12_full, w12_read, w12_out = sem("w12_full"), sem("w12_read"), sem("w12_out")
        more_x_in, stats_read, std_step = [sem("more_x_in0"), sem("more_x_in1")], sem("stats_read"), sem("std_step")
        VAR, STD = 1, 2
        b12_step = sem("b12_step")
        COPIED, TURNED, ADDED = 1, 2, 3
        w_in, c_in, x_in, ga_in, xg_in = sem("w_in"), sem("c_in"), sem("x_in"), sem("ga_in"), sem("xg_in")
        xg_ready, ln_done = sem("xg_ready"), sem("ln_done")
        bank_for_act, bank_for_dve = sem("bank_for_act"), sem("bank_for_dve")
        bank_read = [sem("bank_read0"), sem("bank_read1")]
        swapped, t1_ready, t2_ready, roped = sem("swapped"), sem("t1_ready"), sem("t2_ready"), sem("roped")
        p1_ready, r1_ready, p2_ready, p3_ready = sem("p1_ready"), sem("r1_ready"), sem("p2_ready"), sem("p3_ready")
        parts_out, part_free, scratch_free, group_done = sem("parts_out"), sem("part_free"), sem("scratch_free"), sem("group_done")
        v_done, vp_free, v_moved, vp_ready, xb_free = sem("v_done"), sem("vp_free"), sem("v_moved"), sem("vp_ready"), sem("xb_free")
        x2_done = sem("x2_done")
        unit_in = [sem(f"unit_in{n}") for n in range(G)]
        m_ready, m_split, m_in = sem("m_ready"), sem("m_split"), sem("m_in")
        misc_full, misc_read = sem("misc_full"), sem("misc_read")
        st_full, exp_done, pv_done = sem("st_full"), sem("exp_done"), sem("pv_done")
        o_out, x2_ready, x2_out, link, init, init16 = sem("o_out"), sem("x2_ready"), sem("x2_out"), sem("link"), sem("init"), sem("init16")
        y_ready, bn_done, stats_done, xn_free, o_zero = sem("y_ready"), sem("bn_done"), sem("stats_done"), sem("xn_free"), sem("o_zero")
        block = ctx.enter_context(nc.Block())

        FREE = 1
        SENT = 16
        UNIT = 16 * 2 * len(Q_PART)
        LOOP_TURNS, LAST_TURNS = bank_turns(False), bank_turns(True)

        class Round:

            def __init__(self, b, first=False, last=False):
                self.b, self.ahead, self.last, self.first = b, 0 if first else 1, last, first
                self.turns = FIRST_TURNS if first else LAST_TURNS if last else LOOP_TURNS

            def batch(self, per_batch, n):
                return per_batch * self.b + n

            def following(self, per_batch, n):
                return per_batch * self.b + (per_batch * self.ahead + n)

            def bank_count(self, turn):
                if self.first:
                    return turn // 2
                return len(LOOP_TURNS) // 2 * self.b + (len(FIRST_TURNS) // 2 + turn // 2)

            def product_turn(self, n):
                return misc_turn("product", n) - (1 if self.last else 0)

            def misc_count(self, turn):
                return 0 if self.first else MISC_TURNS * self.b + (1 + turn)

        def bank_empty(eng, r, use):
            turn = r.turns[use]
            eng.wait_ge(bank_read[turn % 2], r.bank_count(turn) + FREE)

        def bank_moved(eng, r, use):
            turn = r.turns[use]
            eng.wait_ge(bank_read[turn % 2], r.bank_count(turn) + (1 + FREE))

        @block.sync
        def _(sp):
            c = Counts(sp)
            for s in (*bank_read, misc_read, o_out, x2_ready, m_ready, ln_done, xg_ready, vp_ready, stats_done, part_free,
                      group_done, scratch_free):
                sp.sem_inc(s, FREE)
            for s in (exp_done, roped):
                sp.sem_inc(s, 2 * FREE)
            sp.sem_inc(pv_done, PT_BUFS * FREE)
            for s in (*unit_in, x2_out):
                sp.sem_inc(s, SENT)
            xv = x.rearrange("(b t p) d -> p b t d", b=B, p=P)
            x_next = x[T:, :].rearrange("(b t p) d -> p b t d", b=B - 1, p=P)
            x2v = x2_dram.rearrange("(b t p) d -> p b t d", b=B, p=P)
            sp.dma_start(xb[:], xv[:, 0, :, :]).then_inc(x_in, 16)
            for dst, src in ((wqk, "wqk"), (wv, "wv"), (wo, "wo")):
                sp.dma_start(dst[:], ins[src].rearrange("(c p) n -> p c n", p=P)).then_inc(w_in, 16)
            sp.dma_start(bqk[:], ins["bqk"]).then_inc(w_in, 16)
            for dst, src in ((bv, "bv"), (bo, "bo")):
                sp.dma_start(dst[:], ins[src].partition_broadcast(P)).then_inc(w_in, 16)
            for dst, src in ((ident[:], "ident"), (tri[:], "tri"), (after, "after")):
                sp.dma_start(dst, ins[src]).then_inc(w_in, 16)

            def folded(e):
                sp.wait_ge(fold_free, e + 1)

            def expert_weights(e):
                n = EXPERT_BUF[e]
                for dst, src in ((w1[n], "w1_t"), (w2[n], "w2")):
                    sp.dma_start(dst, ins[src].rearrange("(e c p) d -> e p c d", c=FC, p=P)[e]).then_inc(fold_in[n], 16)

            sp.dma_start(b1[:].rearrange("p (e c) -> p e c", c=FC), ins["b1_t"].rearrange("e p c -> p e c")).then_inc(w_in, 16)
            sp.dma_start(b12[:], ins["b2"].rearrange("e (m p) -> (e m) p", p=P)).then_inc(w_in, 16)
            for dst, src in ((cos[:], "cos"), (sin[:], "sin")):
                sp.dma_start(dst, ins[src]).then_inc(c_in, 16)
            for e in range(4):
                expert_weights(e)

            def parts_to_scratch(r):
                for s in range(SLOTS):
                    w, m = divmod(s, 2)
                    c.wait(p3_ready)
                    if s == 0:
                        c.wait(scratch_free)
                    sp.dma_start(scratch[w, :, m * P:(m + 1) * P, :].rearrange("s p t -> p s t"),
                                 part[:, s, :, :]).then_inc(parts_out, 16)
                c.wait(parts_out, 16 * SLOTS)
                sp.sem_inc(part_free, 1)

            def operands(g):
                for p in range(len(Q_PART)):
                    for w, dst, which in ((0, qs[g], Q_PART[p]), (1, ks[g], K_PART[p])):
                        src = scratch[w, which, J * DH * g:J * DH * (g + 1), :].rearrange("(j d) t -> d j t", d=DH)
                        sp.dma_start(dst[DH * p:DH * (p + 1), :, :], src).then_inc(unit_in[g], 16)

            def minus_max_rows(g):
                c.wait(m_split)
                for n in range(MROWS):
                    row = qs[g][SROWS + n:SROWS + n + 1, :, :].rearrange("o j (q c) -> o (j q) c", c=P)
                    sp.dma_start(row, mpart[:, n, :]).then_inc(m_in, 16)

            def one_round(r):
                b = r.b
                if not r.last:
                    c.wait(xb_free)
                    sp.dma_start(xb[:], x_next[:, bass.ds(b, 1), :, :].rearrange("p o t d -> p (o t) d")).then_inc(x_in, 16)
                c.wait(group_done)
                operands(G - 1)
                sp.dma_start(ga[:], hold["mod_rows"][0, bass.ds(b, 1), :].partition_broadcast(P)
                             .rearrange("p o d -> p (o d)")).then_inc(ga_in, 16)
                c.wait(stats_done)
                if r.last:
                    sp.wait_ge(x2_out, r.batch(16, SENT))
                else:
                    c.wait(xn_free)
                sp.dma_start(xg[:], xv[:, bass.ds(b, 1), :, :].rearrange("p o t d -> p (o t) d")).then_inc(xg_in, 16)
                minus_max_rows(1)
                minus_max_rows(2)
                if r.last:
                    minus_max_rows(3)
                else:
                    parts_to_scratch(r)
                    c.wait(group_done)
                    operands(0)
                    minus_max_rows(3)
                    for g in range(1, G - 1):
                        c.wait(group_done)
                        operands(g)
                    minus_max_rows(0)
                c.wait(x2_done)
                sp.dma_start(x2v[:, bass.ds(b, 1), :, :].rearrange("p o t d -> p (o t) d"), xg[:]).then_inc(x2_out, 16)

            r = Round(0, first=True)
            bank_moved(sp, r, ("project", TRANSPOSES - 2))
            bank_moved(sp, r, ("project", TRANSPOSES - 1))
            sp.dma_start(x_more[0], xv[:, 1, :, :]).then_inc(more_x_in[0], 16)
            sp.wait_ge(roped, SLOTS + 2 * FREE)
            sp.dma_start(x_more[1], xv[:, 2, :, :]).then_inc(more_x_in[1], 16)
            parts_to_scratch(r)
            sp.wait_ge(stats_read, NT)
            sp.dma_start(x_more[0], xv[:, 3, :, :]).then_inc(more_x_in[0], 16)
            operands(0)
            folded(0)
            expert_weights(4)
            folded(1)
            expert_weights(5)
            folded(2)
            expert_weights(6)
            folded(3)
            operands(1)
            folded(4)
            expert_weights(7)
            folded(6)
            minus_max_rows(0)
            operands(2)
            folded(7)
            with c.rounds(0, B - 1) as b:
                one_round(Round(b))
            one_round(Round(B - 1, last=True))
            sp.wait_ge(x2_out, 16 * B + SENT)

        @block.gpsimd
        def _(pool):
            c = Counts(pool)
            nc.gpsimd.memset(mp[:], LOWEST).then_inc(init, 1)
            pool.wait_ge(init, 1)
            for n in range(G - 1):
                nc.gpsimd.memset(ks[n][SROWS:SROWS + MROWS, :, :], 1.0).then_inc(init, 1)
                pool.wait_ge(init, n + 2)
                if n == 0:
                    pool.wait_ge(w_in, 16 * 11)
                    nc.gpsimd.tensor_copy(ident16[:], ident[:]).then_inc(init16, 1)
                    nc.gpsimd.tensor_copy(after16[:], after).then_inc(init16, 1)
                    pool.wait_ge(init16, 2)
            nc.gpsimd.memset(vp[:, :, :, DH:DH + 1], 1.0).then_inc(init, 1)
            pool.wait_ge(init, G + 1)
            pool.wait_ge(c_in, 16 * 2)

            def times_sine(r, s):
                bank_moved(pool, r, ("project", TRANSPOSES + s))
                bank_moved(pool, r, ("project", TRANSPOSES + SLOTS + s))
                pool.wait_ge(roped, r.following(SLOTS, s + 1))
                nc.gpsimd.tensor_tensor(sw[:, s % 2, :], qk[:, s, :], sin[:], ALU.mult).then_inc(t2_ready, 1)

            def times_cosine(r, s):
                nc.gpsimd.tensor_tensor(qk[:, s, :], qk[:, s, :], cos[:], ALU.mult).then_inc(t1_ready, 1)

            def add_halves(r, s):
                pool.wait_ge(t1_ready, r.following(SLOTS, s + 1))
                pool.wait_ge(swapped, r.following(SLOTS, s + 1))
                nc.gpsimd.tensor_tensor(qk[:, s, :], qk[:, s, :], sw[:, s % 2, :], ALU.add).then_inc(roped, 1)

            def first_rest(r, s):
                pool.wait_ge(p1_ready, r.following(SLOTS, s + 1))
                nc.gpsimd.tensor_tensor(qk[:, s, :], qk[:, s, :], part[:, s, 0, :], ALU.subtract).then_inc(r1_ready, 1)

            def third_part(r, s):
                pool.wait_ge(p2_ready, r.following(SLOTS, s + 1))
                nc.gpsimd.tensor_tensor(part[:, s, 2, :], qk[:, s, :], part[:, s, 1, :], ALU.subtract)\
                    .then_inc(p3_ready, 1)

            def rotate_and_split(r):
                for s in range(SLOTS):
                    times_sine(r, s)
                    if s:
                        add_halves(r, s - 1)
                    if s == SLOTS - 1:
                        first_rest(r, 0)
                    times_cosine(r, s)
                add_halves(r, SLOTS - 1)
                for s in range(SLOTS):
                    if s:
                        first_rest(r, s)
                        third_part(r, s - 1)
                third_part(r, SLOTS - 1)

            def move_v(r):
                c.wait(v_done, V_USES)
                if not r.first:
                    c.wait(vp_free)
                nc.gpsimd.tensor_copy(vp[:, :, :, 0:DH], v_next[:].rearrange("p t (h d) -> p t h d", d=DH))\
                    .then_inc(v_moved, 1)
                c.wait(v_moved)
                pool.sem_inc(vp_ready, 1)
                pool.sem_inc(xb_free, 1)

            def residual(r):
                pool.wait_ge(xg_ready, r.batch(2, 2 + FREE))
                for i in range(NT // 2):
                    c.wait(y_ready)
                    nc.gpsimd.tensor_tensor(xg[:, 2 * i:2 * i + 2, :], xg[:, 2 * i:2 * i + 2, :], y_sb[i % 2], ALU.add)\
                        .then_inc(x2_ready, 1)

            def one_round(r):
                b = r.b
                pool.wait_ge(ga_in, 16 * b + 16)
                nc.gpsimd.tensor_tensor(gabo[:], ga[:], bo[:], ALU.mult).then_inc(xg_ready, 1)
                pool.wait_ge(xg_ready, 2 * b + (1 + FREE))
                pool.wait_ge(xg_in, 16 * b + 16)
                nc.gpsimd.tensor_tensor(xg[:], xg[:], gabo[:].unsqueeze(1).to_broadcast([P, NT, D]), ALU.add)\
                    .then_inc(xg_ready, 1)
                if not r.last:
                    rotate_and_split(r)
                    move_v(r)
                residual(r)

            r = Round(0, first=True)
            for s in range(SLOTS):
                times_sine(r, s)
            for s in range(SLOTS):
                third_part(r, s)
            move_v(r)
            pool.wait_ge(fold_free, 4)
            nc.gpsimd.memset(ks[G - 1][SROWS:SROWS + MROWS, :, :], 1.0).then_inc(init, 1)
            pool.wait_ge(init, G + 2)
            with c.rounds(0, B - 1) as b:
                one_round(Round(b))
            one_round(Round(B - 1, last=True))

        @block.tensor
        def _(pe):
            pe.wait_ge(w_in, 16 * 11)
            pe.wait_ge(o_zero, 1)

            def fold(e, m, f):
                n = EXPERT_BUF[e]
                if (m, f) == (0, 0):
                    pe.wait_ge(fold_in[n], 32 * EXPERT_BUF[:e + 1].count(n))
                    if e >= 2:
                        pe.wait_ge(w12_read, e - 1)
                product = nc.tensor.matmul(w12_ps[e % 2][:, m, :], w1[n][:, f, m * P:(m + 1) * P], w2[n][:, f, :],
                                           start=(f == 0), stop=(f == FC - 1))
                column = e * KC + m
                bias = nc.tensor.matmul(o_ps[:, column:column + 1], w2[n][:, f, m * P:(m + 1) * P],
                                        b1[:, e * FC + f:e * FC + f + 1], start=(f == 0), stop=(f == FC - 1))
                if (m, f) == (KC - 1, FC - 1):
                    product.then_inc(w12_full, 1)
                    bias.then_inc(fold_free, 1)

            def project(r, n):
                bank_empty(pe, r, ("project", n))
                bank = bank_ps[:, r.turns["project", n] % 2, :]
                if n < TRANSPOSES:
                    half, k = divmod(n, KC)
                    pe.wait_ge(ln_done, r.following(NT, 4 * (half + 1) + FREE))
                    for i in range(4):
                        last = nc.tensor.transpose(bank[:, i * P:(i + 1) * P],
                                                   xn[:, 4 * half + i, k * P:(k + 1) * P], ident[:])
                    last.then_inc(bank_for_act, 1)
                elif n < TRANSPOSES + QK_USES:
                    half, s = divmod(n - TRANSPOSES, SLOTS)
                    if s == 0:
                        bank_moved(pe, r, ("project", 2 * half))
                        bank_moved(pe, r, ("project", 2 * half + 1))
                    for k in range(KC):
                        last = nc.tensor.matmul(bank, wqk[:, k, s * P:(s + 1) * P], ht[:, k, half * HALF:(half + 1) * HALF],
                                                start=(k == 0), stop=(k == KC - 1))
                    last.then_inc(bank_for_act, 1)
                else:
                    i = n - TRANSPOSES - QK_USES
                    for t in (2 * i, 2 * i + 1):
                        for k in range(KC):
                            last = nc.tensor.matmul(bank[:, (t % 2) * D:(t % 2 + 1) * D],
                                                    ht[:, k, t * P:(t + 1) * P], wv[:, k, :],
                                                    start=(k == 0), stop=(k == KC - 1))
                    last.then_inc(bank_for_dve, 1)

            def score_chunk(r, chunk):
                g, ch = chunk[0] % G, chunk[1]
                qt, k0, keys, _ = CHUNK[ch % len(CHUNK)]
                j = ch // len(CHUNK)
                if ch == 0:
                    pe.wait_ge(unit_in[g], r.batch(UNIT, UNIT + SENT) if chunk[0] < G else r.following(UNIT, UNIT + SENT))
                    if g == G - 1:
                        pe.sem_inc(scratch_free, 1)
                bank_empty(pe, r, chunk)
                nc.tensor.matmul(bank_ps[:, r.turns[chunk] % 2, 0:keys], qs[g][0:SROWS, j, qt * P:(qt + 1) * P],
                                 ks[g][0:SROWS, j, k0:k0 + keys], start=True, stop=True).then_inc(bank_for_dve, 1)

            def misc_empty(r, turn):
                pe.wait_ge(misc_read, r.misc_count(turn) + FREE)

            def transpose_maxima(r, g):
                misc_empty(r, misc_turn("maxima", g))
                pe.wait_ge(m_ready, r.batch(G, g + 1 + FREE) if g else r.following(G, 1 + FREE))
                nc.tensor.transpose(misc_ps[0:J * NT, 0:P], negm[:], ident[:]).then_inc(misc_full, 1)

            def scores_for_exp(b, g, s, h):
                qh, kb, off, diagonal = STEP[s]
                if s == 0 and h == 0:
                    pe.wait_ge(m_in, 16 * MROWS * G * b + 16 * MROWS * (g + 1))
                pe.wait_ge(exp_done, 2 * STEPS * G * b + (2 * STEPS * g + 2 * s + h - 1 + 2 * FREE))
                for i in range(2):
                    j = 2 * h + i
                    if diagonal:
                        nc.tensor.matmul(st_ps[:, h, i, off:off + P], ident16[:], after16[:],
                                         start=True, stop=False, skip_group_check=True)
                    last = nc.tensor.matmul(st_ps[:, h, i, off:HALF],
                                            ks[g][0:SROWS + MROWS, j, kb * P:(kb + 1) * P],
                                            qs[g][0:SROWS + MROWS, j, qh * HALF + off:(qh + 1) * HALF],
                                            start=not diagonal, stop=True, skip_group_check=diagonal)
                last.then_inc(st_full, 1)

            def weigh_values(b, g, s, h):
                qh, kb, off, _ = STEP[s]
                pe.wait_ge(exp_done, 2 * STEPS * G * b + (2 * STEPS * g + 2 * s + h + 1 + 2 * FREE))
                if kb == 0 and h == 0:
                    pe.wait_ge(o_out, 2 * G * b + (2 * g + qh + FREE))
                if g == 0 and s == 0 and h == 0:
                    pe.wait_ge(vp_ready, b + (1 + FREE))
                for j in (2 * h, 2 * h + 1):
                    last = nc.tensor.matmul(o_ps[32 * j:32 * j + DH + 1, off:HALF], vp[:, kb, J * g + j, :],
                                            pt[:, s % PT_BUFS, j, off:HALF],
                                            start=(kb == 0), stop=(kb == 4 * qh + 3))
                if h:
                    last.then_inc(pv_done, 1)

            def transpose_output(r, g, qh):
                misc_empty(r, misc_turn("output", g, qh))
                pe.wait_ge(o_out, r.batch(2 * G, 2 * g + qh + 1 + FREE))
                for i in range(4):
                    last = nc.tensor.transpose(misc_ps[:, i * P:(i + 1) * P], o_sb[:, i * P:(i + 1) * P], ident[:])
                last.then_inc(misc_full, 1)

            def output_product(r, n):
                misc_empty(r, r.product_turn(n))
                if n < TRANSPOSES:
                    half, k = divmod(n, KC)
                    for i in range(4):
                        last = nc.tensor.transpose(misc_ps[:, i * P:(i + 1) * P],
                                                   ot[:, 4 * half + i, k * P:(k + 1) * P], ident[:])
                else:
                    i = n - TRANSPOSES
                    for t in (2 * i, 2 * i + 1):
                        for k in range(KC):
                            last = nc.tensor.matmul(misc_ps[:, (t % 2) * D:(t % 2 + 1) * D],
                                                    ht[:, k, t * P:(t + 1) * P], wo[:, k, :],
                                                    start=(k == 0), stop=(k == KC - 1))
                last.then_inc(misc_full, 1)

            def one_round(r):
                b = r.b
                for place in PLACES:
                    g, s = place
                    if not r.last:
                        for n in PROJECT_AT.get(place, ()):
                            project(r, n)
                    chunks = iter(chunks_at(place, r.last))

                    def next_chunk():
                        for chunk in chunks:
                            score_chunk(r, chunk)
                            break

                    next_chunk()
                    if g < G:
                        for h in range(2):
                            scores_for_exp(b, g, s, h)
                            next_chunk()
                        for h in range(2):
                            if s:
                                weigh_values(b, g, s - 1, h)
                            next_chunk()
                        if s == 1 and g:
                            transpose_output(r, g - 1, 1)
                        if s == 6:
                            transpose_output(r, g, 0)
                        if s == EARLY_STEP and g < G - 1:
                            transpose_maxima(r, g + 1)
                        if s == STEPS - 1:
                            for h in range(2):
                                weigh_values(b, g, s, h)
                    elif s == 0:
                        transpose_output(r, G - 1, 1)
                        if not r.last:
                            transpose_maxima(r, 0)
                    else:
                        output_product(r, s - 1)
                    next_chunk()

            r = Round(0, first=True)
            pieces = [(m, f) for m in range(KC) for f in range(FC)]
            for n in range(TRANSPOSES):
                project(r, n)
            for n in range(TRANSPOSES, PROJECT):
                project(r, n)
            for e in range(4):
                for piece in pieces:
                    fold(e, *piece)
            for i in range(CHUNKS + EARLY):
                if i == CHUNKS:
                    transpose_maxima(r, 0)
                score_chunk(r, (G, i) if i < CHUNKS else (G + 1, i - CHUNKS))
                fold(4 + i // len(pieces), *pieces[i % len(pieces)])
            pe.wait_ge(misc_read, 1 + FREE)
            pe.wait_ge(b12_step, COPIED)
            nc.tensor.transpose(misc_ps[0:E * KC, 0:P], b12c[:], ident[:]).then_inc(b12_step, 1)
            pe.wait_ge(b12_step, ADDED)
            pe.wait_ge(w12_read, E)
            pe.wait_ge(init, G + 2)
            pe.wait_ge(init16, 2)
            with pe.Fori(0, B - 1) as b:
                one_round(Round(b))
            one_round(Round(B - 1, last=True))

        @block.scalar
        def _(act):
            c = Counts(act)
            act.wait_ge(w_in, 16 * 11)

            def folded(e):
                act.wait_ge(w12_full, e + 1)
                if e:
                    act.wait_ge(w12_out, 16 * e)
                nc.scalar.activation(o_sb[:].rearrange("p (m d) -> p m d", m=KC), w12_ps[e % 2], ACT.Copy).then_inc(w12_read, 1)
                act.wait_ge(w12_read, e + 1)
                act.dma_start(hold["w12"].rearrange("(e m p) d -> e p m d", m=KC, p=P)[e],
                              o_sb[:].rearrange("p (m d) -> p m d", m=KC)).then_inc(w12_out, 16)

            def projected(r, n):
                turn = r.turns["project", n]
                bank, read = bank_ps[:, turn % 2, :], bank_read[turn % 2]
                if n < TRANSPOSES:
                    half, k = divmod(n, KC)
                    c.wait(bank_for_act)
                    nc.scalar.activation(ht[:, k, half * HALF:(half + 1) * HALF], bank, ACT.Identity,
                                         bias=ca1_sa[:, 1, k, bass.ds(r.b + r.ahead, 1)],
                                         scale=ca1_sa[:, 0, k, bass.ds(r.b + r.ahead, 1)]).then_inc(read, 1)
                else:
                    half, s = divmod(n - TRANSPOSES, SLOTS)
                    if n == TRANSPOSES:
                        c.wait(part_free)
                    c.wait(bank_for_act)
                    nc.scalar.activation(qk[:, s, half * HALF:(half + 1) * HALF], bank, ACT.Identity,
                                         bias=bqk[:, s:s + 1]).then_inc(read, 1)

            def first_part(r, s):
                act.wait_ge(roped, r.following(SLOTS, s + 1 + 2 * FREE))
                nc.scalar.activation(part[:, s, 0, :], qk[:, s, :], ACT.Copy).then_inc(p1_ready, 1)

            def second_part(r, s):
                act.wait_ge(r1_ready, r.following(SLOTS, s + 1))
                nc.scalar.activation(part[:, s, 1, :], qk[:, s, :], ACT.Copy).then_inc(p2_ready, 1)

            def output_out(r, g, qh):
                act.wait_ge(pv_done, r.batch(STEPS * G, STEPS * g + 4 + 8 * qh + PT_BUFS * FREE))
                if qh:
                    act.wait_ge(misc_full, r.misc_count(misc_turn("output", g, 0) + 1))
                elif g:
                    act.wait_ge(misc_full, r.misc_count(misc_turn("output", g - 1, 1) + 1))
                else:
                    act.wait_ge(misc_full, r.misc_count(0))
                nc.scalar.activation(o_sb[:], o_ps[:], ACT.Copy).then_inc(o_out, 1)
                if qh:
                    act.sem_inc(group_done, 1)

            def one_round(r):
                b = r.b
                for place in PLACES:
                    g, s = place
                    if not r.last:
                        for n in PROJECT_AT.get(place, ()):
                            if n < TRANSPOSES + QK_USES:
                                projected(r, n)
                            if n == TRANSPOSES - 1:
                                act.sem_inc(xn_free, 1)
                        if at(place, 17) is not None:
                            first_part(r, at(place, 17))
                        if at(place, 20) is not None:
                            second_part(r, at(place, 20))
                    if g < G:
                        off = STEP[s][2]
                        act.wait_ge(pv_done, STEPS * G * b + (STEPS * g + s + FREE))
                        for h in range(2):
                            act.wait_ge(st_full, 2 * STEPS * G * b + (2 * STEPS * g + 2 * s + h + 1))
                            nc.scalar.activation(pt[:, s % PT_BUFS, 2 * h:2 * h + 2, off:HALF], st_ps[:, h, :, off:HALF],
                                                 ACT.Exp, scale=DH ** -0.5).then_inc(exp_done, 1)
                        if s == 0 and g:
                            output_out(r, g - 1, 1)
                        if s == 4:
                            output_out(r, g, 0)
                    elif s == 0:
                        output_out(r, G - 1, 1)
                        act.sem_inc(vp_free, 1)
                    elif s <= TRANSPOSES:
                        half, k = divmod(s - 1, KC)
                        act.wait_ge(misc_full, r.misc_count(r.product_turn(s - 1) + 1))
                        nc.scalar.activation(ht[:, k, half * HALF:(half + 1) * HALF], misc_ps[:], ACT.Copy)\
                            .then_inc(misc_read, 1)

            r = Round(0, first=True)
            for n in range(TRANSPOSES + QK_USES):
                projected(r, n)
            for s in range(SLOTS):
                first_part(r, s)
            for s in range(SLOTS):
                second_part(r, s)
            act.wait_ge(init16, 2)
            for e in range(E):
                folded(e)
                if e == 3:
                    act.wait_ge(std_step, VAR)
                    nc.scalar.activation(mean_rstd1[:, NT:, 1], mean_rstd1[:, NT:, 1], ACT.Sqrt).then_inc(std_step, 1)
            act.wait_ge(fold_free, E)
            nc.scalar.activation(b12c[:], o_ps[:, 0:E * KC], ACT.Copy).then_inc(b12_step, 1)
            act.wait_ge(b12_step, ADDED)
            act.dma_start(hold["b12"].rearrange("e (m p) -> (e m) p", p=P), b12[:]).then_inc(w12_out, 16)
            act.wait_ge(w12_out, 16 * (E + 1))
            with c.rounds(0, B - 1) as b:
                one_round(Round(b))
            one_round(Round(B - 1, last=True))

        @block.vector
        def _(dve):
            c = Counts(dve)
            nc.vector.memset(o_ps[:], 0.0).then_inc(o_zero, 1)
            dve.wait_ge(w_in, 16 * 11)
            dve.wait_ge(c_in, 16 * 2)
            swap = [DH * (i // DH) + (i + DH // 2) % DH for i in range(32)]

            def hand_over(*instructions):
                for ins in instructions:
                    ins.then_inc(link, 1)
                c.wait(link, len(instructions))

            def norm(r, half):
                if half == 0:
                    hand_over(nc.vector.tensor_copy(stat[:], mean_rstd1[:, bass.ds(NT * r.b + NT * r.ahead, NT), :]))
                    dve.wait_ge(x_in, r.following(16, 16))
                    dve.wait_ge(x2_out, r.batch(16, SENT))
                for t in range(4 * half, 4 * half + 4):
                    nc.vector.tensor_scalar(xn[:, t, :], xb[:, t, :], stat[:, t, 0:1], stat[:, t, 1:2],
                                            ALU.subtract, ALU.mult).then_inc(ln_done, 1)

            def swap_halves(s):
                c.wait(t2_ready)
                nc.vector.stream_shuffle(sw[:, s % 2, :], sw[:, s % 2, :], swap).then_inc(swapped, 1)

            def times_cosine(s):
                nc.vector.tensor_tensor(qk[:, s, :], qk[:, s, :], cos[:], ALU.mult).then_inc(t1_ready, 1)

            def add_halves(s):
                dve.wait_ge(t1_ready, s + 1)
                dve.wait_ge(swapped, s + 1)
                nc.vector.tensor_tensor(qk[:, s, :], qk[:, s, :], sw[:, s % 2, :], ALU.add).then_inc(roped, 1)

            def first_rest(s):
                dve.wait_ge(p1_ready, s + 1)
                nc.vector.tensor_tensor(qk[:, s, :], qk[:, s, :], part[:, s, 0, :], ALU.subtract).then_inc(r1_ready, 1)

            def v_out(r, i):
                turn = r.turns["project", TRANSPOSES + QK_USES + i]
                if i == 0:
                    dve.wait_ge(vp_ready, r.following(1, FREE))
                c.wait(bank_for_dve)
                hand_over(nc.vector.tensor_tensor(
                    v_next[:, 2 * i:2 * i + 2, :], bank_ps[:, turn % 2, :].rearrange("p (t d) -> p t d", t=2),
                    bv[:].unsqueeze(1).to_broadcast([P, 2, D]), ALU.add))
                dve.sem_inc(v_done, 1)
                dve.sem_inc(bank_read[turn % 2], 1)

            def chunk_maximum(r, chunk):
                turn, ch = r.turns[chunk], chunk[1]
                qt, _, keys, diagonal = CHUNK[ch % len(CHUNK)]
                row = ch // len(CHUNK) * NT + qt
                c.wait(bank_for_dve)
                if diagonal:
                    ins = nc.vector.tensor_tensor_reduce(
                        out=junk[:, turn % 2, 0:keys], in0=bank_ps[:, turn % 2, 0:keys], in1=tri[:, HALF - keys:HALF],
                        scale=1.0, scalar=LOWEST, op0=ALU.add, op1=ALU.max, accum_out=mp[:, row, 0:1])
                else:
                    ins = nc.vector.tensor_reduce(mp[:, row, 1:2], bank_ps[:, turn % 2, 0:keys], AX.X, ALU.max)
                ins.then_inc(bank_read[turn % 2], 1)

            def group_maxima(r, g):
                bank_moved(dve, r, (g, CHUNKS - 2))
                bank_moved(dve, r, (g, CHUNKS - 1))
                hand_over(nc.vector.tensor_reduce(negm[:], mp[:], AX.X, ALU.max, negate=True))
                dve.sem_inc(m_ready, 1)

            def split_maxima(r, g):
                turn = misc_turn("maxima", g)
                dve.wait_ge(misc_full, r.misc_count(turn) + 1)
                if not r.first:
                    dve.wait_ge(m_in, r.batch(16 * MROWS * G, 16 * MROWS * (g if g else G)))
                hand_over(nc.vector.tensor_copy(mpart[:, 0, :], misc_ps[0:J * NT, 0:P]))
                nc.vector.tensor_tensor(mres[:], misc_ps[0:J * NT, 0:P], mpart[:, 0, :], ALU.subtract)\
                    .then_inc(misc_read, 1)
                dve.wait_ge(misc_read, r.misc_count(turn) + (1 + FREE))
                hand_over(nc.vector.tensor_copy(mpart[:, 1, :], mres[:]))
                nc.vector.tensor_tensor(mpart[:, 2, :], mres[:], mpart[:, 1, :], ALU.subtract).then_inc(m_split, 1)

            def divide_output(r, g, qh):
                dve.wait_ge(misc_full, r.misc_count(misc_turn("output", g, qh) + 1))
                o = misc_ps[:].rearrange("p (t j d) -> p t j d", t=4, j=J)
                hand_over(nc.vector.reciprocal(rec[:], o[:, :, :, DH]))
                nc.vector.tensor_tensor(
                    ot[:, 4 * qh:4 * qh + 4, J * DH * g:J * DH * (g + 1)].rearrange("p t (j d) -> p t j d", d=DH),
                    o[:, :, :, 0:DH], rec[:].unsqueeze(3).to_broadcast([P, 4, J, DH]), ALU.mult)\
                    .then_inc(misc_read, 1)

            def statistics(r, i):
                dve.wait_ge(x2_ready, r.batch(NT // 2, i + 1 + FREE))
                for t in (2 * i, 2 * i + 1):
                    nc.vector.bn_stats(stat6[:, t, :], xg[:, t, :]).then_inc(bn_done, 1)

            def gated(r, i):
                turn = r.product_turn(TRANSPOSES + i)
                dve.wait_ge(misc_full, r.misc_count(turn + 1))
                hand_over(nc.vector.tensor_tensor(y_sb[i % 2], misc_ps[:].rearrange("p (t d) -> p t d", t=2),
                                                  ga[:].unsqueeze(1).to_broadcast([P, 2, D]), ALU.mult))
                dve.sem_inc(misc_read, 1)
                dve.sem_inc(y_ready, 1)
                if i:
                    statistics(r, i - 1)

            def one_round(r):
                b = r.b
                for place in PLACES:
                    g, s = place
                    if not r.last:
                        for n in PROJECT_AT.get(place, ()):
                            if n >= TRANSPOSES + QK_USES:
                                v_out(r, n - TRANSPOSES - QK_USES)
                    for chunk in chunks_at(place, r.last):
                        chunk_maximum(r, chunk)
                    if g < G:
                        if s == 2 and g:
                            divide_output(r, g - 1, 1)
                        if s == 7:
                            divide_output(r, g, 0)
                        if g < G - 1:
                            if s == EARLY_STEP - 1:
                                group_maxima(r, g + 1)
                            if s == EARLY_STEP + 1:
                                split_maxima(r, g + 1)
                        elif s == STEPS - 1 and not r.last:
                            group_maxima(r, G)
                    elif s == 0:
                        divide_output(r, G - 1, 1)
                        if not r.last:
                            split_maxima(r, 0)
                    elif s > TRANSPOSES:
                        gated(r, s - 1 - TRANSPOSES)
                    if not r.last:
                        if place in ((0, 4), (0, 5)):
                            norm(r, s - 4)
                        if at(place, 13) is not None:
                            swap_halves(at(place, 13))
                statistics(r, NT // 2 - 1)
                dve.sem_inc(x2_done, 1)
                c.wait(bn_done, NT)
                dve.sem_inc(stats_done, 1)
                hand_over(*[nc.vector.bn_aggr(stat2[:, t, :], stat6[:, t, :]) for t in range(NT)])
                hand_over(nc.vector.tensor_copy(mean_var2[:, bass.ds(NT * b, NT), :], stat2[:]))

            r = Round(0, first=True)
            norm(r, 0)
            norm(r, 1)
            for s in range(2):
                swap_halves(s)
                times_cosine(s)
            for s in range(2):
                v_out(r, s)
                add_halves(s)
            for s in range(2, SLOTS):
                swap_halves(s)
                times_cosine(s)
                v_out(r, s)
            for s in range(2, SLOTS):
                add_halves(s)
            for s in range(SLOTS):
                first_rest(s)
            for b in range(1, B):
                n = (b - 1) % 2
                dve.wait_ge(more_x_in[n], 16 * ((b + 1) // 2))
                for t in range(NT):
                    nc.vector.bn_stats(stat6[:, t, :], x_more[n][:, t, :]).then_inc(stats_read, 1)
                dve.wait_ge(stats_read, NT * b)
                hand_over(*[nc.vector.bn_aggr(mean_rstd1[:, NT * b + t, :], stat6[:, t, :]) for t in range(NT)])
            nc.vector.tensor_scalar(mean_rstd1[:, NT:, 1], mean_rstd1[:, NT:, 1], EPS, None, ALU.add).then_inc(std_step, 1)
            dve.wait_ge(init, G + 1)
            for ch in range(CHUNKS):
                chunk_maximum(r, (G, ch))
            dve.wait_ge(std_step, STD)
            hand_over(nc.vector.reciprocal(mean_rstd1[:, NT:, 1], mean_rstd1[:, NT:, 1]))
            group_maxima(r, G)
            split_maxima(r, 0)
            for ch in range(EARLY):
                chunk_maximum(r, (G + 1, ch))
            dve.wait_ge(b12_step, TURNED)
            nc.vector.tensor_tensor(b12[:], b12[:], misc_ps[0:E * KC, 0:P], ALU.add).then_inc(b12_step, 1)
            with c.rounds(0, B - 1) as b:
                one_round(Round(b))
            one_round(Round(B - 1, last=True))


PAIRS = NT // 2


def batch_attention(nc, ins, hold):
    with ExitStack() as ctx:
        sb = lambda name, shape, dt=F32: ctx.enter_context(nc.sbuf_tensor(name, shape, dt))
        sem = lambda name: ctx.enter_context(nc.semaphore(name))
        ps = lambda name, shape: ctx.enter_context(nc.psum_tensor(name, shape, F32))
        H2 = 4
        D2 = D // H2
        w_in, w_out, bias_in, bias_out = (sb("b_w_in", [P, KC, 3 * D]), sb("b_w_out", [P, KC, D]),
                                          sb("b_bias_in", [P, 3 * D]), sb("b_bias_out", [P, D]))
        cb1, sbb, ident = sb("b_cb1", [P, B, D]), sb("b_sb", [P, B, D]), sb("b_ident", [P, P])
        x2 = [sb(f"b_x2_{n}", [P, B, D]) for n in range(2)]
        h = [sb(f"b_h_{n}", [P, B, D]) for n in range(2)]
        hb = [sb(f"b_hb_{n}", [P, B, D]) for n in range(2)]
        h_t = sb("b_h_t", [P, KC, B * P])
        qkv = [sb(f"b_qkv_{n}", [P, B, 3 * D]) for n in range(2)]
        stat = [sb(f"b_stat_{n}", [P, B, 2]) for n in range(2)]
        prod = [sb(f"b_prod_{n}", [P, B, D]) for n in range(4)]
        score, top, pr, total = sb("b_score", [P, B, B, H2]), sb("b_top", [P, B, H2]), sb("b_pr", [P, B, B, H2]), sb("b_total", [P, B, H2])
        weighted = [sb(f"b_weighted_{n}", [P, B, D]) for n in range(4)]
        o_t = sb("b_o_t", [P, KC, B * P])
        y = sb("b_y", [P, B, D])
        st6, st2 = sb("b_st6", [P, B, 6]), sb("b_st2", [P, B, 2])
        zero = sb("b_zero", [P, 4 * D])
        t_ps, qkv_ps, y_ps = ps("b_t_ps", [P, 2, HALF]), ps("b_qkv_ps", [P, 2, 2 * HALF]), ps("b_y_ps", [P, 2, HALF])
        mean_rstd2, mean_rstd3, y_all = hold["mean_rstd2"], hold["mean_rstd3"], hold["y_all"]

        c_in, weights_in, zero_ready, zero_out = sem("b_c_in"), sem("b_w_in"), sem("b_zero_ready"), sem("b_zero_out")
        x2_in, x2_free = [sem("b_x2_in0"), sem("b_x2_in1")], sem("b_x2_free")
        var_ready, std_ready, h_for_pe, h_for_pool = sem("b_var"), sem("b_std"), sem("b_h_for_pe"), sem("b_h_for_pool")
        h_free, hb_free, hb_made = sem("b_h_free"), sem("b_hb_free"), sem("b_hb_made")
        hb_ready, t_full, t_read = sem("b_hb_ready"), sem("b_t_full"), sem("b_t_read")
        qkv_full, qkv_out, qkv_read = sem("b_qkv_full"), sem("b_qkv_out"), sem("b_qkv_read")
        qkv_for_pool = sem("b_qkv_for_pool")
        qkv_ready, bias_added, prod_free = sem("b_qkv_ready"), sem("b_bias_added"), sem("b_prod_free")
        qk_product, pr_for_pool, v_product = sem("b_qk_product"), sem("b_pr_for_pool"), sem("b_v_product")
        exp_in, exp_out, o_ready, o_full, o_read = sem("b_exp_in"), sem("b_exp_out"), sem("b_o_ready"), sem("b_o_full"), sem("b_o_read")
        y_full, y_read, y_ready, y_copied, link = sem("b_y_full"), sem("b_y_read"), sem("b_y_ready"), sem("b_y_copied"), sem("b_link")
        block = ctx.enter_context(nc.Block())
        x2v = hold["x2"].rearrange("(b i n p) d -> n p i b d", b=B, n=2, p=P)

        def schedule(c, one_round):
            one_round(0, None, None, 1)
            one_round(1, 0, None, 0)
            with c.rounds(0, PAIRS - 1) as i:
                for this in (1, 2):
                    one_round(2 * i + (this + 1), 2 * i + this, 2 * i + (this - 1), this % 2)
            one_round(None, NT - 1, NT - 2, 1)
            one_round(None, None, NT - 1, 0)

        @block.sync
        def _(sp):
            c = Counts(sp)
            sp.sem_inc(x2_free, 2)

            def load_x2(i, n):
                c.wait(x2_free)
                for b in range(B):
                    sp.dma_start(x2[n][:, b, :], x2v[n][:, bass.ds(i, 1), b, :].rearrange("p o d -> p (o d)"))\
                      .then_inc(x2_in[n], 16)

            for dst, n in ((cb1, 2), (sbb, 3)):
                sp.dma_start(dst[:], hold["mod_rows"][n].partition_broadcast(P)).then_inc(c_in, 16)
            load_x2(0, 0)
            sp.dma_start(ident[:], ins["ident"]).then_inc(weights_in, 16)
            for dst, src in ((w_in, "w_in"), (w_out, "w_out")):
                sp.dma_start(dst[:], ins[src].rearrange("(c p) n -> p c n", p=P)).then_inc(weights_in, 16)
            for dst, src in ((bias_in, "b_in"), (bias_out, "b_out")):
                sp.dma_start(dst[:], ins[src].partition_broadcast(P)).then_inc(weights_in, 16)
            with c.rounds(0, PAIRS - 1) as i:
                load_x2(i, 1)
                load_x2(i + 1, 0)
            load_x2(PAIRS - 1, 1)
            sp.wait_ge(zero_ready, 1)
            slots = hold["slots_in"].rearrange("(r p t) d -> r p (t d)", p=P, t=4)
            for r in range(E):
                sp.dma_start(slots[r], zero[:]).then_inc(zero_out, 16)
            sp.wait_ge(zero_out, 16 * E)

        @block.tensor
        def _(pe):
            c = Counts(pe)
            pe.wait_ge(weights_in, 16 * 5)

            def project(n):
                c.wait(h_for_pe)
                for k in range(KC):
                    for b in range(B):
                        last = nc.tensor.transpose(t_ps[:, k, b * P:(b + 1) * P], h[n][:, b, k * P:(k + 1) * P], ident[:])
                    last.then_inc(t_full, 1)
                c.wait(t_read, 2)
                for b in range(B):
                    c.wait(qkv_read)
                    for lo, hi in ((0, HALF), (HALF, 3 * D)):
                        for k in range(KC):
                            last = nc.tensor.matmul(qkv_ps[:, b % 2, lo:hi], h_t[:, k, b * P:(b + 1) * P],
                                                    w_in[:, k, lo:hi], start=(k == 0), stop=(k == KC - 1))
                    last.then_inc(qkv_full, 1)

            def output():
                c.wait(y_read, 2)
                c.wait(o_ready)
                for l in range(B):
                    if l == 2:
                        c.wait(v_product, 2)
                    for k in range(KC):
                        terms = B if l >= 2 else B // 2
                        for m in range(terms):
                            last = nc.tensor.matmul(y_ps[:, k, l * P:(l + 1) * P], weighted[l][:, m, k * P:(k + 1) * P], ident[:],
                                                    start=(m == 0), stop=(m == terms - 1))
                        if l == B - 1:
                            last.then_inc(o_full, 1)
                c.wait(o_read, 2)
                for u in range(2):
                    for b in (2 * u, 2 * u + 1):
                        for k in range(KC):
                            last = nc.tensor.matmul(y_ps[:, u, (b % 2) * D:(b % 2 + 1) * D], o_t[:, k, b * P:(b + 1) * P],
                                                    w_out[:, k, :], start=(k == 0), stop=(k == KC - 1))
                    last.then_inc(y_full, 1)

            def one_round(after, this, before, n):
                if after is not None:
                    project(1 - n)
                if this is not None:
                    output()

            schedule(c, one_round)

        @block.scalar
        def _(act):
            c = Counts(act)
            c.wait(var_ready)
            nc.scalar.activation(mean_rstd2[:, :, 1], mean_rstd2[:, :, 1], ACT.Sqrt).then_inc(std_ready, 1)
            act.sem_inc(qkv_read, 2)

            def one_round(after, this, before, n):
                if after is not None:
                    for k in range(KC):
                        c.wait(t_full)
                        nc.scalar.activation(h_t[:, k, :], t_ps[:, k, :], ACT.Copy).then_inc(t_read, 1)
                if this is not None:
                    c.wait(exp_in)
                    nc.scalar.activation(pr[:], score[:], ACT.Exp, scale=D2 ** -0.5).then_inc(exp_out, 1)
                if before is not None:
                    c.wait(y_ready)
                    nc.scalar.activation(y_all[:].rearrange("p (b t) d -> p b t d", b=B)[:, :, bass.ds(before, 1), :]
                                         .rearrange("p b o d -> p b (o d)"), y[:], ACT.Copy).then_inc(y_copied, 1)
                if after is not None:
                    for b in range(B):
                        c.wait(qkv_full)
                        nc.scalar.activation(qkv[1 - n][:, b, :], qkv_ps[:, b % 2, 0:3 * D], ACT.Copy).then_inc(qkv_out, 1)
                        c.wait(qkv_out)
                        act.sem_inc(qkv_read, 1)
                        act.sem_inc(qkv_for_pool, 1)
                if this is not None:
                    for k in range(KC):
                        c.wait(o_full)
                        nc.scalar.activation(o_t[:, k, :], y_ps[:, k, :], ACT.Copy).then_inc(o_read, 1)

            schedule(c, one_round)

        @block.gpsimd
        def _(pool):
            c = Counts(pool)
            nc.gpsimd.memset(zero[:], 0.0).then_inc(zero_ready, 1)
            pool.wait_ge(weights_in, 16 * 5)

            def one_round(after, this, before, n):
                if this is not None:
                    c.wait(prod_free, 2)
                    for l in (2, 3):
                        nc.gpsimd.tensor_tensor(prod[l][:], qkv[n][:, l:l + 1, 0:D].to_broadcast([P, B, D]),
                                                qkv[n][:, :, D:2 * D], ALU.mult).then_inc(qk_product, 1)
                if this is not None:
                    c.wait(pr_for_pool)
                    for l in (2, 3):
                        nc.gpsimd.tensor_tensor(weighted[l][:].rearrange("p m (h d) -> p m h d", h=H2),
                                                qkv[n][:, :, 2 * D:3 * D].rearrange("p m (h d) -> p m h d", h=H2),
                                                pr[:, l, :, :].unsqueeze(3).to_broadcast([P, B, H2, D2]), ALU.mult)\
                            .then_inc(v_product, 1)
                if after is not None:
                    for b in range(B):
                        c.wait(qkv_for_pool)
                        nc.gpsimd.tensor_tensor(qkv[1 - n][:, b, :], qkv[1 - n][:, b, :], bias_in[:], ALU.add)\
                            .then_inc(bias_added, 1)
                    c.wait(bias_added, B)
                    pool.sem_inc(qkv_ready, 1)
                    c.wait(h_for_pool)
                    c.wait(hb_free)
                    nc.gpsimd.tensor_tensor(hb[1 - n][:], h[1 - n][:], bias_out[:].unsqueeze(1).to_broadcast([P, B, D]), ALU.add)\
                        .then_inc(hb_made, 1)
                    c.wait(hb_made)
                    pool.sem_inc(h_free, 1)
                    pool.sem_inc(hb_ready, 1)

            schedule(c, one_round)

        @block.vector
        def _(dve):
            c = Counts(dve)

            def hand_over(*instructions):
                for ins in instructions:
                    ins.then_inc(link, 1)
                c.wait(link, len(instructions))

            dve.sem_inc(y_copied, 1)
            hand_over(nc.vector.tensor_scalar(mean_rstd2[:, :, 1], mean_rstd2[:, :, 1], EPS, None, ALU.add))
            dve.sem_inc(var_ready, 1)
            c.wait(std_ready)
            hand_over(nc.vector.reciprocal(mean_rstd2[:, :, 1], mean_rstd2[:, :, 1]))
            dve.wait_ge(c_in, 16 * 2)
            dve.sem_inc(y_read, 2)
            dve.sem_inc(h_free, 2)
            dve.sem_inc(hb_free, 2)
            dve.sem_inc(prod_free, 2)

            def norm(tile, n):
                c.wait(h_free)
                hand_over(nc.vector.tensor_copy(stat[n][:], mean_rstd2[:].rearrange("p (b t) s -> p b t s", b=B)
                                                [:, :, bass.ds(tile, 1), :].rearrange("p b o s -> p b (o s)")))
                c.wait(x2_in[n], 64)
                hand_over(*[nc.vector.scalar_tensor_tensor(h[n][:, b, :], x2[n][:, b, :], stat[n][:, b, 0:1], cb1[:, b, :],
                                                           ALU.subtract, ALU.mult) for b in range(B)])
                dve.sem_inc(x2_free, 1)
                hand_over(*[nc.vector.scalar_tensor_tensor(h[n][:, b, :], h[n][:, b, :], stat[n][:, b, 1:2], sbb[:, b, :],
                                                           ALU.mult, ALU.add) for b in range(B)])
                dve.sem_inc(h_for_pe, 1)
                dve.sem_inc(h_for_pool, 1)

            def attend(n):
                c.wait(qkv_ready)
                hand_over(*[nc.vector.tensor_tensor(prod[l][:], qkv[n][:, l:l + 1, 0:D].to_broadcast([P, B, D]),
                                                    qkv[n][:, :, D:2 * D], ALU.mult) for l in range(2)])
                sums = []
                for l in range(B):
                    if l >= 2:
                        c.wait(qk_product)
                    sums.append(nc.vector.tensor_reduce(score[:, l, :, :].rearrange("p m h -> p (m h)"),
                                                        prod[l][:].rearrange("p m (h d) -> p (m h) d", h=H2),
                                                        AX.X, ALU.add))
                    sums[-1].then_inc(link, 1)
                c.wait(link, B)
                dve.sem_inc(prod_free, 2)
                hand_over(nc.vector.tensor_reduce(top[:], score[:].rearrange("p l m h -> p l h m"), AX.X, ALU.max))
                hand_over(nc.vector.tensor_tensor(score[:], score[:], top[:].unsqueeze(2).to_broadcast([P, B, B, H2]),
                                                  ALU.subtract))
                dve.sem_inc(exp_in, 1)

            def divide():
                c.wait(exp_out)
                hand_over(nc.vector.tensor_reduce(total[:], pr[:].rearrange("p l m h -> p l h m"), AX.X, ALU.add))
                hand_over(nc.vector.reciprocal(total[:], total[:]))
                hand_over(nc.vector.tensor_tensor(pr[:], pr[:], total[:].unsqueeze(2).to_broadcast([P, B, B, H2]), ALU.mult))
                dve.sem_inc(pr_for_pool, 1)

            def weigh(n):
                hand_over(*[nc.vector.tensor_tensor(weighted[l][:].rearrange("p m (h d) -> p m h d", h=H2),
                                                    qkv[n][:, :, 2 * D:3 * D].rearrange("p m (h d) -> p m h d", h=H2),
                                                    pr[:, l, :, :].unsqueeze(3).to_broadcast([P, B, H2, D2]), ALU.mult)
                            for l in range(2)])
                hand_over(*[nc.vector.tensor_tensor(weighted[l][:, 0:2, :], weighted[l][:, 0:2, :], weighted[l][:, 2:4, :], ALU.add)
                            for l in range(2)])
                dve.sem_inc(o_ready, 1)

            def output(tile, n):
                c.wait(y_copied)
                c.wait(hb_ready)
                for u in range(2):
                    c.wait(y_full)
                    nc.vector.tensor_tensor(y[:, 2 * u:2 * u + 2, :], y_ps[:, u, :].rearrange("p (b d) -> p b d", b=2),
                                            hb[n][:, 2 * u:2 * u + 2, :], ALU.add).then_inc(link, 1)
                c.wait(link, 2)
                dve.sem_inc(hb_free, 1)
                dve.sem_inc(y_read, 2)
                dve.sem_inc(y_ready, 1)
                hand_over(*[nc.vector.bn_stats(st6[:, b, :], y[:, b, :]) for b in range(B)])
                hand_over(*[nc.vector.bn_aggr(st2[:, b, :], st6[:, b, :]) for b in range(B)])
                hand_over(nc.vector.tensor_copy(mean_rstd3[:].rearrange("p (b t) s -> p b t s", b=B)
                                                [:, :, bass.ds(tile, 1), :].rearrange("p b o s -> p b (o s)"), st2[:]))

            def one_round(after, this, before, n):
                if after is not None:
                    norm(after, 1 - n)
                if this is not None:
                    attend(n)
                    divide()
                if before is not None:
                    output(before, 1 - n)
                if this is not None:
                    weigh(n)

            schedule(c, one_round)


def experts(nc, ins, hold):
    with ExitStack() as ctx:
        sb = lambda name, shape, dt=F32: ctx.enter_context(nc.sbuf_tensor(name, shape, dt))
        sem = lambda name: ctx.enter_context(nc.semaphore(name))
        ps = lambda name, shape: ctx.enter_context(nc.psum_tensor(name, shape, F32))
        R = 4
        NR = TILES // R
        mean_rstd3, y_all = hold["mean_rstd3"], hold["y_all"]
        slots_in, slots_out = hold["slots_in"], hold["slots_out"]
        g1, b1, g2, b2 = (sb(f"e_{n}", [P, D]) for n in ("g1", "b1", "g2", "b2"))
        gb, gain, shift = sb("e_gb", [P, B, D]), sb("e_gain", [P, B, D]), sb("e_shift", [P, B, D])
        ident, wg = sb("e_ident", [P, P]), sb("e_wg", [P, KC, E])
        w12, b12 = sb("e_w12", [P, E, KC, D]), sb("e_b12", [P, E, D])
        order, upto, ones = sb("e_order", [P, E]), sb("e_upto", [P, P], BF16), sb("e_ones", [P, P], BF16)
        upto32 = sb("e_upto32", [P, P])
        stat = [sb(f"e_stat_{n}", [P, R, 2]) for n in range(2)]
        y1 = [sb(f"e_y1_{n}", [P, R, D]) for n in range(2)]
        y1_t = [sb(f"e_y1_t_{n}", [P, KC, R * P]) for n in range(2)]
        logits, expo = sb("e_logits", [P, TILES, E]), sb("e_expo", [P, TILES, E])
        top, gate, first, kept = sb("e_top", [P, TILES]), sb("e_gate", [P, TILES]), sb("e_first", [P, TILES]), sb("e_kept", [P, TILES])
        hot, hot16 = sb("e_hot", [P, TILES, E]), sb("e_hot16", [P, TILES, E], BF16)
        sums = [sb(f"e_sums_{n}", [P, TILES, E]) for n in range(2)]
        place, slot, to, frm = sb("e_place", [P, TILES]), sb("e_slot", [P, TILES]), sb("e_to", [P, TILES]), sb("e_from", [P, TILES])
        to_i, frm_i = sb("e_to_i", [P, TILES], I32), sb("e_from_i", [P, TILES], I32)
        rows = [sb(f"e_rows_{n}", [P, R, D]) for n in range(2)]
        rows_t = [sb(f"e_rows_t_{n}", [P, KC, R * P]) for n in range(2)]
        res = [sb(f"e_res_{n}", [P, R, D]) for n in range(2)]
        got = sb("e_got", [P, TILES, D])
        st6, mr4 = sb("e_st6", [P, R, 6]), [sb(f"e_mr4_{n}", [P, R, 2]) for n in range(2)]
        minus = [sb(f"e_minus_{n}", [P, R]) for n in range(2)]
        x2 = sb("e_x2", [P, TILES, D])
        z, zn = [sb(f"e_z_{n}", [P, R, D]) for n in range(2)], [sb(f"e_zn_{n}", [P, R, D]) for n in range(2)]
        t_ps = [ps(f"e_t_ps{n}", [P, KC, HALF]) for n in range(2)]
        p_ps = [ps(f"e_p_ps{n}", [P, HALF]) for n in range(2)]
        q_ps = [ps(f"e_q_ps{n}", [P, HALF]) for n in range(2)]

        names = ("c_in", "link", "var_ready", "std_ready", "y1_for_pe", "y1_for_act", "t_full", "t_read",
                 "logit_full", "logit_read", "logits_ready", "exp_in", "exp_out", "hot_ready", "count_ready", "to_ready",
                 "fin_dve_ready", "scattered", "rows_free", "res_full", "res_read", "res_ready",
                 "all_out", "y1_c_in", "xb_ready", "z_normal", "zn_free", "scaled", "fin_ready", "fin_for_sp", "got_used",
                 "init", "y_kept", "all_y", "w_in", "rstd_ready")
        S = {n: sem("e_" + n) for n in names}
        rows_in, res_out = [sem("e_rows_in0"), sem("e_rows_in1")], [sem("e_res_out0"), sem("e_res_out1")]
        fin_out = sem("e_fin_out")
        gathered = [sem("e_gathered0"), sem("e_gathered1")]
        block = ctx.enter_context(nc.Block())
        Y1_CONSTS, CONSTS, WEIGHTS = 16 * 4, 16 * 5, 16 * 4
        slots_v = slots_in.rearrange("(i n t p) d -> n p i t d", n=2, t=R, p=P)
        res_v = slots_out.rearrange("(i n t p) d -> n p i t d", n=2, t=R, p=P)
        out_v = hold["out"].rearrange("(t p) d -> p t d", p=P)

        @block.sync
        def _(sp):
            c = Counts(sp)
            for dst, src in ((g1, "g1"), (b1, "ln1_b")):
                sp.dma_start(dst[:], ins[src].partition_broadcast(P)).then_inc(S["y1_c_in"], 16)
            sp.dma_start(ident[:], ins["ident"]).then_inc(S["y1_c_in"], 16)
            sp.dma_start(wg[:], ins["wg"].rearrange("(c p) e -> p c e", p=P)).then_inc(S["y1_c_in"], 16)
            for dst, src in ((g2, "g2"), (b2, "ln2_b"), (order, "order")):
                sp.dma_start(dst[:], ins[src].partition_broadcast(P)).then_inc(S["c_in"], 16)
            sp.dma_start(upto32[:], ins["upto"]).then_inc(S["c_in"], 16)
            sp.dma_start(gb[:], hold["mod_rows"][1].partition_broadcast(P)).then_inc(S["c_in"], 16)
            for h in range(2):
                e = E // 2
                sp.dma_start(w12[:, h * e:(h + 1) * e, :, :], hold["w12"].rearrange("(e c p) n -> p e c n", c=KC, p=P)
                             [:, h * e:(h + 1) * e, :, :]).then_inc(S["w_in"], 16)
            sp.dma_start(b12[:], hold["b12"].partition_broadcast(P)).then_inc(S["w_in"], 16)
            sp.dma_start(x2[:], hold["x2"].rearrange("(t p) d -> p t d", p=P)).then_inc(S["w_in"], 16)
            sp.sem_inc(S["rows_free"], 2)
            sp.wait_ge(S["scattered"], 16 * TILES)
            with c.rounds(0, E // 2) as i:
                for n in range(2):
                    c.wait(S["rows_free"])
                    sp.dma_start(rows[n][:], slots_v[n][:, bass.ds(i, 1), :, :].rearrange("p o t d -> p (o t) d"))\
                      .then_inc(rows_in[n], 16)
            for r in range(NR):
                c.wait(S["fin_dve_ready"] if r % 2 else S["fin_for_sp"])
                sp.dma_start(out_v[:, R * r:R * (r + 1), :], x2[:, R * r:R * (r + 1), :]).then_inc(fin_out, 16)
            sp.wait_ge(fin_out, 16 * NR)

        @block.tensor
        def _(pe):
            c = Counts(pe)
            pe.wait_ge(S["y1_c_in"], Y1_CONSTS)

            def transpose_y1(n):
                c.wait(S["y1_for_pe"])
                for k in range(KC):
                    for t in range(R):
                        last = nc.tensor.transpose(t_ps[n][:, k, t * P:(t + 1) * P], y1[n][:, t, k * P:(k + 1) * P], ident[:])
                    last.then_inc(S["t_full"], 1)

            def make_logits(n):
                c.wait(S["t_read"], KC)
                c.wait(S["logit_read"])
                for t in range(R):
                    for k in range(KC):
                        last = nc.tensor.matmul(p_ps[n][:, t * E:(t + 1) * E], y1_t[n][:, k, t * P:(t + 1) * P], wg[:, k, :],
                                                start=(k == 0), stop=(k == KC - 1))
                last.then_inc(S["logit_full"], 1)

            transpose_y1(0)
            with c.rounds(0, NR // 2 - 1):
                for n in range(2):
                    transpose_y1(1 - n)
                    make_logits(n)
            transpose_y1(1)
            make_logits(0)
            make_logits(1)
            pe.wait_ge(S["init"], 2)
            c.wait(S["hot_ready"])
            flat = hot16[:].rearrange("p t e -> p (t e)")
            nc.tensor.matmul(q_ps[0][:, 0:TILES * E], upto[:], flat, start=True, stop=True)
            nc.tensor.matmul(q_ps[1][:, 0:TILES * E], ones[:], flat, start=True, stop=True).then_inc(S["count_ready"], 1)

            def transpose_rows(n):
                c.wait(rows_in[n], 16)
                for k in range(KC):
                    for t in range(R):
                        last = nc.tensor.transpose(t_ps[n][:, k, t * P:(t + 1) * P], rows[n][:, t, k * P:(k + 1) * P], ident[:])
                    last.then_inc(S["t_full"], 1)

            def multiply(expert, n):
                c.wait(S["t_read"], KC)
                for u in range(2):
                    c.wait(S["res_read"])
                    for t in (2 * u, 2 * u + 1):
                        for k in range(KC):
                            last = nc.tensor.matmul(p_ps[u][:, (t % 2) * D:(t % 2 + 1) * D], rows_t[n][:, k, t * P:(t + 1) * P],
                                                    w12[:, bass.ds(expert, 1), k, :].rearrange("p o n -> p (o n)"),
                                                    start=(k == 0), stop=(k == KC - 1))
                    last.then_inc(S["res_full"], 1)

            pe.wait_ge(S["w_in"], WEIGHTS)
            transpose_rows(0)
            with c.rounds(0, E // 2 - 1) as i:
                for n in range(2):
                    transpose_rows(1 - n)
                    multiply(2 * i + n, n)
            transpose_rows(1)
            multiply(E - 2, 0)
            multiply(E - 1, 1)

        @block.scalar
        def _(act):
            c = Counts(act)
            c.wait(S["var_ready"])
            nc.scalar.activation(mean_rstd3[:, :, 1], mean_rstd3[:, :, 1], ACT.Sqrt).then_inc(S["std_ready"], 1)
            act.sem_inc(S["logit_read"], 2)

            def keep_y1(tile, n):
                for k in range(KC):
                    c.wait(S["t_full"])
                    nc.scalar.activation(y1_t[n][:, k, :], t_ps[n][:, k, :], ACT.Copy).then_inc(S["t_read"], 1)
                c.wait(S["y1_for_act"])
                nc.scalar.activation(y_all[:, bass.ds(tile, R), :], y1[n][:], ACT.Copy).then_inc(S["y_kept"], 1)

            def keep_logits(tile, n):
                c.wait(S["logit_full"])
                nc.scalar.activation(logits[:, bass.ds(tile, R), :].rearrange("p t e -> p (t e)"), p_ps[n][:, 0:R * E], ACT.Copy)\
                    .then_inc(S["logits_ready"], 1)
                c.wait(S["logits_ready"])
                act.sem_inc(S["logit_read"], 1)

            keep_y1(0, 0)
            with c.rounds(0, NR // 2 - 1) as i:
                for n in range(2):
                    keep_y1(2 * R * i + (R * n + R), 1 - n)
                    keep_logits(2 * R * i + R * n, n)
            keep_y1(TILES - R, 1)
            keep_logits(TILES - 2 * R, 0)
            keep_logits(TILES - R, 1)
            act.sem_inc(S["all_y"], 1)
            c.wait(S["exp_in"])
            nc.scalar.activation(expo[:], expo[:], ACT.Exp).then_inc(S["exp_out"], 1)

            def rows_from_ps(n):
                for k in range(KC):
                    c.wait(S["t_full"])
                    nc.scalar.activation(rows_t[n][:, k, :], t_ps[n][:, k, :], ACT.Copy).then_inc(S["t_read"], 1)
                act.sem_inc(S["rows_free"], 1)

            def store(pair, n):
                c.wait(S["res_ready"])
                act.dma_start(res_v[n][:, bass.ds(pair, 1), :, :].rearrange("p o t d -> p (o t) d"), res[n][:])\
                   .then_inc(res_out[n], 16)

            rows_from_ps(0)
            with c.rounds(0, E // 2 - 1) as i:
                for n in range(2):
                    rows_from_ps(1 - n)
                    store(i, n)
            rows_from_ps(1)
            store(E // 2 - 1, 0)
            store(E // 2 - 1, 1)

            def deviation(n):
                c.wait(S["var_ready"])
                nc.scalar.activation(mr4[n][:, :, 1], mr4[n][:, :, 1], ACT.Sqrt).then_inc(S["std_ready"], 1)

            def normalise(n):
                c.wait(S["rstd_ready"])
                if n == 0:
                    c.wait(S["zn_free"])
                for t in range(R):
                    last = nc.scalar.activation(zn[n][:, t, :], z[n][:, t, :], ACT.Identity,
                                                bias=minus[n][:, t:t + 1], scale=mr4[n][:, t, 1:2]).then_inc(S["z_normal"], 1)

            with c.rounds(0, NR // 2):
                for n in range(2):
                    deviation(n)
                    normalise(n)

        @block.gpsimd
        def _(pool):
            c = Counts(pool)
            nc.gpsimd.memset(ones[:], 1.0).then_inc(S["init"], 1)
            pool.wait_ge(S["c_in"], CONSTS)
            pool.wait_ge(S["init"], 1)
            nc.gpsimd.tensor_copy(upto[:], upto32[:]).then_inc(S["init"], 1)
            pool.wait_ge(S["init"], 2)
            nc.gpsimd.tensor_tensor(gain[:], gb[:], g2[:].unsqueeze(1).to_broadcast([P, B, D]), ALU.mult).then_inc(S["init"], 1)
            pool.wait_ge(S["init"], 3)
            nc.gpsimd.tensor_tensor(shift[:], gb[:], b2[:].unsqueeze(1).to_broadcast([P, B, D]), ALU.mult).then_inc(S["init"], 1)
            pool.wait_ge(S["init"], 4)
            pool.wait_ge(S["w_in"], WEIGHTS)
            for b in range(B):
                nc.gpsimd.tensor_tensor(x2[:, NT * b:NT * (b + 1), :], x2[:, NT * b:NT * (b + 1), :],
                                        shift[:, b:b + 1, :].to_broadcast([P, NT, D]), ALU.add).then_inc(S["xb_ready"], 1)
            c.wait(S["xb_ready"], B)
            c.wait(S["to_ready"])
            for t in range(TILES):
                nc.gpsimd.indirect_dma_start(
                    out=slots_in, out_offset=bass.IndirectOffsetOnAxis(ap=to_i[:, t:t + 1], axis=0),
                    in_=y_all[:, t, :], in_offset=None, bounds_check=E * CAP - 1, oob_is_err=False)\
                    .then_inc(S["scattered"], 16)
            c.wait(S["all_out"])

            def gather(r):
                for t in range(R * r, R * (r + 1)):
                    nc.gpsimd.indirect_dma_start(
                        out=got[:, t, :], out_offset=None, in_=slots_out,
                        in_offset=bass.IndirectOffsetOnAxis(ap=frm_i[:, t:t + 1], axis=0)).then_inc(gathered[r % 2], 16)

            gather(0)
            gather(1)
            for r in range(NR + 1):
                if r + 2 < NR:
                    c.wait(S["got_used"])
                    gather(r + 2)
                if r % 2:
                    c.wait(S["scaled"])
                    rows = x2[:, R * (r - 1):R * r, :]
                    nc.gpsimd.tensor_tensor(rows, rows, zn[0][:], ALU.add)\
                        .then_inc(S["fin_ready"], 1)
                    c.wait(S["fin_ready"])
                    pool.sem_inc(S["zn_free"], 1)
                    pool.sem_inc(S["fin_for_sp"], 1)

        @block.vector
        def _(dve):
            c = Counts(dve)

            def hand_over(*instructions):
                for ins_ in instructions:
                    ins_.then_inc(S["link"], 1)
                c.wait(S["link"], len(instructions))

            hand_over(nc.vector.tensor_scalar(mean_rstd3[:, :, 1], mean_rstd3[:, :, 1], EPS, None, ALU.add))
            dve.sem_inc(S["var_ready"], 1)
            c.wait(S["std_ready"])
            hand_over(nc.vector.reciprocal(mean_rstd3[:, :, 1], mean_rstd3[:, :, 1]))
            dve.wait_ge(S["y1_c_in"], Y1_CONSTS)
            dve.sem_inc(S["y_kept"], 2)
            with c.rounds(0, NR // 2) as i:
                for n in range(2):
                    tile = 2 * R * i + R * n
                    c.wait(S["y_kept"])
                    hand_over(nc.vector.tensor_copy(stat[n][:], mean_rstd3[:, bass.ds(tile, R), :]))
                    hand_over(*[nc.vector.scalar_tensor_tensor(
                        y1[n][:, t, :], y_all[:, bass.ds(tile + t, 1), :].rearrange("p o d -> p (o d)"), stat[n][:, t, 0:1], g1[:],
                        ALU.subtract, ALU.mult) for t in range(R)])
                    hand_over(*[nc.vector.scalar_tensor_tensor(y1[n][:, t, :], y1[n][:, t, :], stat[n][:, t, 1:2], b1[:],
                                                               ALU.mult, ALU.add) for t in range(R)])
                    dve.sem_inc(S["y1_for_pe"], 1)
                    dve.sem_inc(S["y1_for_act"], 1)
            c.wait(S["all_y"])
            dve.wait_ge(S["c_in"], CONSTS)
            wide = lambda a: a[:].unsqueeze(2).to_broadcast([P, TILES, E])
            hand_over(nc.vector.tensor_reduce(top[:], logits[:], AX.X, ALU.max))
            hand_over(nc.vector.tensor_tensor(expo[:], logits[:], wide(top), ALU.subtract),
                      nc.vector.tensor_tensor(hot[:], logits[:], wide(top), ALU.is_ge))
            dve.sem_inc(S["exp_in"], 1)
            hand_over(nc.vector.tensor_tensor(hot[:], hot[:], order[:].unsqueeze(1).to_broadcast([P, TILES, E]), ALU.mult))
            hand_over(nc.vector.tensor_reduce(first[:], hot[:], AX.X, ALU.max))
            hand_over(nc.vector.tensor_tensor(hot[:], hot[:], wide(first), ALU.is_equal))
            hand_over(nc.vector.tensor_copy(hot16[:], hot[:]))
            dve.sem_inc(S["hot_ready"], 1)
            c.wait(S["count_ready"])
            a, b = sums
            hand_over(nc.vector.memset(a[:, 0:1, :], 0.0),
                      nc.vector.tensor_copy(a[:, 1:TILES, :].rearrange("p t e -> p (t e)"), q_ps[1][:, 0:(TILES - 1) * E]))
            step = 1
            while step < TILES:
                hand_over(nc.vector.tensor_copy(b[:, 0:step, :], a[:, 0:step, :]),
                          nc.vector.tensor_tensor(b[:, step:, :], a[:, step:, :], a[:, 0:TILES - step, :], ALU.add))
                a, b = b, a
                step *= 2
            hand_over(nc.vector.tensor_tensor(a[:].rearrange("p t e -> p (t e)"), a[:].rearrange("p t e -> p (t e)"),
                                              q_ps[0][:, 0:TILES * E], ALU.add))
            hand_over(nc.vector.tensor_tensor(a[:], a[:], hot[:], ALU.mult))
            hand_over(nc.vector.tensor_reduce(place[:], a[:], AX.X, ALU.add))
            hand_over(nc.vector.tensor_scalar(slot[:], first[:], -float(CAP), float(E * CAP - 1), ALU.mult, ALU.add),
                      nc.vector.tensor_scalar(kept[:], place[:], float(CAP), None, ALU.is_le))
            hand_over(nc.vector.tensor_tensor(slot[:], slot[:], place[:], ALU.add),
                      nc.vector.tensor_scalar(to[:], kept[:], -float(2 * E * CAP), float(2 * E * CAP), ALU.mult, ALU.add))
            hand_over(nc.vector.tensor_tensor(to[:], to[:], slot[:], ALU.add),
                      nc.vector.tensor_scalar(frm[:], slot[:], float(E * CAP - 1), None, ALU.min))
            hand_over(nc.vector.tensor_copy(to_i[:], to[:]), nc.vector.tensor_copy(frm_i[:], frm[:]))
            dve.sem_inc(S["to_ready"], 1)
            c.wait(S["exp_out"])
            hand_over(nc.vector.tensor_reduce(gate[:], expo[:], AX.X, ALU.add))
            hand_over(nc.vector.reciprocal(gate[:], gate[:]))
            hand_over(nc.vector.tensor_tensor(gate[:], gate[:], kept[:], ALU.mult))
            dve.sem_inc(S["res_read"], 2)
            dve.wait_ge(S["w_in"], WEIGHTS)
            for n in range(2):
                dve.sem_inc(res_out[n], 16)
            with c.rounds(0, E // 2) as i:
                for n in range(2):
                    c.wait(res_out[n], 16)
                    for u in range(2):
                        c.wait(S["res_full"])
                        hand_over(nc.vector.tensor_tensor(
                            res[n][:, 2 * u:2 * u + 2, :], p_ps[u][:].rearrange("p (t d) -> p t d", t=2),
                            b12[:, bass.ds(2 * i + n, 1), :].to_broadcast([P, 2, D]), ALU.add))
                        dve.sem_inc(S["res_read"], 1)
                    dve.sem_inc(S["res_ready"], 1)
            for n in range(2):
                c.wait(res_out[n], 16)
            dve.sem_inc(S["all_out"], 1)
            dve.wait_ge(S["init"], 4)
            dve.sem_inc(S["zn_free"], 1)
            dve.wait_ge(S["xb_ready"], B)

            def total(pair, n):
                r = 2 * pair + n
                hand_over(nc.vector.tensor_copy(stat[n][:, :, 0], gate[:, bass.ds(R * r, R)]))
                dve.wait_ge(gathered[n], 16 * R * pair + 16 * R)
                hand_over(*[nc.vector.scalar_tensor_tensor(
                    z[n][:, t, :], got[:, bass.ds(R * r + t, 1), :].rearrange("p o d -> p (o d)"), stat[n][:, t, 0:1],
                    y_all[:, bass.ds(R * r + t, 1), :].rearrange("p o d -> p (o d)"), ALU.mult, ALU.add) for t in range(R)])
                dve.sem_inc(S["got_used"], 1)
                hand_over(*[nc.vector.bn_stats(st6[:, t, :], z[n][:, t, :]) for t in range(R)])
                hand_over(*[nc.vector.bn_aggr(mr4[n][:, t, :], st6[:, t, :]) for t in range(R)])
                hand_over(nc.vector.tensor_scalar(mr4[n][:, :, 1], mr4[n][:, :, 1], EPS, None, ALU.add))
                dve.sem_inc(S["var_ready"], 1)

            def invert(n):
                c.wait(S["std_ready"])
                hand_over(nc.vector.reciprocal(mr4[n][:, :, 1], mr4[n][:, :, 1]))
                hand_over(nc.vector.scalar_tensor_tensor(minus[n][:], mr4[n][:, :, 0], -1.0, mr4[n][:, :, 1], ALU.mult, ALU.mult))
                dve.sem_inc(S["rstd_ready"], 1)

            def scale(b, n):
                c.wait(S["z_normal"], R)
                hand_over(nc.vector.tensor_tensor(zn[n][:], zn[n][:], gain[:, bass.ds(b, 1), :].to_broadcast([P, R, D]), ALU.mult))
                if n == 0:
                    dve.sem_inc(S["scaled"], 1)
                else:
                    rows = x2[:, bass.ds(2 * R * b + R, R), :]
                    hand_over(nc.vector.tensor_tensor(rows, rows, zn[n][:], ALU.add))
                    dve.sem_inc(S["fin_dve_ready"], 1)

            total(0, 0)
            invert(0)
            with c.rounds(0, NR // 2 - 1) as i:
                for n in range(2):
                    total(i + n, 1 - n)
                    scale(i, n)
                    invert(1 - n)
            total(NR // 2 - 1, 1)
            scale(B - 1, 0)
            invert(1)
            scale(B - 1, 1)


def build(nc, ins, out):
    with ExitStack() as ctx:
        sb = lambda name, shape, dt=F32: ctx.enter_context(nc.sbuf_tensor(name, shape, dt))
        dram = lambda name, shape, dt=F32: nc.dram_tensor(name, shape, dt, kind="Internal").ap()
        hold = {
            "mean_rstd1": sb("mean_rstd1", [P, TILES, 2]),
            "mean_rstd2": sb("mean_rstd2", [P, TILES, 2]),
            "ca1_sa": sb("ca1_sa", [P, 2, KC, B]),
            "mod_rows": dram("mod_rows", (4, B, D)),
            "qk_scratch": dram("qk_scratch", (2, 3, D, T), BF16),
            "x2": dram("x2", (B * T, D)),
            "w12": dram("w12", (E * D, D)),
            "b12": dram("b12", (E, D)),
            "slots_in": dram("slots_in", (E * CAP, D)),
            "slots_out": dram("slots_out", (E * CAP, D)),
            "out": out,
        }
        prepare(nc, ins, hold)
        attention(nc, ins, hold)
        hold["mean_rstd3"] = sb("mean_rstd3", [P, TILES, 2])
        hold["y_all"] = sb("y_all", [P, TILES, D])
        batch_attention(nc, ins, hold)
        experts(nc, ins, hold)


def layouts(i):
    import numpy as np
    order = np.arange(D).reshape(H1, DH // 2, 2).transpose(0, 2, 1).reshape(D)
    half = DH // 2
    theta = np.float32(1.0) / np.float32(10000.0) ** (np.arange(half, dtype=np.float32) / np.float32(half))
    angle = (np.arange(T, dtype=np.float32)[:, None] * theta[None, :]).astype(np.float32).T
    c, s = np.cos(angle), np.sin(angle)
    t = lambda a: np.ascontiguousarray(np.asarray(a).T)
    wq, wk = t(i["L0_attn_W_q"])[:, order], t(i["L0_attn_W_k"])[:, order]
    bq, bk = np.asarray(i["L0_attn_b_q"])[order], np.asarray(i["L0_attn_b_k"])[order]
    row, col = np.arange(P)[:, None], np.arange(HALF)[None, :]
    return {
        "x": np.asarray(i["L0_attn_x"]).reshape(B * T, D),
        "c_t": t(i["L0_c"]),
        "wmod": np.asarray(i["L0_wmod"]),
        "wqk": np.concatenate([wq, wk], 1),
        "bqk": np.ascontiguousarray(np.concatenate([bq, bk]).reshape(SLOTS, P).T),
        "wv": t(i["L0_attn_W_v"]), "bv": np.asarray(i["L0_attn_b_v"]),
        "wo": t(i["L0_attn_W_o"]), "bo": np.asarray(i["L0_attn_b_o"]),
        "w1_t": np.ascontiguousarray(np.asarray(i["L0_ffn_w1"]).transpose(0, 2, 1)).reshape(E * FF, D),
        "w2": np.asarray(i["L0_ffn_w2"]).reshape(E * FF, D),
        "b1_t": np.ascontiguousarray(np.asarray(i["L0_ffn_b1"]).reshape(E, FC, P).transpose(0, 2, 1)),
        "b2": np.asarray(i["L0_ffn_b2"]),
        "g1": np.asarray(i["L0_ffn_ln1_g"]), "ln1_b": np.asarray(i["L0_ffn_ln1_b"]),
        "g2": np.asarray(i["L0_ffn_ln2_g"]), "ln2_b": np.asarray(i["L0_ffn_ln2_b"]),
        "wg": np.asarray(i["L0_ffn_wg"]),
        "order": np.arange(E, 0, -1).astype(np.float32),
        "upto": np.triu(np.ones((P, P), np.float32)),
        "w_in": t(i["L0_ffn_in_proj_w"]), "b_in": np.asarray(i["L0_ffn_in_proj_b"]),
        "w_out": t(i["L0_ffn_out_proj_w"]), "b_out": np.asarray(i["L0_ffn_out_proj_b"]),
        "cos": np.tile(np.concatenate([c, c]), (P // DH, 1)).astype(np.float32),
        "sin": np.tile(np.concatenate([s, -s]), (P // DH, 1)).astype(np.float32),
        "ident": np.eye(P, dtype=np.float32),
        "tri": np.where(col - (HALF - P) > row, np.float32(-1e30), np.float32(0)).astype(np.float32),
        "after": np.where(row > col[:, :P], np.float32(-1e30), np.float32(0)).astype(np.float32),
    }


def kernel(**inputs):
    import numpy as np
    import concourse.bacc as bacc
    from concourse.bass_utils import run_bass_kernel_spmd as run

    nc = bacc.Bacc("TRN2", target_bir_lowering=False, num_devices=1)
    arrays = {f"in_{name}": np.ascontiguousarray(a) for name, a in layouts(inputs).items()}
    ins = {name[3:]: nc.dram_tensor(name, a.shape, mybir.dt.from_np(a.dtype), kind="ExternalInput").ap()
           for name, a in arrays.items()}
    out = nc.dram_tensor("out_dram", (B * T, D), F32, kind="ExternalOutput").ap()
    build(nc, ins, out)
    r = run(nc, [arrays], core_ids=[0])
    return r.results[0]["out_dram"].reshape(B, T, D)
```
